# Optimizing a Trainium2 kernel written in Bass

```python
import numpy as np
import jax
import jax.numpy as jnp

def _softmax(x, axis=-1):
    return jax.nn.softmax(x, axis=axis)

def _gelu(x):
    return jax.nn.gelu(x, approximate=True)

def _silu(x):
    return jax.nn.silu(x)

def _sigmoid(x):
    return jax.nn.sigmoid(x)

def _layernorm(x, axis=-1, eps=1e-05):
    m = jnp.mean(x, axis=axis, keepdims=True)
    v = jnp.var(x, axis=axis, keepdims=True)
    return (x - m) / jnp.sqrt(v + eps)

def _scatter_add(tgt, idx, src, axis=0):
    return tgt.at[idx].add(src)

def _segment_sum(src, seg, n):
    return jax.ops.segment_sum(src, seg, n)
kernel_name = 'mk_flamingo_gated_d4_seqx_r8_06ac28'

def setup_inputs(seed: int=0):
    np.random.seed(seed)
    _w = jnp.asarray

    def _rec_inputs():
        import jax
        import jax.numpy as jnp
        _rk = jax.random.key(seed)
        x = 0.0002417 + 0.9998 * jax.random.normal(jax.random.fold_in(_rk, 1), (2, 512, 128), jnp.float32)
        _lenS = 512 - jax.random.randint(jax.random.fold_in(_rk, 7), (2,), 0, max(1, 512 // 4) + 1, jnp.int32)
        _lenS2 = 77 - jax.random.randint(jax.random.fold_in(_rk, 8), (2,), 0, max(1, 77 // 4) + 1, jnp.int32)
        _ctx_1024P = jax.random.normal(jax.random.fold_in(_rk, 11), (2, 16, 128), jnp.float32)
        _ctx_1024c = jax.random.dirichlet(jax.random.fold_in(_rk, 511), 0.3 * jnp.ones((16,), jnp.float32), (2, 77))
        _ctx_1024t = jnp.einsum('bsk,bkd->bsd', _ctx_1024c, _ctx_1024P)
        _ctx_1024t = _ctx_1024t * jax.lax.rsqrt(jnp.mean(jnp.square(_ctx_1024t)) + 1e-12) * 0.953939
        ctx_1024 = 7.22013e-05 + 1.00017 * (_ctx_1024t + 0.3 * jax.random.normal(jax.random.fold_in(_rk, 611), (2, 77, 128), jnp.float32))
        fside_Bx16xSxS2_0 = 9.80324e-06 + 0.100009 * jax.random.normal(jax.random.fold_in(_rk, 13), (2, 16, 512, 77), jnp.float32)
        fside_SxS2_0 = -2.64403e-05 + 0.100002 * jax.random.normal(jax.random.fold_in(_rk, 15), (512, 77), jnp.float32)
        _validS = jnp.arange(512)[None, :] < _lenS[:, None]
        _validS2 = jnp.arange(77)[None, :] < _lenS2[:, None]
        _causal = jnp.tril(jnp.ones((512, 512), dtype=bool))
        mask_BxS2_if0 = jnp.where(jnp.ones((2, 77), dtype=bool), 0, 1).astype(jnp.int32)
        mask_BxS2_bf0 = jnp.logical_not(jnp.ones((2, 77), dtype=bool))
        mask_SxS2_ik0 = jnp.where(jnp.broadcast_to(_validS2[0:1, :], (512, 77)), 0, 1).astype(jnp.int32)
        _g = jax.random.normal(jax.random.fold_in(_rk, 9001), (2, 4), jnp.float32)
        _g = jnp.sign(_g) * jnp.maximum(jnp.abs(_g), 1.0) + (_g == 0) * 1.0
        g_xattn = _g[0]
        g_ffn = _g[1]
        return (x, ctx_1024, fside_Bx16xSxS2_0, fside_SxS2_0, mask_BxS2_if0, mask_BxS2_bf0, mask_SxS2_ik0, g_xattn, g_ffn)
    x, ctx_1024, fside_Bx16xSxS2_0, fside_SxS2_0, mask_BxS2_if0, mask_BxS2_bf0, mask_SxS2_ik0, g_xattn, g_ffn = _rec_inputs()

    def _L0_xattn_setup():
        import jax, jax.numpy as jnp
        import numpy as np
        import math
        B, M, D, H, NK = (4, 256, 128, 16, 5)
        HD = D // H

        def _gather_pad0(x, idx):
            Bx, Hx, W, hd = x.shape
            valid = (idx >= 0) & (idx < W)
            idxc = jnp.clip(idx, 0, W - 1).reshape(Bx, Hx, -1)
            g = jnp.take_along_axis(x, idxc[..., None], axis=2)
            g = g.reshape(idx.shape + (hd,))
            return g * valid[..., None].astype(x.dtype)
        key = jax.random.key(seed)
        ks = jax.random.split(key, 9)
        w = lambda k, shape: jax.random.normal(k, shape, jnp.float32) * 0.02
        return {'k': jax.random.normal(ks[0], (B, M, D), jnp.float32), 'v': jax.random.normal(ks[1], (B, M, D), jnp.float32), 'q': jax.random.normal(ks[2], (B, M, D), jnp.float32), 'mask': jnp.zeros((B, M), jnp.int32), 'Wk': w(ks[3], (D, D)), 'bk': jnp.zeros((D,), jnp.float32), 'Wv': w(ks[4], (D, D)), 'bv': jnp.zeros((D,), jnp.float32), 'Wq': w(ks[5], (D, D)), 'bq': jnp.zeros((D,), jnp.float32), 'Woff': w(ks[6], (H * NK, D)), 'boff': jnp.zeros((H * NK,), jnp.float32), 'Wo': w(ks[7], (D, D)), 'bo': jnp.zeros((D,), jnp.float32)}
    _L0_xattn_all = _L0_xattn_setup()
    _L0_xattn_in = {k: v for k, v in _L0_xattn_all.items() if k in ('Wk', 'bk', 'Wv', 'bv', 'Wq', 'bq', 'Woff', 'boff', 'Wo', 'bo')}
    del _L0_xattn_all

    def _L0_ffn_setup():
        import jax, jax.numpy as jnp
        import numpy as np
        H_DIM, E_DIM = (128, 64)
        N_SHARED, N_ROUTED, TOP_K = (2, 16, 4)
        B, S = (4, 256)
        key = jax.random.key(seed)
        ks = jax.random.split(key, 6)
        sc = 1.0 / np.sqrt(H_DIM)
        ec = 1.0 / np.sqrt(E_DIM)
        return {'x': jax.random.normal(ks[0], (B, S, H_DIM), dtype=jnp.float32), 'shared_up': jax.random.uniform(ks[1], (N_SHARED, E_DIM, H_DIM), jnp.float32, -sc, sc), 'shared_down': jax.random.uniform(ks[2], (N_SHARED, H_DIM, E_DIM), jnp.float32, -ec, ec), 'routed_up': jax.random.uniform(ks[3], (N_ROUTED, E_DIM, H_DIM), jnp.float32, -sc, sc), 'routed_down': jax.random.uniform(ks[4], (N_ROUTED, H_DIM, E_DIM), jnp.float32, -ec, ec), 'router_w': jax.random.uniform(ks[5], (N_ROUTED, H_DIM), jnp.float32, -sc, sc)}
    _L0_ffn_all = _L0_ffn_setup()
    _L0_ffn_in = {k: v for k, v in _L0_ffn_all.items() if k in ('shared_up', 'shared_down', 'routed_up', 'routed_down', 'router_w')}
    del _L0_ffn_all

    def _L1_xattn_setup():
        import jax, jax.numpy as jnp
        import numpy as np
        E = 128
        H = 16
        D = E // H
        key = jax.random.key(seed)
        ks = jax.random.split(key, 12)
        B, T, S = (2, 256, 256)
        inp = {'query': jax.random.normal(ks[0], (B, T, E), jnp.float32), 'key': jax.random.normal(ks[1], (B, S, E), jnp.float32), 'value': jax.random.normal(ks[2], (B, S, E), jnp.float32), 'spatial_bias': jax.random.normal(ks[3], (B, H, T, S), jnp.float32) * 0.1, 'directional_bias': jax.random.normal(ks[4], (B, H, T, S), jnp.float32) * 0.1, 'key_padding_mask': jnp.zeros((B, S), dtype=bool), 'attn_mask': jax.random.normal(ks[5], (T, S), jnp.float32) * 0.1, 'Wq': jax.random.normal(ks[6], (E, E), jnp.float32) / np.sqrt(E), 'bq': jnp.zeros((E,), jnp.float32), 'Wk': jax.random.normal(ks[7], (E, E), jnp.float32) / np.sqrt(E), 'bk': jnp.zeros((E,), jnp.float32), 'Wv': jax.random.normal(ks[8], (E, E), jnp.float32) / np.sqrt(E), 'bv': jnp.zeros((E,), jnp.float32), 'Wo': jax.random.normal(ks[9], (E, E), jnp.float32) / np.sqrt(E), 'bo': jnp.zeros((E,), jnp.float32)}
        return inp
    _L1_xattn_all = _L1_xattn_setup()
    _L1_xattn_in = {k: v for k, v in _L1_xattn_all.items() if k in ('Wq', 'bq', 'Wk', 'bk', 'Wv', 'bv', 'Wo', 'bo')}
    del _L1_xattn_all

    def _L1_ffn_setup():
        import jax, jax.numpy as jnp
        import numpy as np
        TOP_K = 2
        key = jax.random.key(seed)
        k0, k1, k2, k3, k4 = jax.random.split(key, 5)
        B, S, H, I, E = (1, 512, 128, 256, 8)
        hidden_states = jax.random.normal(k0, (B, S, H), dtype=jnp.float32)
        wg = jax.random.normal(k1, (E, H), dtype=jnp.float32) * 0.02
        w1 = jax.random.normal(k2, (E, I, H), dtype=jnp.float32) * 0.02
        w3 = jax.random.normal(k3, (E, I, H), dtype=jnp.float32) * 0.02
        w2 = jax.random.normal(k4, (E, H, I), dtype=jnp.float32) * 0.02
        return {'hidden_states': hidden_states, 'wg': wg, 'w1': w1, 'w3': w3, 'w2': w2}
    _L1_ffn_all = _L1_ffn_setup()
    _L1_ffn_in = {k: v for k, v in _L1_ffn_all.items() if k in ('wg', 'w1', 'w3', 'w2')}
    del _L1_ffn_all

    def _L2_xattn_setup():
        import jax, jax.numpy as jnp
        import numpy as np
        import math
        D = 128
        H = 16
        B = 4
        S = 256

        def _split_heads(x):
            b, s, d = x.shape
            return x.reshape(b, s, H, d // H).transpose(0, 2, 1, 3)
        key = jax.random.key(seed)
        ks = jax.random.split(key, 11)
        s = 1.0 / math.sqrt(D)
        inp = {'queries': jax.random.normal(ks[0], (B, S, D), jnp.float32), 'keys': jax.random.normal(ks[1], (B, S, D), jnp.float32), 'values': jax.random.normal(ks[2], (B, S, D), jnp.float32), 'Wq': jax.random.normal(ks[3], (D, D), jnp.float32) * s, 'bq': jnp.zeros((D,), jnp.float32), 'Wk': jax.random.normal(ks[4], (D, D), jnp.float32) * s, 'bk': jnp.zeros((D,), jnp.float32), 'Wv': jax.random.normal(ks[5], (D, D), jnp.float32) * s, 'bv': jnp.zeros((D,), jnp.float32), 'Wo': jax.random.normal(ks[6], (D, D), jnp.float32) * s, 'bo': jnp.zeros((D,), jnp.float32)}
        return inp
    _L2_xattn_all = _L2_xattn_setup()
    _L2_xattn_in = {k: v for k, v in _L2_xattn_all.items() if k in ('Wq', 'bq', 'Wk', 'bk', 'Wv', 'bv', 'Wo', 'bo')}
    del _L2_xattn_all

    def _L2_ffn_setup():
        import jax, jax.numpy as jnp
        import numpy as np
        MANT_BITS = 8
        _PWL_X = jnp.linspace(-4.0, 4.0, 33, dtype=jnp.float32)
        _PWL_Y = 0.5 * _PWL_X * (1.0 + jax.lax.erf(_PWL_X / jnp.sqrt(jnp.float32(2.0))))

        def float2fix(x, mantissa_bits):
            s = jnp.float32(2.0 ** mantissa_bits)
            q = jnp.round(x * s) / s
            return x + jax.lax.stop_gradient(q - x)

        def pwlin_gelu_basic(x, mantissa_bits_in, mantissa_bits_out):
            xq = float2fix(x, mantissa_bits_in)
            y = jnp.interp(xq, _PWL_X, _PWL_Y)
            y = jnp.where(xq > 4.0, xq, jnp.where(xq < -4.0, jnp.float32(0.0), y))
            return float2fix(y, mantissa_bits_out)
        key = jax.random.key(seed)
        k_x, k_w1, k_b1, k_w2, k_b2 = jax.random.split(key, 5)
        dim, ff_dim = (128, 512)
        B, S = (32, 64)
        sc1 = 1.0 / np.sqrt(dim)
        sc2 = 1.0 / np.sqrt(ff_dim)
        return {'x': jax.random.normal(k_x, (B, S, dim), dtype=jnp.float32), 'w1': jax.random.uniform(k_w1, (dim, ff_dim), jnp.float32, -sc1, sc1), 'b1': jax.random.uniform(k_b1, (ff_dim,), jnp.float32, -sc1, sc1), 'w2': jax.random.uniform(k_w2, (ff_dim, dim), jnp.float32, -sc2, sc2), 'b2': jax.random.uniform(k_b2, (dim,), jnp.float32, -sc2, sc2)}
    _L2_ffn_all = _L2_ffn_setup()
    _L2_ffn_in = {k: v for k, v in _L2_ffn_all.items() if k in ('w1', 'b1', 'w2', 'b2')}
    del _L2_ffn_all

    def _L3_xattn_setup():
        import jax, jax.numpy as jnp
        import numpy as np
        MODEL_DIM = 128
        NUM_HEADS = 16
        HEAD_DIM = MODEL_DIM // NUM_HEADS

        def _split_heads(x):
            B, S, D = x.shape
            return x.reshape(B, S, NUM_HEADS, HEAD_DIM).transpose(0, 2, 1, 3)
        key = jax.random.key(seed)
        ks = jax.random.split(key, 11)
        B, S, D = (2, 256, MODEL_DIM)
        scale = 1.0 / np.sqrt(D)
        inp = {'Q': jax.random.normal(ks[0], (B, S, D), jnp.float32), 'K': jax.random.normal(ks[1], (B, S, D), jnp.float32), 'V': jax.random.normal(ks[2], (B, S, D), jnp.float32), 'mask': jnp.tril(jnp.ones((S, S), jnp.int32)), 'Wq': jax.random.normal(ks[3], (D, D), jnp.float32) * scale, 'bq': jax.random.normal(ks[4], (D,), jnp.float32) * 0.01, 'Wk': jax.random.normal(ks[5], (D, D), jnp.float32) * scale, 'bk': jax.random.normal(ks[6], (D,), jnp.float32) * 0.01, 'Wv': jax.random.normal(ks[7], (D, D), jnp.float32) * scale, 'bv': jax.random.normal(ks[8], (D,), jnp.float32) * 0.01, 'Wo': jax.random.normal(ks[9], (D, D), jnp.float32) * scale, 'bo': jax.random.normal(ks[10], (D,), jnp.float32) * 0.01}
        return inp
    _L3_xattn_all = _L3_xattn_setup()
    _L3_xattn_in = {k: v for k, v in _L3_xattn_all.items() if k in ('Wq', 'bq', 'Wk', 'bk', 'Wv', 'bv', 'Wo', 'bo')}
    del _L3_xattn_all

    def _L3_ffn_setup():
        import math
        import jax, jax.numpy as jnp
        import numpy as np
        B, L, D, FF, E, K = (4, 256, 128, 512, 8, 2)
        CAPACITY_FACTOR = 1.25
        T = B * L
        CAP = math.ceil(CAPACITY_FACTOR * T * K / E)
        key = jax.random.key(seed)
        ks = jax.random.split(key, 7)
        return {'h': jax.random.normal(ks[0], (B, L, D), dtype=jnp.float32), 'gate_w': 0.02 * jax.random.normal(ks[1], (E, D), dtype=jnp.float32), 'gate_b': jnp.zeros((E,), dtype=jnp.float32), 'W1': 0.02 * jax.random.normal(ks[2], (E, D, FF), dtype=jnp.float32), 'b1': jnp.zeros((E, FF), dtype=jnp.float32), 'W2': 0.02 * jax.random.normal(ks[3], (E, FF, D), dtype=jnp.float32), 'b2': jnp.zeros((E, D), dtype=jnp.float32)}
    _L3_ffn_all = _L3_ffn_setup()
    _L3_ffn_in = {k: v for k, v in _L3_ffn_all.items() if k in ('gate_w', 'gate_b', 'W1', 'b1', 'W2', 'b2')}
    del _L3_ffn_all
    return {'x': x, 'ctx_1024': ctx_1024, 'fside_Bx16xSxS2_0': fside_Bx16xSxS2_0, 'fside_SxS2_0': fside_SxS2_0, 'mask_BxS2_if0': mask_BxS2_if0, 'mask_BxS2_bf0': mask_BxS2_bf0, 'mask_SxS2_ik0': mask_SxS2_ik0, 'g_xattn': g_xattn, 'g_ffn': g_ffn, 'L0_xattn_Wk': _L0_xattn_in['Wk'], 'L0_xattn_bk': _L0_xattn_in['bk'], 'L0_xattn_Wv': _L0_xattn_in['Wv'], 'L0_xattn_bv': _L0_xattn_in['bv'], 'L0_xattn_Wq': _L0_xattn_in['Wq'], 'L0_xattn_bq': _L0_xattn_in['bq'], 'L0_xattn_Woff': _L0_xattn_in['Woff'], 'L0_xattn_boff': _L0_xattn_in['boff'], 'L0_xattn_Wo': _L0_xattn_in['Wo'], 'L0_xattn_bo': _L0_xattn_in['bo'], 'L0_ffn_shared_up': _L0_ffn_in['shared_up'], 'L0_ffn_shared_down': _L0_ffn_in['shared_down'], 'L0_ffn_routed_up': _L0_ffn_in['routed_up'], 'L0_ffn_routed_down': _L0_ffn_in['routed_down'], 'L0_ffn_router_w': _L0_ffn_in['router_w'], 'L1_xattn_Wq': _L1_xattn_in['Wq'], 'L1_xattn_bq': _L1_xattn_in['bq'], 'L1_xattn_Wk': _L1_xattn_in['Wk'], 'L1_xattn_bk': _L1_xattn_in['bk'], 'L1_xattn_Wv': _L1_xattn_in['Wv'], 'L1_xattn_bv': _L1_xattn_in['bv'], 'L1_xattn_Wo': _L1_xattn_in['Wo'], 'L1_xattn_bo': _L1_xattn_in['bo'], 'L1_ffn_wg': _L1_ffn_in['wg'], 'L1_ffn_w1': _L1_ffn_in['w1'], 'L1_ffn_w3': _L1_ffn_in['w3'], 'L1_ffn_w2': _L1_ffn_in['w2'], 'L2_xattn_Wq': _L2_xattn_in['Wq'], 'L2_xattn_bq': _L2_xattn_in['bq'], 'L2_xattn_Wk': _L2_xattn_in['Wk'], 'L2_xattn_bk': _L2_xattn_in['bk'], 'L2_xattn_Wv': _L2_xattn_in['Wv'], 'L2_xattn_bv': _L2_xattn_in['bv'], 'L2_xattn_Wo': _L2_xattn_in['Wo'], 'L2_xattn_bo': _L2_xattn_in['bo'], 'L2_ffn_w1': _L2_ffn_in['w1'], 'L2_ffn_b1': _L2_ffn_in['b1'], 'L2_ffn_w2': _L2_ffn_in['w2'], 'L2_ffn_b2': _L2_ffn_in['b2'], 'L3_xattn_Wq': _L3_xattn_in['Wq'], 'L3_xattn_bq': _L3_xattn_in['bq'], 'L3_xattn_Wk': _L3_xattn_in['Wk'], 'L3_xattn_bk': _L3_xattn_in['bk'], 'L3_xattn_Wv': _L3_xattn_in['Wv'], 'L3_xattn_bv': _L3_xattn_in['bv'], 'L3_xattn_Wo': _L3_xattn_in['Wo'], 'L3_xattn_bo': _L3_xattn_in['bo'], 'L3_ffn_gate_w': _L3_ffn_in['gate_w'], 'L3_ffn_gate_b': _L3_ffn_in['gate_b'], 'L3_ffn_W1': _L3_ffn_in['W1'], 'L3_ffn_b1': _L3_ffn_in['b1'], 'L3_ffn_W2': _L3_ffn_in['W2'], 'L3_ffn_b2': _L3_ffn_in['b2']}

def reference(x, ctx_1024, fside_Bx16xSxS2_0, fside_SxS2_0, mask_BxS2_if0, mask_BxS2_bf0, mask_SxS2_ik0, g_xattn, g_ffn, L0_xattn_Wk, L0_xattn_bk, L0_xattn_Wv, L0_xattn_bv, L0_xattn_Wq, L0_xattn_bq, L0_xattn_Woff, L0_xattn_boff, L0_xattn_Wo, L0_xattn_bo, L0_ffn_shared_up, L0_ffn_shared_down, L0_ffn_routed_up, L0_ffn_routed_down, L0_ffn_router_w, L1_xattn_Wq, L1_xattn_bq, L1_xattn_Wk, L1_xattn_bk, L1_xattn_Wv, L1_xattn_bv, L1_xattn_Wo, L1_xattn_bo, L1_ffn_wg, L1_ffn_w1, L1_ffn_w3, L1_ffn_w2, L2_xattn_Wq, L2_xattn_bq, L2_xattn_Wk, L2_xattn_bk, L2_xattn_Wv, L2_xattn_bv, L2_xattn_Wo, L2_xattn_bo, L2_ffn_w1, L2_ffn_b1, L2_ffn_w2, L2_ffn_b2, L3_xattn_Wq, L3_xattn_bq, L3_xattn_Wk, L3_xattn_bk, L3_xattn_Wv, L3_xattn_bv, L3_xattn_Wo, L3_xattn_bo, L3_ffn_gate_w, L3_ffn_gate_b, L3_ffn_W1, L3_ffn_b1, L3_ffn_W2, L3_ffn_b2):
    import jax
    import jax.numpy as jnp

    def _L0_xattn_ref(k, v, q, mask, Wk, bk, Wv, bv, Wq, bq, Woff, boff, Wo, bo):
        import jax, jax.numpy as jnp
        import numpy as np
        import math
        B, M, D, H, NK = (4, 256, 128, 16, 5)
        HD = D // H

        def _gather_pad0(x, idx):
            Bx, Hx, W, hd = x.shape
            valid = (idx >= 0) & (idx < W)
            idxc = jnp.clip(idx, 0, W - 1).reshape(Bx, Hx, -1)
            g = jnp.take_along_axis(x, idxc[..., None], axis=2)
            g = g.reshape(idx.shape + (hd,))
            return g * valid[..., None].astype(x.dtype)
        Bq, Q, _ = q.shape
        key_len = k.shape[1]
        K = jnp.einsum('bmd,ed->bme', k, Wk) + bk
        V = jnp.einsum('bmd,ed->bme', v, Wv) + bv
        Qp = jnp.einsum('bqd,ed->bqe', q, Wq) + bq
        off = jnp.einsum('bqd,ed->bqe', Qp, Woff) + boff
        off = off.reshape(Bq, Q, H, NK).transpose(0, 2, 1, 3)
        Kh = K.reshape(Bq, key_len, H, HD).transpose(0, 2, 1, 3)
        Vh = V.reshape(Bq, key_len, H, HD).transpose(0, 2, 1, 3)
        Qh = Qp.reshape(Bq, Q, H, HD).transpose(0, 2, 1, 3)
        loc = jnp.arange(Q, dtype=jnp.float32)[:, None]
        left = -NK // 2
        ref = jnp.arange(left, NK + left, dtype=jnp.float32)
        sign_lens = (1 - mask).sum(-1).astype(jnp.float32) - 1.0
        loc_x = jnp.mod(ref + off + loc, sign_lens[:, None, None, None])
        xg = loc_x / (key_len - 1) * 2.0 - 1.0
        ix = ((xg + 1.0) * key_len - 1.0) / 2.0
        x0 = jnp.floor(ix)
        dx = ix - x0
        i0 = x0.astype(jnp.int32)
        i1 = i0 + 1
        w0 = (1.0 - dx)[..., None]
        w1 = dx[..., None]
        sk = 0.5 * (w0 * _gather_pad0(Kh, i0) + w1 * _gather_pad0(Kh, i1))
        sv = 0.5 * (w0 * _gather_pad0(Vh, i0) + w1 * _gather_pad0(Vh, i1))
        scores = jnp.einsum('bhqd,bhqkd->bhqk', Qh / math.sqrt(HD), sk)
        attn = jax.nn.softmax(scores, axis=-1)
        ctx = jnp.einsum('bhqk,bhqkd->bhqd', attn, sv)
        ctx = ctx.transpose(0, 2, 1, 3).reshape(Bq, Q, H * HD)
        return jnp.einsum('bqd,ed->bqe', ctx, Wo) + bo

    def _L0_ffn_ref(x, shared_up, shared_down, routed_up, routed_down, router_w):
        import jax, jax.numpy as jnp
        import numpy as np
        H_DIM, E_DIM = (128, 64)
        N_SHARED, N_ROUTED, TOP_K = (2, 16, 4)
        B, S = (4, 256)
        b, s, h = x.shape
        xt = x.reshape(-1, h)
        up_s = jnp.einsum('th,seh->tse', xt, shared_up)
        shared = jnp.einsum('tse,she->th', jax.nn.gelu(up_s, approximate=False), shared_down)
        probs = jax.nn.softmax(xt @ router_w.T, axis=-1)
        topk_p, topk_i = jax.lax.top_k(probs, TOP_K)
        gate = jnp.zeros_like(probs).at[jnp.arange(xt.shape[0])[:, None], topk_i].add(topk_p)
        up_r = jnp.einsum('th,reh->tre', xt, routed_up)
        act = jax.nn.gelu(up_r, approximate=False) * gate[:, :, None]
        routed = jnp.einsum('tre,rhe->th', act, routed_down)
        return (shared + routed).reshape(b, s, h)

    def _L1_xattn_ref(query, key, value, spatial_bias, directional_bias, key_padding_mask, attn_mask, Wq, bq, Wk, bk, Wv, bv, Wo, bo):
        import jax, jax.numpy as jnp
        import numpy as np
        E = 128
        H = 16
        D = E // H
        B, T, _ = query.shape
        S = key.shape[1]
        scale = D ** (-0.5)
        q = (query @ Wq.T + bq).reshape(B, T, H, D).transpose(0, 2, 1, 3)
        k = (key @ Wk.T + bk).reshape(B, S, H, D).transpose(0, 2, 1, 3)
        v = (value @ Wv.T + bv).reshape(B, S, H, D).transpose(0, 2, 1, 3)
        scores = jnp.einsum('bhtd,bhsd->bhts', q, k) * scale
        scores = scores + attn_mask[None, None, :, :]
        pad = key_padding_mask[:, None, None, :]
        scores = jnp.where(pad, -jnp.inf, scores)
        if T == S:
            scores = scores + spatial_bias + directional_bias
        probs = jax.nn.softmax(scores, axis=-1)
        out = jnp.einsum('bhts,bhsd->bhtd', probs, v)
        out = out.transpose(0, 2, 1, 3).reshape(B, T, E)
        return out @ Wo.T + bo

    def _L1_ffn_ref(hidden_states, wg, w1, w3, w2):
        import jax, jax.numpy as jnp
        import numpy as np
        TOP_K = 2
        orig_shape = hidden_states.shape
        H = orig_shape[-1]
        E = wg.shape[0]
        x = hidden_states.reshape(-1, H)
        router_logits = x @ wg.T
        probs = jax.nn.softmax(router_logits, axis=-1)
        topk_w, topk_idx = jax.lax.top_k(probs, TOP_K)
        topk_w = topk_w / jnp.sum(topk_w, axis=-1, keepdims=True)
        expert_w = jnp.sum(jax.nn.one_hot(topk_idx, E, dtype=x.dtype) * topk_w[..., None], axis=1)
        h1 = jnp.einsum('th,eih->tei', x, w1)
        h3 = jnp.einsum('th,eih->tei', x, w3)
        y = jnp.einsum('tei,ehi->teh', jax.nn.silu(h1) * h3, w2)
        out = jnp.einsum('te,teh->th', expert_w, y)
        return out.reshape(orig_shape)

    def _L2_xattn_ref(queries, keys, values, Wq, bq, Wk, bk, Wv, bv, Wo, bo):
        import jax, jax.numpy as jnp
        import numpy as np
        import math
        D = 128
        H = 16
        B = 4
        S = 256

        def _split_heads(x):
            b, s, d = x.shape
            return x.reshape(b, s, H, d // H).transpose(0, 2, 1, 3)
        q = jax.nn.relu(queries @ Wq + bq)
        k = jax.nn.relu(keys @ Wk + bk)
        v = jax.nn.relu(values @ Wv + bv)
        q, k, v = (_split_heads(q), _split_heads(k), _split_heads(v))
        dk = q.shape[-1]
        scores = jnp.einsum('bhqd,bhkd->bhqk', q, k) / jnp.sqrt(jnp.float32(dk))
        attn = jax.nn.softmax(scores, axis=-1)
        y = jnp.einsum('bhqk,bhkd->bhqd', attn, v)
        y = y.transpose(0, 2, 1, 3).reshape(queries.shape[0], queries.shape[1], -1)
        return jax.nn.relu(y @ Wo + bo)

    def _L2_ffn_ref(x, w1, b1, w2, b2):
        import jax, jax.numpy as jnp
        import numpy as np
        MANT_BITS = 8
        _PWL_X = jnp.linspace(-4.0, 4.0, 33, dtype=jnp.float32)
        _PWL_Y = 0.5 * _PWL_X * (1.0 + jax.lax.erf(_PWL_X / jnp.sqrt(jnp.float32(2.0))))

        def float2fix(x, mantissa_bits):
            s = jnp.float32(2.0 ** mantissa_bits)
            q = jnp.round(x * s) / s
            return x + jax.lax.stop_gradient(q - x)

        def pwlin_gelu_basic(x, mantissa_bits_in, mantissa_bits_out):
            xq = float2fix(x, mantissa_bits_in)
            y = jnp.interp(xq, _PWL_X, _PWL_Y)
            y = jnp.where(xq > 4.0, xq, jnp.where(xq < -4.0, jnp.float32(0.0), y))
            return float2fix(y, mantissa_bits_out)
        h = jnp.einsum('bsd,df->bsf', x, w1) + b1
        h = float2fix(h, MANT_BITS)
        h = pwlin_gelu_basic(h, MANT_BITS, MANT_BITS)
        h = float2fix(h, MANT_BITS)
        out = jnp.einsum('bsf,fd->bsd', h, w2) + b2
        return float2fix(out, MANT_BITS)

    def _L3_xattn_ref(Q, K, V, mask, Wq, bq, Wk, bk, Wv, bv, Wo, bo):
        import jax, jax.numpy as jnp
        import numpy as np
        MODEL_DIM = 128
        NUM_HEADS = 16
        HEAD_DIM = MODEL_DIM // NUM_HEADS

        def _split_heads(x):
            B, S, D = x.shape
            return x.reshape(B, S, NUM_HEADS, HEAD_DIM).transpose(0, 2, 1, 3)
        q = _split_heads(Q @ Wq.T + bq)
        k = _split_heads(K @ Wk.T + bk)
        v = _split_heads(V @ Wv.T + bv)
        scores = jnp.einsum('bhqd,bhkd->bhqk', q, k) / jnp.sqrt(jnp.float32(HEAD_DIM))
        scores = jnp.where(mask == 0, jnp.float32(-1e-09), scores)
        probs = jax.nn.softmax(scores, axis=-1)
        attn = jnp.einsum('bhqk,bhkd->bhqd', probs, v)
        B, H, S, hd = attn.shape
        out = attn.transpose(0, 2, 1, 3).reshape(B, S, MODEL_DIM)
        return out @ Wo.T + bo

    def _L3_ffn_ref(h, gate_w, gate_b, W1, b1, W2, b2):
        import math
        import jax, jax.numpy as jnp
        import numpy as np
        B, L, D, FF, E, K = (4, 256, 128, 512, 8, 2)
        CAPACITY_FACTOR = 1.25
        T = B * L
        CAP = math.ceil(CAPACITY_FACTOR * T * K / E)
        Bb, Ll, Dm = h.shape
        Tt = Bb * Ll
        x = h.reshape(Tt, Dm)
        logits = x @ gate_w.T + gate_b
        probs = jax.nn.softmax(logits, axis=-1)
        topk_prob, topk_idx = jax.lax.top_k(probs, K)
        y = jnp.zeros((Tt, Dm), dtype=h.dtype)
        n_slots = E * CAP
        for c in range(K):
            idx = topk_idx[:, c]
            prb = topk_prob[:, c]
            oh = jax.nn.one_hot(idx, E, dtype=jnp.int32)
            pos = jnp.take_along_axis(jnp.cumsum(oh, axis=0) - 1, idx[:, None], axis=1)[:, 0]
            keep = pos < CAP
            buf_idx = jnp.where(keep, idx * CAP + pos, n_slots)
            xbuf = jnp.zeros((n_slots, Dm), x.dtype).at[buf_idx].set(x, mode='drop')
            xb = xbuf.reshape(E, CAP, Dm)
            hmid = jax.nn.relu(jnp.einsum('ecd,edf->ecf', xb, W1) + b1[:, None, :])
            yb = jnp.einsum('ecf,efd->ecd', hmid, W2) + b2[:, None, :]
            ytok = yb.reshape(n_slots, Dm)[jnp.clip(buf_idx, 0, n_slots - 1)]
            y = y + ytok * (prb * keep.astype(prb.dtype))[:, None]
        return y.reshape(Bb, Ll, Dm)
    x = x + jnp.tanh(g_xattn[0]) * _L0_xattn_ref(ctx_1024, ctx_1024, _layernorm(x, axis=-1), mask_BxS2_if0, L0_xattn_Wk, L0_xattn_bk, L0_xattn_Wv, L0_xattn_bv, L0_xattn_Wq, L0_xattn_bq, L0_xattn_Woff, L0_xattn_boff, L0_xattn_Wo, L0_xattn_bo)
    x = x + jnp.tanh(g_ffn[0]) * _L0_ffn_ref(_layernorm(x, axis=-1), L0_ffn_shared_up, L0_ffn_shared_down, L0_ffn_routed_up, L0_ffn_routed_down, L0_ffn_router_w)
    x = x + jnp.tanh(g_xattn[1]) * _L1_xattn_ref(_layernorm(x, axis=-1), ctx_1024, ctx_1024, fside_Bx16xSxS2_0, fside_Bx16xSxS2_0, mask_BxS2_bf0, fside_SxS2_0, L1_xattn_Wq, L1_xattn_bq, L1_xattn_Wk, L1_xattn_bk, L1_xattn_Wv, L1_xattn_bv, L1_xattn_Wo, L1_xattn_bo)
    x = x + jnp.tanh(g_ffn[1]) * _L1_ffn_ref(_layernorm(x, axis=-1), L1_ffn_wg, L1_ffn_w1, L1_ffn_w3, L1_ffn_w2)
    x = x + jnp.tanh(g_xattn[2]) * _L2_xattn_ref(_layernorm(x, axis=-1), ctx_1024, ctx_1024, L2_xattn_Wq, L2_xattn_bq, L2_xattn_Wk, L2_xattn_bk, L2_xattn_Wv, L2_xattn_bv, L2_xattn_Wo, L2_xattn_bo)
    x = x + jnp.tanh(g_ffn[2]) * _L2_ffn_ref(_layernorm(x, axis=-1), L2_ffn_w1, L2_ffn_b1, L2_ffn_w2, L2_ffn_b2)
    x = x + jnp.tanh(g_xattn[3]) * _L3_xattn_ref(_layernorm(x, axis=-1), ctx_1024, ctx_1024, mask_SxS2_ik0, L3_xattn_Wq, L3_xattn_bq, L3_xattn_Wk, L3_xattn_bk, L3_xattn_Wv, L3_xattn_bv, L3_xattn_Wo, L3_xattn_bo)
    x = x + jnp.tanh(g_ffn[3]) * _L3_ffn_ref(_layernorm(x, axis=-1), L3_ffn_gate_w, L3_ffn_gate_b, L3_ffn_W1, L3_ffn_b1, L3_ffn_W2, L3_ffn_b2)
    return x

_drawn_inputs = setup_inputs


def setup_inputs(seed=0):
    import zlib

    import numpy as np

    out = dict(_drawn_inputs(seed))
    spreads = {'L0_xattn_bk': (0.0, 2.0),
     'L0_xattn_bv': (0.0, 0.8),
     'L0_xattn_bq': (0.0, 0.8),
     'L0_xattn_boff': (0.0, 0.8),
     'L0_xattn_bo': (0.0, 0.1),
     'L1_xattn_bq': (0.0, 0.442),
     'L1_xattn_bk': (0.0, 2.0),
     'L1_xattn_bv': (0.0, 0.1),
     'L1_xattn_bo': (0.0, 0.1),
     'L2_xattn_bq': (0.0, 2.0),
     'L2_xattn_bk': (0.0, 2.0),
     'L2_xattn_bv': (0.0, 0.933),
     'L2_xattn_bo': (0.0, 0.338),
     'L3_ffn_gate_b': (0.0, 0.572),
     'L3_ffn_b1': (0.0, 0.8),
     'L3_ffn_b2': (0.0, 0.5)}
    factors = {'fside_SxS2_0': 4.762,
     'g_ffn': 8.0,
     'L0_xattn_Wk': 8.0,
     'L0_xattn_Wv': 4.997,
     'L0_xattn_Wq': 8.0,
     'L0_xattn_Woff': 8.0,
     'L0_xattn_Wo': 4.367,
     'L1_ffn_wg': 8.0,
     'L1_ffn_w1': 8.0,
     'L1_ffn_w3': 8.0,
     'L1_ffn_w2': 8.0,
     'L2_ffn_b1': 5.172,
     'L2_ffn_b2': 3.511,
     'L3_xattn_bq': 64.0,
     'L3_xattn_bk': 64.0,
     'L3_xattn_bv': 26.016,
     'L3_xattn_bo': 21.682,
     'L3_ffn_gate_w': 3.093,
     'L3_ffn_W1': 5.734,
     'L3_ffn_W2': 4.441,
     'L2_xattn_Wq': 4.637,
     'L2_xattn_Wk': 3.293,
     'L3_xattn_Wq': 3.806,
     'L3_xattn_Wk': 3.637}
    for name, (base, spread) in spreads.items():
        noise = np.random.default_rng([zlib.crc32(name.encode()), seed]).standard_normal(out[name].shape)
        drawn = base * np.exp(spread * noise) if base else spread * noise
        out[name] = jnp.asarray(drawn.astype(out[name].dtype))
    for name, factor in factors.items():
        out[name] = (out[name] * factor).astype(out[name].dtype)
    return out
```

```python
import concourse.bass as bass
from concourse import mybir
from contextlib import ExitStack

B, T, D = 2, 512, 128
M = 77
H, HD = 16, 8
G, HG = 4, 4
NT, TT = T // 128, 128
NK = 5
MO = M + 1
ATT = 3
GATES = ((16, 4), (8, 2), (8, 2))
CAP = 320
EPS = 1e-5
MAGIC = 12582912.0
NEG = -1e30

CONST_W = dict(ident=128, tri=128, id32=32, id16=16, headmask=4, tie=256, patA=128, patW=128,
               patWb=1, refk=1, pos=1, selS=4)
L0_W = dict(wq=128, wqrep=512, woff=128, wkv=256, worep=512, ctx=B * (M + 2), bq=1, bqrep=4, boff=1, bo=1)
ATT_W = dict(wq=384, wk=384, wv=128, wo=128, bq=4, bk=4, bo=1)
F0_W = dict(rw=16, up=1152, down=1152)
F1_W = dict(rw=8, w1=2048, w3=2048, w2=2048)
F2_W = dict(w1=512, w2=512, b1=4, b2=1)
F3_W = dict(rw=8, b1=32, b2=8)
F3_BIG = dict(w1=4096, w2=4096)
ROW_W = dict(bkv=256, valid=2 * MO, bv=ATT * 128, gb=8)


def offsets(widths):
    at, out = 0, {}
    for name, w in widths.items():
        out[name] = (at, w)
        at += w
    return out, at


class Signal:

    def __init__(self, sem, *dims):
        self.sem, self.dims = sem, dims

    def after(self, *key):
        n = 0
        for k, d in zip(key, self.dims):
            assert 0 <= k < d
            n = n * d + k
        return self.sem, n + 1


def bass_flamingo_gated_layers_kernel(nc, xT, g8, const, l0, att, f0, f1, f2, f3, f3big, rows, am_tok, am_T,
                  ik_tok, ik_T, mif, mbf_tok, mbf_T, outT):
    f32, bf16, i32 = mybir.dt.float32, mybir.dt.bfloat16, mybir.dt.int32
    ALU, ACT, AX = mybir.AluOpType, mybir.ActivationFunctionType, mybir.AxisListType
    V, A, P, E = nc.vector, nc.scalar, nc.gpsimd, nc.tensor

    with ExitStack() as ctx:
        def sb(name, shape, dt=f32):
            return ctx.enter_context(nc.sbuf_tensor(name, shape, dt))

        def signal(name, *dims):
            return Signal(ctx.enter_context(nc.semaphore(name)), *dims)

        def packed(tile, widths):
            cols, _ = offsets(widths)
            return lambda name: tile[:, cols[name][0]:cols[name][0] + cols[name][1]]

        x = sb("x", [128, B, T])
        tg = sb("tg", [128, 8])
        g_raw = sb("g_raw", [128, 8])
        const_sb = sb("const_sb", [128, offsets(CONST_W)[1]])
        C = packed(const_sb, CONST_W)
        l0_sb = sb("l0_sb", [128, offsets(L0_W)[1]])
        L0 = packed(l0_sb, L0_W)
        f0_sb = sb("f0_sb", [128, offsets(F0_W)[1]])
        F0 = packed(f0_sb, F0_W)
        f3_sb = sb("f3_sb", [128, offsets(F3_W)[1]])
        F3 = packed(f3_sb, F3_W)
        rows_sb = sb("rows_sb", [1, offsets(ROW_W)[1]])
        R = packed(rows_sb, ROW_W)
        ones_row = sb("ones_row", [1, 128])
        eps_col = sb("eps_col", [128, 1])
        mean_w = sb("mean_w", [128, 128])
        ones_bf = sb("ones_bf", [128, 128], bf16)
        ident_bf = sb("ident_bf", [128, 128], bf16)
        neg_ident = sb("neg_ident", [128, 128], bf16)
        tri_bf = sb("tri_bf", [128, 128], bf16)

        xc = sb("xc", [128, B, T])
        sq = sb("sq", [128, T])
        rstd = sb("rstd", [128, T])
        xn = sb("xn", [128, B, T])
        y_tmp = sb("y_tmp", [128, T])

        arena = sb("arena", [128, B * G * NK * T])
        GW = arena[:, :].rearrange("p (b u t) -> p b u t", b=B, u=G * NK)
        n_f3, n_f1, n_att = offsets(F3_BIG)[1], offsets(F1_W)[1], ATT * offsets(ATT_W)[1]
        f3w = arena[:, 0:n_f3]
        F3B = packed(f3w, F3_BIG)
        f1_sb = arena[:, n_f3:n_f3 + n_f1]
        F1 = packed(f1_sb, F1_W)
        att_sb = arena[:, n_f3 + n_f1:n_f3 + n_f1 + n_att].rearrange("p (a n) -> p a n", a=ATT)
        AW = [packed(att_sb[:, a, :], ATT_W) for a in range(ATT)]
        amp = arena[:, n_f3 + n_f1 + n_att:n_f3 + n_f1 + n_att + B * NT * M].rearrange(
            "p (b t m) -> p b t m", b=B, t=NT)

        work = sb("work", [128, 10752])
        early = sb("early", [128, 7500])
        at, base = [0], [work]

        def piece(n, dt=f32):
            w = n if dt == f32 else (n + 1) // 2
            assert at[0] + w <= base[0].shape[1], at[0]
            v = base[0][:, at[0]:at[0] + w]
            at[0] += w
            return v if dt == f32 else v.bitcast(dt)

        qp = piece(T)
        qrep = piece(B * G * T).rearrange("p (b g t) -> p b g t", b=B, g=G)
        ixt = piece(T)
        ix1 = piece(T)
        ix2 = piece(T)
        i0bf = piece(B * T, bf16).rearrange("p (b t) -> p b t", b=B)
        w1hi = piece(B * T, bf16).rearrange("p (b t) -> p b t", b=B)
        w1lo = piece(B * T, bf16).rearrange("p (b t) -> p b t", b=B)
        at_wf = piece(2 * T).rearrange("p (r t) -> p r t", r=2)
        tq = piece(3 * T).rearrange("p (r t) -> p r t", r=3)
        ahi = piece(T, bf16)
        alo = piece(T, bf16)
        end_l0 = at[0]
        at[0] = 0
        qf = piece(G * T).rearrange("p (g t) -> p g t", g=G)
        qst = piece(G * T, bf16).rearrange("p (g t) -> p g t", g=G)
        nT = piece(T, bf16)
        pT = piece(4 * T).rearrange("p (r t) -> p r t", r=4)
        bT = piece(3 * T).rearrange("p (r t) -> p r t", r=3)
        s_tok = piece(H * M)
        oN = piece(NT * D).rearrange("p (t d) -> p t d", t=NT)
        oT = piece(T)
        at[0] = 0
        gbc = piece(8 * T).rearrange("p (e t) -> p e t", e=8)
        hid = piece(3 * T).rearrange("p (r t) -> p r t", r=3)
        hid2 = piece(4 * T).rearrange("p (r t) -> p r t", r=4)
        acc = piece(T)
        yg = piece(2 * T).rearrange("p (r t) -> p r t", r=2)
        big = gbc[:, 4:6, :].rearrange("p e t -> p (e t)")
        big2 = gbc[:, 6:8, :].rearrange("p e t -> p (e t)")
        gr1, glo = hid[0:16, 2, :], hid[0:16, 1, 0:T // 2].bitcast(bf16)
        base[0], at[0] = early, 0
        loc = piece(T)
        selB = piece(20 * MO, bf16).rearrange("p (r m) -> p r m", r=20)
        selA = piece(NK * 128, bf16).rearrange("p (k c) -> p k c", k=NK)
        selW = piece(NK * 128, bf16).rearrange("p (k c) -> p k c", k=NK)
        tab = piece(B * 2 * H * 32, bf16)[0:MO].rearrange("p (b a h c) -> p b a h c", b=B, a=2, h=H)
        ib = piece(4 * T, bf16)[0:MO].rearrange("p (p2 t) -> p p2 t", p2=2)
        oh = piece(8 * T, bf16)[0:MO].rearrange("p (r p2 t) -> p r p2 t", r=2, p2=2)
        s80 = piece(NT * H * NK)
        e80 = piece(NT * H * NK)
        ap_ = piece(NT * 128).rearrange("p (t c) -> p t c", t=NT)
        mcnt = piece(2 * M)
        mif_sb = piece(2 * M).bitcast(i32)
        at[0] = 0
        KB = piece(ATT * B * G * HG * M, bf16)[0:96].rearrange("p (a b g h m) -> p a b g h m", a=ATT, b=B, g=G, h=HG)
        V9 = piece(ATT * B * H * 9)[0:M].rearrange("p (a b h c) -> p a b h c", a=ATT, b=B, h=H)
        f2_sb = piece(offsets(F2_W)[1])
        F2 = packed(f2_sb, F2_W)
        kf = piece(G * M)[0:96]
        kst = piece(G * M, bf16)[0:96]
        selN = piece(H * M, bf16)[0:32].rearrange("p (h m) -> p h m", h=H)
        uw = piece(NT * H * 9).rearrange("p (t h c) -> p t h c", t=NT, h=H)
        base[0], at[0] = f0_sb, 0
        zTf = piece(T)[0:M]
        ik_sb = piece(NT * M).bitcast(i32).rearrange("p (t m) -> p t m", t=NT)
        ikT_sb = piece(T).bitcast(i32)[0:M]
        z = piece(NT * M, bf16).rearrange("p (t m) -> p t m", t=NT)
        zT = piece(T, bf16)[0:M]
        gst = sb("gst", [96, T], bf16)

        refl = sb("refl", [128, 8])
        bq_s = sb("bq_s", [128, 4])
        Lb = sb("Lb", [128, 2, 8])
        s64 = sb("s64", [128, 3, NT * H])

        hm_bf = sb("hm_bf", [96, HG], bf16)
        bqs = sb("bqs", [96, ATT, G])
        nmx = sb("nmx", [128, NT, H])
        nst = sb("nst", [128, NT, 2, H], bf16)
        am_sb = sb("am_sb", [128, NT, M])
        amT_sb = sb("amT_sb", [M, T])
        mb8T = sb("mb8T", [M, B], i32)
        mb8 = sb("mb8", [128, B * M], i32)
        pad_row = sb("pad_row", [128, B * M])
        padT = sb("padT", [M, B])
        zany = sb("zany", [128, 3, NT])
        w0z = sb("w0z", [128, NT, H])
        rden = sb("rden", [128, NT, H])

        lg = sb("lg", [128, 5, NT, 16])
        g4 = sb("g4", [128, 4, NT])
        oh12 = sb("oh12", [128, B, NT, 2, 8], bf16)
        k12 = sb("k12", [128, NT, 2, 8])
        gate = sb("gate", [128, NT, 16])
        sel0 = sb("sel0", [96, 16, 64], bf16)
        sel1 = sb("sel1", [96, 8, 128], bf16)
        b2x = sb("b2x", [128, 2])

        ps = ctx.enter_context(nc.psum_tensor("ps", [128, 8, 512], f32))

        def dma_sem(name):
            return ctx.enter_context(nc.semaphore(name))

        in_first, in_l0, in_rows, in_att, in_f0, in_f1, in_f2, in_f3, in_masks, in_big, in_ik = (dma_sem(n) for n in (
            "x_and_consts_in", "layer0_weights_in", "bias_rows_in", "attention_weights_in", "ffn0_weights_in",
            "ffn1_weights_in", "ffn2_weights_in", "ffn3_biases_in", "masks_in", "ffn3_weights_in", "overwrite_mask_in"))
        out_sem = dma_sem("out_stored")
        consts_ready = signal("consts_ready", 1)
        dve_consts = signal("dve_consts", 1)
        gates_tanh = signal("gates_tanh", 1)
        dve_step = ctx.enter_context(nc.semaphore("dve_step"))
        act_step = ctx.enter_context(nc.semaphore("act_step"))
        pool_step = ctx.enter_context(nc.semaphore("pool_step"))
        steps = {"dve": 0, "act": 0, "pool": 0}

        ln_mean = signal("ln_mean", 8, B)
        ln_centered = signal("ln_centered", 8, B)
        ln_squared = signal("ln_squared", 8, B)
        ln_var = signal("ln_var", 8, B)
        ln_log = signal("ln_log", 8, B)
        ln_rstd = signal("ln_rstd", 8, B)
        xn_ready = signal("xn_ready", 8, B)
        out_done = signal("out_done", 6, B)
        out_read = signal("out_read", 8, B)
        residual = signal("residual", 8, B)

        tab_done = signal("tab_done", B)
        tab_ready = signal("tab_ready", B)
        qp_done = signal("qp_done", B)
        qp_ready = signal("qp_ready", B)
        off_done = signal("off_done", B)
        off_read = signal("off_read", B)
        qrep_done = signal("qrep_done", B, G)
        qrep_ready = signal("qrep_ready", B, G)
        ix_ready = signal("ix_ready", B)
        U = G * NK
        bc_done = signal("bc_done", B, U, 2)
        ib_ready = signal("ib_ready", B, G, 3, 2)
        oh_ready = signal("oh_ready", B, U, 2)
        gather_done = signal("gather_done", B, U)
        wf_done = signal("wf_done", B, U)
        wf_ready = signal("wf_ready", B, U)
        gw_ready = signal("gw_ready", B, U)
        tq_ready = signal("tq_ready", B, U)
        score_done = signal("score_done", B, U)
        s_shifted = signal("s_shifted", B)
        s_exp = signal("s_exp", B)
        a_ready = signal("a_ready", B)
        aT_done = signal("aT_done", B)
        aT_ready = signal("aT_ready", B)
        ab_done = signal("ab_done", B, U)
        t2_ready = signal("t2_ready", B, U)
        t2_used = signal("t2_used", B, U)

        k_done = signal("k_done", ATT, B)
        kf_ready = signal("kf_ready", ATT, B)
        kb_ready = signal("kb_ready", ATT, B)
        v_done = signal("v_done", ATT, B)
        v_ready = signal("v_ready", ATT, B)
        q_done = signal("q_done", ATT, B, G)
        qf_ready = signal("qf_ready", ATT, B, G)
        qst_ready = signal("qst_ready", ATT, B)
        st_done = signal("st_done", ATT, B, NT)
        st_read = signal("st_read", ATT, B, NT)
        nst_ready = signal("nst_ready", ATT, B)
        nT_done = signal("nT_done", ATT, B)
        nT_ready = signal("nT_ready", ATT, B)
        sT_done = signal("sT_done", ATT, B, H)
        bT_ready = signal("bT_ready", B, H)
        pT_ready = signal("pT_ready", ATT, B, H)
        pv_done = signal("pv_done", ATT, B, H)
        o_norm = signal("o_norm", ATT, B)
        oT_done = signal("oT_done", ATT, B)
        oT_ready = signal("oT_ready", ATT, B)
        amp_ready = signal("amp_ready", 1)
        w0_shift = signal("w0_shift", B)
        w0_ready = signal("w0_ready", B)
        u_done = signal("u_done", B)
        u_read = signal("u_read", B)
        z_ready = signal("z_ready", 1)
        bqs_ready = signal("bqs_ready", 1)
        pad_ready = signal("pad_ready", 1)
        v_ones = signal("v_ones", 1)

        lg_done = signal("lg_done", 3, B)
        lg_shift = signal("lg_shift", 3, B)
        lg_exp = signal("lg_exp", 3, B)
        oh12_ready = signal("oh12_ready", B)
        cum_done = signal("cum_done", B)
        gate_ready = signal("gate_ready", 3, B)
        gT_done = signal("gT_done", 3, B)
        gst_ready = signal("gst_ready", 3, B)
        gb_done = signal("gb_done", 2, B, 8)
        gbc_ready = signal("gbc_ready", 2, B, 8)
        up0_done = signal("up0_done", B, 9)
        gelu0 = signal("gelu0", B, 9)
        ga_done = signal("ga_done", B, 8)
        hg_ready = signal("hg_ready", B, 8)
        dn0_done = signal("dn0_done", B, 9)
        up1_done = signal("up1_done", B, 16)
        silu1 = signal("silu1", B, 16)
        hh_ready = signal("hh_ready", B, 16)
        dn1_done = signal("dn1_done", B, 16)
        yg_ready = signal("yg_ready", 2, B, 8)
        acc_ready = signal("acc_ready", 2, B, 8)
        up2_done = signal("up2_done", B, 4)
        q2_ready = signal("q2_ready", B, 4)
        gelu2 = signal("gelu2", B, 4)
        h2_ready = signal("h2_ready", B, 4)
        up3_done = signal("up3_done", B, 32)
        relu3 = signal("relu3", B, 32)
        dn3_done = signal("dn3_done", B, 32)

        block = ctx.enter_context(nc.Block())
        PSQ = [ps[:, k, :] for k in range(8)]

        @block.sync
        def _(sp):
            sp.dma_start(x[:, :, :], xT.rearrange("p (b t) -> p b t", b=B)).then_inc(in_first, 16)
            sp.dma_start(const_sb[:, :], const).then_inc(in_first, 16)
            sp.dma_start(mif_sb[:, :], mif).then_inc(in_first, 16)
            sp.dma_start(g_raw[:, :], g8).then_inc(in_first, 16)
            sp.dma_start(l0_sb[:, :], l0).then_inc(in_l0, 16)
            sp.dma_start(rows_sb[:, :], rows).then_inc(in_rows, 16)
            sp.dma_start(f0_sb[:, :], f0).then_inc(in_f0, 16)
            for dst, src in ((am_sb[:, :, :], am_tok), (amT_sb[:, :], am_T), (mb8[:, :], mbf_tok), (mb8T[:, :], mbf_T)):
                sp.dma_start(dst, src).then_inc(in_masks, 16)
            sp.dma_start(f3_sb[:, :], f3).then_inc(in_f3, 16)
            sp.wait_ge(*out_read.after(0, B - 1))
            sp.dma_start(att_sb, att.rearrange("p (a n) -> p a n", a=ATT)).then_inc(in_att, 16)
            sp.dma_start(f1_sb[:, :], f1).then_inc(in_f1, 16)
            sp.dma_start(f2_sb[:, :], f2).then_inc(in_f2, 16)
            sp.dma_start(f3w, f3big).then_inc(in_big, 16)
            sp.wait_ge(*out_read.after(1, B - 1))
            sp.dma_start(ik_sb, ik_tok).then_inc(in_ik, 16)
            sp.dma_start(ikT_sb, ik_T).then_inc(in_ik, 16)
            for b in range(B):
                sp.wait_ge(*residual.after(7, b))
                sp.dma_start(outT[:, b * T:(b + 1) * T], x[:, b, :]).then_inc(out_sem, 16)
            sp.wait_ge(out_sem, 16 * B)

        @block.tensor
        def _(pe):
            def layernorm(s, b):
                if s == 0:
                    if b == 0:
                        pe.wait_ge(in_first, 64)
                        pe.wait_ge(*consts_ready.after(0))
                else:
                    pe.wait_ge(*residual.after(s - 1, b))
                if (s, b) != (0, 0):
                    pe.wait_ge(*ln_log.after(s if b else s - 1, 1 - b))
                E.matmul(PSQ[7], mean_w[:, :], x[:, b, :], start=True, stop=True).then_inc(ln_mean.sem, 1)
                pe.wait_ge(*ln_squared.after(s, b))
                E.matmul(PSQ[7], mean_w[:, :], sq[:, :], start=True, stop=True).then_inc(ln_var.sem, 1)

            def after_branch(s, b):
                if (s, b) != (0, 0):
                    pe.wait_ge(*out_read.after(s if b else s - 1, 1 - b))

            def l0_front(b):
                if b:
                    pe.wait_ge(*qrep_ready.after(0, G - 1))
                    pe.wait_ge(*tab_ready.after(0))
                    pe.wait_ge(*off_read.after(0))
                else:
                    pe.wait_ge(in_l0, 16)
                    pe.wait_ge(in_rows, 16)
                for slot in range(2):
                    out = PSQ[0][0:MO, slot * 256:(slot + 1) * 256]
                    c0 = b * (M + 2) + slot
                    E.matmul(out, L0("ctx")[:, c0:c0 + MO], L0("wkv"), start=True, stop=False)
                    last = E.matmul(out, R("valid")[:, slot * MO:(slot + 1) * MO], R("bkv"), start=False, stop=True)
                last.then_inc(tab_done.sem, 1)
                pe.wait_ge(*xn_ready.after(0, b))
                E.matmul(PSQ[1], L0("wq"), xn[:, b, :], start=True, stop=True).then_inc(qp_done.sem, 1)
                pe.wait_ge(*qp_ready.after(b))
                E.matmul(PSQ[2], L0("woff"), qp, start=True, stop=True).then_inc(off_done.sem, 1)
                for g in range(G):
                    if g >= 2:
                        pe.wait_ge(*qrep_ready.after(b, g - 2))
                    E.matmul(PSQ[3 + g % 2], L0("wqrep")[:, g * 128:(g + 1) * 128], xn[:, b, :],
                             start=True, stop=True).then_inc(qrep_done.sem, 1)

            def l0_gather(b):
                def spread(u, g, k):
                    for p in range(2):
                        if u:
                            pe.wait_ge(*oh_ready.after(b, u - 1, p))
                        elif b:
                            pe.wait_ge(*oh_ready.after(b - 1, U - 1, p))
                        for i in range(2):
                            r = NK * (2 * p + i) + k
                            last = E.matmul(PSQ[2 * p + i][0:MO, :], selB[32 * g:32 * g + 32, r, :],
                                            i0bf[32 * g:32 * g + 32, b, :], start=True, stop=True,
                                            tile_position=(32 * g, 0))
                        last.then_inc(bc_done.sem, 1)
                    if u:
                        pe.wait_ge(*wf_ready.after(b, u - 1))
                    elif b:
                        pe.wait_ge(*wf_ready.after(b - 1, U - 1))
                    E.matmul(PSQ[5], selW[32 * g:32 * g + 32, k, :], w1hi[32 * g:32 * g + 32, b, :],
                             start=True, stop=False, tile_position=(32 * g, 0))
                    E.matmul(PSQ[5], selW[32 * g:32 * g + 32, k, :], w1lo[32 * g:32 * g + 32, b, :],
                             start=False, stop=True, tile_position=(32 * g, 0)).then_inc(wf_done.sem, 1)

                def gather(u, g, k):
                    if u:
                        pe.wait_ge(*gw_ready.after(b, u - 1))
                    elif b:
                        pe.wait_ge(*gw_ready.after(b - 1, U - 1))
                    for p in range(2):
                        pe.wait_ge(*oh_ready.after(b, u, p))
                        for part in range(2):
                            for i in range(2):
                                h = 2 * p + i
                                last = E.matmul(PSQ[4][32 * h:32 * h + 32, :], tab[:, b, part, HG * g + h, :],
                                                oh[:, u % 2, p, i * T:(i + 1) * T], start=part == 0, stop=part == 1,
                                                tile_position=(0, 32 * h))
                    last.then_inc(gather_done.sem, 1)

                def score(u, g, k):
                    pe.wait_ge(*tq_ready.after(b, u))
                    if u == 0 and b:
                        pe.wait_ge(*s_shifted.after(b - 1))
                    sc = PSQ[6][:, 0:NT * H * NK].rearrange("p (t h k) -> p t h k", t=NT, h=H)
                    for t in range(NT):
                        last = E.matmul(sc[:, t, HG * g:HG * g + HG, k], tq[:, u % 3, t * 128:(t + 1) * 128],
                                        C("selS"), start=True, stop=True)
                    last.then_inc(score_done.sem, 1)

                units = [(g * NK + k, g, k) for g in range(G) for k in range(NK)]
                pe.wait_ge(*ix_ready.after(B - 1))
                pe.wait_ge(*tab_ready.after(B - 1))
                pe.wait_ge(*qrep_ready.after(B - 1, G - 1))
                spread(*units[0])
                for n in range(U):
                    if n + 1 < U:
                        spread(*units[n + 1])
                    gather(*units[n])
                    if n:
                        score(*units[n - 1])
                score(*units[U - 1])

            def l0_back(b):
                pe.wait_ge(*a_ready.after(b))
                if b == 0:
                    pe.wait_ge(*gw_ready.after(B - 1, U - 1))
                    pe.wait_ge(*s_shifted.after(B - 1))
                else:
                    pe.wait_ge(*out_read.after(0, 0))
                for t in range(NT):
                    last = E.transpose(PSQ[0][:, t * 128:(t + 1) * 128], ap_[:, t, :], C("ident"))
                last.then_inc(aT_done.sem, 1)
                pe.wait_ge(*aT_ready.after(b))

                def project(u):
                    pe.wait_ge(*t2_ready.after(b, u))
                    g = u // NK
                    last = E.matmul(PSQ[6], L0("worep")[:, g * 128:(g + 1) * 128], GW[:, b, u, :],
                                    start=u == 0, stop=u == U - 1)
                    last.then_inc(*((out_done.sem, 1) if u == U - 1 else (t2_used.sem, 1)))

                for u in range(U):
                    g, k = u // NK, u % NK
                    if u >= 3:
                        pe.wait_ge(*t2_ready.after(b, u - 3))
                    E.matmul(PSQ[1 + u % 3], selA[32 * g:32 * g + 32, k, :], ahi[32 * g:32 * g + 32, :],
                             start=True, stop=False, tile_position=(32 * g, 0))
                    E.matmul(PSQ[1 + u % 3], selA[32 * g:32 * g + 32, k, :], alo[32 * g:32 * g + 32, :],
                             start=False, stop=True, tile_position=(32 * g, 0)).then_inc(ab_done.sem, 1)
                    if u >= 2:
                        project(u - 2)
                project(U - 2)
                project(U - 1)

            def kv_prepare(a, b):
                if (a, b) == (0, 0):
                    pe.wait_ge(in_att, 16)
                else:
                    pe.wait_ge(*kf_ready.after(a if b else a - 1, 1 - b))
                    pe.wait_ge(*v_ready.after(a if b else a - 1, 1 - b))
                c0 = b * (M + 2) + 1
                for g in range(G):
                    last = E.matmul(PSQ[0][0:96, g * M:(g + 1) * M], AW[a]("wk")[:, g * 96:(g + 1) * 96],
                                    L0("ctx")[:, c0:c0 + M], start=True, stop=True)
                last.then_inc(k_done.sem, 1)
                E.matmul(PSQ[1][0:M, 0:128], L0("ctx")[:, c0:c0 + M], AW[a]("wv"), start=True, stop=False)
                E.matmul(PSQ[1][0:M, 0:128], ones_row[:, 0:M], R("bv")[:, a * 128:(a + 1) * 128],
                         start=False, stop=True).then_inc(v_done.sem, 1)

            def attention(a, b):
                s = 2 * a + 2
                after_branch(s, b)
                pe.wait_ge(*xn_ready.after(s, b))
                for g in range(G):
                    if g >= 2:
                        pe.wait_ge(*qf_ready.after(a, b, g - 2))
                    E.matmul(PSQ[g % 2][0:96, :], AW[a]("wq")[:, g * 96:(g + 1) * 96], xn[:, b, :],
                             start=True, stop=True).then_inc(q_done.sem, 1)
                if a == 2:
                    pe.wait_ge(*z_ready.after(0))
                    pe.wait_ge(*v_ones.after(0))
                    for t in range(NT):
                        last = E.matmul(PSQ[4 + t // 2][:, (t % 2) * 144:(t % 2) * 144 + 144],
                                        zTf[:, t * 128:(t + 1) * 128],
                                        V9[:, a, b, :, :].rearrange("m h c -> m (h c)"), start=True, stop=True)
                    last.then_inc(u_done.sem, 1)
                pe.wait_ge(*qst_ready.after(a, b))
                pe.wait_ge(*kb_ready.after(a, b))
                if a == 2:
                    pe.wait_ge(*u_read.after(b))
                for t in range(NT):
                    if t:
                        pe.wait_ge(*st_read.after(a, b, t - 1))
                    for g in range(G):
                        out = PSQ[2 + g][:, 0:HG * M]
                        last = E.matmul(out, qst[0:96, g, t * 128:(t + 1) * 128],
                                        KB[:, a, b, g, :, :].rearrange("p h m -> p (h m)"), start=True, stop=a != 2)
                        if a == 2:
                            last = E.matmul(out.rearrange("p (h m) -> p h m", h=HG), neg_ident[:, :],
                                            z[:, t, :].unsqueeze(1).broadcast_to([128, HG, M]), start=False, stop=True)
                    last.then_inc(st_done.sem, 1)
                pe.wait_ge(*nst_ready.after(a, b))
                for t in range(NT):
                    last = E.matmul(PSQ[0][0:32, t * 128:(t + 1) * 128], nst[:, t, :, :].rearrange("p a h -> p (a h)"),
                                    ident_bf[:, :], start=True, stop=True)
                last.then_inc(nT_done.sem, 1)
                pe.wait_ge(*nT_ready.after(a, b))
                pe.wait_ge(*bqs_ready.after(0))
                pe.wait_ge(*st_read.after(a, b, NT - 1))

                def scores_T(h):
                    if h >= 4:
                        if a == 0:
                            pe.wait_ge(*bT_ready.after(b, h - 4))
                        else:
                            pe.wait_ge(*pT_ready.after(a, b, h - 4))
                    out = PSQ[h % 4][0:M, :]
                    E.matmul(out, KB[:, a, b, h // HG, h % HG, :], qst[0:96, h // HG, :], start=True, stop=False)
                    last = E.matmul(out, selN[:, h, :], nT[0:32, :], start=False, stop=a != 2)
                    if a == 2:
                        last = E.matmul(out, neg_ident[0:M, 0:M], zT[:, :], start=False, stop=True)
                    last.then_inc(sT_done.sem, 1)

                def values(h):
                    pe.wait_ge(*pT_ready.after(a, b, h))
                    if h == 0:
                        pe.wait_ge(*v_ready.after(a, b))
                        pe.wait_ge(*v_ones.after(0))
                    for t in range(NT):
                        c = (t % 2) * 144 + h * 9
                        last = E.matmul(PSQ[4 + t // 2][:, c:c + 9], pT[0:M, h % 4, t * 128:(t + 1) * 128],
                                        V9[:, a, b, h, :], start=True, stop=True)
                    last.then_inc(pv_done.sem, 1)

                for h in range(H):
                    scores_T(h)
                    if h >= 3:
                        values(h - 3)
                for h in range(H - 3, H):
                    values(h)
                pe.wait_ge(*o_norm.after(a, b))
                for t in range(NT):
                    last = E.transpose(PSQ[0][:, t * 128:(t + 1) * 128], oN[:, t, :], C("ident"))
                last.then_inc(oT_done.sem, 1)
                pe.wait_ge(*oT_ready.after(a, b))
                E.matmul(PSQ[6], AW[a]("wo"), oT, start=True, stop=True).then_inc(out_done.sem, 1)

            def gates(r, s, b, rw, bias):
                ne = GATES[r][0]
                after_branch(s, b)
                pe.wait_ge(*xn_ready.after(s, b))
                for t in range(NT):
                    out = PSQ[1][:, t * ne:(t + 1) * ne]
                    last = E.matmul(out, xn[:, b, t * 128:(t + 1) * 128], rw, start=True, stop=bias is None)
                    if bias is not None:
                        last = E.matmul(out, ones_row[:, :], bias, start=False, stop=True)
                last.then_inc(lg_done.sem, 1)
                if r == 2:
                    pe.wait_ge(*oh12_ready.after(b))
                    for t in range(NT):
                        out = PSQ[2][:, t * 16:(t + 1) * 16]
                        before = [(bb, tt) for bb in range(B) for tt in range(NT) if (bb, tt) < (b, t)]
                        last = E.matmul(out, tri_bf[:, :], oh12[:, b, t, :, :].rearrange("p c e -> p (c e)"),
                                        start=True, stop=not before)
                        for n, (bb, tt) in enumerate(before):
                            last = E.matmul(out, ones_bf[:, :], oh12[:, bb, tt, :, :].rearrange("p c e -> p (c e)"),
                                            start=False, stop=n == len(before) - 1)
                    last.then_inc(cum_done.sem, 1)
                pe.wait_ge(*gate_ready.after(r, b))
                for t in range(NT):
                    last = E.transpose(PSQ[0][0:ne, t * 128:(t + 1) * 128], gate[:, t, 0:ne], C("ident"))
                last.then_inc(gT_done.sem, 1)
                pe.wait_ge(*gst_ready.after(r, b))
                if r:
                    for e in range(8):
                        if e >= 2:
                            pe.wait_ge(*gbc_ready.after(r - 1, b, e - 2))
                        E.matmul(PSQ[2 + e % 2], sel1[:, e, :], gst[:, :], start=True,
                                 stop=True).then_inc(gb_done.sem, 1)
                    pe.wait_ge(*gbc_ready.after(r - 1, b, 7))

            def ffn0(b):
                if b == 0:
                    pe.wait_ge(in_f0, 16)
                gates(0, 1, b, F0("rw"), None)

                def down(j):
                    if j:
                        pe.wait_ge(*hg_ready.after(b, j - 1))
                    else:
                        pe.wait_ge(*gelu0.after(b, 0))
                    src = hid[:, 0, :] if j == 0 else hid2[:, j % 4, :]
                    last = E.matmul(PSQ[6], F0("down")[:, j * 128:(j + 1) * 128], src, start=j == 0, stop=j == 8)
                    last.then_inc(*((out_done.sem, 1) if j == 8 else (dn0_done.sem, 1)))

                for j in range(9):
                    if j >= 2:
                        pe.wait_ge(*gelu0.after(b, j - 2))
                    E.matmul(PSQ[2 + j % 2], F0("up")[:, j * 128:(j + 1) * 128], xn[:, b, :], start=True,
                             stop=True).then_inc(up0_done.sem, 1)
                    if j:
                        if j >= 3:
                            pe.wait_ge(*hg_ready.after(b, j - 3))
                        E.matmul(PSQ[4 + j % 2], sel0[:, 2 * j - 2:2 * j, :].rearrange("p a c -> p (a c)"), gst[:, :],
                                 start=True, stop=True).then_inc(ga_done.sem, 1)
                    if j >= 2:
                        down(j - 2)
                down(7)
                down(8)

            def ffn1(b):
                if b == 0:
                    pe.wait_ge(in_f1, 16)
                gates(1, 3, b, F1("rw"), None)

                def down(n):
                    e = n // 2
                    pe.wait_ge(*hh_ready.after(b, n))
                    if n % 2 == 0 and e >= 2:
                        pe.wait_ge(*yg_ready.after(0, b, e - 2))
                    E.matmul(PSQ[4 + e % 2], F1("w2")[:, n * 128:(n + 1) * 128], hid2[:, n % 4, :],
                             start=n % 2 == 0, stop=n % 2 == 1).then_inc(dn1_done.sem, 1)

                for n in range(16):
                    if n >= 2:
                        pe.wait_ge(*hh_ready.after(b, n - 2))
                    E.matmul(PSQ[n % 2], F1("w1")[:, n * 128:(n + 1) * 128], xn[:, b, :], start=True, stop=True)
                    E.matmul(PSQ[2 + n % 2], F1("w3")[:, n * 128:(n + 1) * 128], xn[:, b, :], start=True,
                             stop=True).then_inc(up1_done.sem, 1)
                    if n >= 2:
                        down(n - 2)
                down(14)
                down(15)

            def ffn2(b):
                if b == 0:
                    pe.wait_ge(in_f2, 16)
                after_branch(5, b)
                pe.wait_ge(*xn_ready.after(5, b))
                for j in range(4):
                    E.matmul(PSQ[j], F2("w1")[:, j * 128:(j + 1) * 128], xn[:, b, :], start=True,
                             stop=True).then_inc(up2_done.sem, 1)
                for j in range(4):
                    pe.wait_ge(*h2_ready.after(b, j))
                    last = E.matmul(PSQ[6], F2("w2")[:, j * 128:(j + 1) * 128], hid2[:, j, :], start=j == 0,
                                    stop=j == 3)
                last.then_inc(out_done.sem, 1)

            def ffn3(b):
                if b == 0:
                    pe.wait_ge(in_f3, 16)
                gates(2, 7, b, F3("rw"), R("gb"))
                if b == 0:
                    pe.wait_ge(in_big, 16)

                def down(n):
                    e, j = n // 4, n % 4
                    pe.wait_ge(*relu3.after(b, n))
                    if j == 0 and e >= 2:
                        pe.wait_ge(*yg_ready.after(1, b, e - 2))
                    E.matmul(PSQ[4 + e % 2], F3B("w2")[:, n * 128:(n + 1) * 128], hid2[:, n % 4, :],
                             start=j == 0, stop=j == 3).then_inc(dn3_done.sem, 1)

                for n in range(32):
                    if n >= 4:
                        pe.wait_ge(*relu3.after(b, n - 4))
                    E.matmul(PSQ[n % 4], F3B("w1")[:, n * 128:(n + 1) * 128], xn[:, b, :], start=True,
                             stop=True).then_inc(up3_done.sem, 1)
                    if n >= 2:
                        down(n - 2)
                down(30)
                down(31)

            layernorm(0, 0)
            layernorm(0, 1)
            l0_front(0)
            l0_front(1)
            l0_gather(0)
            l0_gather(1)
            l0_back(0)
            l0_back(1)
            stages = [None, ffn0, lambda b: attention(0, b), ffn1, lambda b: attention(1, b), ffn2,
                      lambda b: attention(2, b), ffn3]
            for s in range(1, 8):
                layernorm(s, 0)
                layernorm(s, 1)
                if s == 2:
                    after_branch(2, 0)
                    for a in range(ATT):
                        for b in range(B):
                            kv_prepare(a, b)
                    pe.wait_ge(*kf_ready.after(ATT - 1, B - 1))
                    pe.wait_ge(*v_ready.after(ATT - 1, B - 1))
                stages[s](0)
                stages[s](1)

        def big_gelu(j):
            return gbc[:, j % 4, :]

        def y01(j, i):
            return gbc[:, 2 * (j % 2) + i, :]

        def qlow(j):
            return gbc[:, 4 + j % 2, :]

        @block.scalar
        def _(act):
            def link(ins):
                steps["act"] += 1
                ins.then_inc(act_step, 1)
                act.wait_ge(act_step, steps["act"])

            def layernorm(s, b):
                act.wait_ge(*ln_centered.after(s, b))
                if (s, b) != (0, 0):
                    act.wait_ge(*ln_var.after(s if b else s - 1, 1 - b))
                A.activation(sq[:, :], xc[:, b, :], ACT.Square).then_inc(ln_squared.sem, 1)
                act.wait_ge(*ln_var.after(s, b))
                if (s, b) != (0, 0):
                    act.wait_ge(*xn_ready.after(s if b else s - 1, 1 - b))
                A.activation(rstd[:, :], PSQ[7], ACT.Ln, bias=eps_col[:, :]).then_inc(ln_log.sem, 1)
                act.wait_ge(*ln_log.after(s, b))
                A.activation(rstd[:, :], rstd[:, :], ACT.Exp, scale=-0.5).then_inc(ln_rstd.sem, 1)

            S0 = 0.5 / HD ** 0.5

            def l0_front(b):
                act.wait_ge(*qp_done.after(b))
                if b:
                    act.wait_ge(*off_done.after(b - 1))
                else:
                    act.wait_ge(in_l0, 16)
                    act.wait_ge(*dve_consts.after(0))
                A.activation(qp, PSQ[1], ACT.Identity, bias=L0("bq")).then_inc(qp_ready.sem, 1)
                for g in range(G):
                    act.wait_ge(*qrep_done.after(b, g))
                    A.activation(qrep[:, b, g, :], PSQ[3 + g % 2], ACT.Identity, bias=bq_s[:, g:g + 1],
                                 scale=S0).then_inc(qrep_ready.sem, 1)

            def l0_gather(b):
                for u in range(U):
                    g, k = u // NK, u % NK
                    if k < 3:
                        for p in range(2):
                            act.wait_ge(*bc_done.after(b, u, p))
                            n = (b * G + g) * 3 + k
                            if n:
                                prev = (b, u - 1) if k else ((b, u - 3) if u else (b - 1, U - 3))
                                act.wait_ge(*oh_ready.after(prev[0], prev[1], p))
                            A.activation(ib[:, p, :], ps[0:MO, 2 * p:2 * p + 2, :], ACT.Copy).then_inc(ib_ready.sem, 1)
                    act.wait_ge(*wf_done.after(b, u))
                    if u >= 2:
                        act.wait_ge(*gw_ready.after(b, u - 2))
                    elif b:
                        act.wait_ge(*gw_ready.after(b - 1, U - 2 + u))
                    A.activation(at_wf[:, u % 2, :], PSQ[5], ACT.Identity, bias=C("patWb")).then_inc(wf_ready.sem, 1)

            def l0_softmax(b):
                act.wait_ge(*s_shifted.after(b))
                A.activation(e80, s80, ACT.Exp).then_inc(s_exp.sem, 1)

            def kv_prepare(a, b):
                act.wait_ge(*k_done.after(a, b))
                if (a, b) == (0, 0):
                    act.wait_ge(in_att, 16)
                else:
                    act.wait_ge(*kb_ready.after(a if b else a - 1, 1 - b))
                fn = ACT.Relu if a == 1 else ACT.Identity
                for g in range(G):
                    last = A.activation(kf[:, g * M:(g + 1) * M], PSQ[0][0:96, g * M:(g + 1) * M], fn,
                                        bias=AW[a]("bk")[0:96, g:g + 1])
                last.then_inc(kf_ready.sem, 1)
                act.wait_ge(*v_done.after(a, b))
                A.activation(V9[:, a, b, :, 0:8], PSQ[1][0:M, 0:128].rearrange("m (h d) -> m h d", h=H), fn
                             ).then_inc(v_ready.sem, 1)

            def attention(a, b):
                fn = ACT.Relu if a == 1 else ACT.Identity
                if (a, b) == (0, 0):
                    act.wait_ge(*bqs_ready.after(0))
                for g in range(G):
                    act.wait_ge(*q_done.after(a, b, g))
                    A.activation(qf[0:96, g, :], PSQ[g % 2][0:96, :], fn, bias=bqs[:, a, g:g + 1],
                                 scale=HD ** -0.5).then_inc(qf_ready.sem, 1)
                if a == 2:
                    act.wait_ge(*w0_shift.after(b))
                    A.activation(w0z[:, :, :], nmx[:, :, :], ACT.Exp, bias=refl[:, 7:8]
                                 ).then_inc(w0_ready.sem, 1)
                act.wait_ge(*nT_done.after(a, b))
                A.activation(nT[0:32, :], PSQ[0][0:32, :], ACT.Copy).then_inc(nT_ready.sem, 1)
                for h in range(H):
                    if h >= 4:
                        act.wait_ge(*pv_done.after(a, b, h - 4))
                    if a == 0:
                        act.wait_ge(*bT_ready.after(b, h))
                        A.activation(pT[0:M, h % 4, :], bT[0:M, h % 3, :], ACT.Exp, bias=padT[:, b:b + 1]
                                     ).then_inc(pT_ready.sem, 1)
                    else:
                        act.wait_ge(*sT_done.after(a, b, h))
                        A.activation(pT[0:M, h % 4, :], PSQ[h % 4][0:M, :], ACT.Exp).then_inc(pT_ready.sem, 1)
                act.wait_ge(*oT_done.after(a, b))
                A.activation(oT, PSQ[0], ACT.Copy).then_inc(oT_ready.sem, 1)

            def gates(r, b):
                ne = GATES[r][0]
                act.wait_ge(*lg_shift.after(r, b))
                A.activation(lg[:, 1, :, 0:ne], lg[:, 0, :, 0:ne], ACT.Exp).then_inc(lg_exp.sem, 1)
                if r:
                    for e in range(8):
                        act.wait_ge(*gb_done.after(r - 1, b, e))
                        A.activation(gbc[:, e, :], PSQ[2 + e % 2], ACT.Copy).then_inc(gbc_ready.sem, 1)

            def ffn0(b):
                gates(0, b)
                for j in range(9):
                    act.wait_ge(*up0_done.after(b, j))
                    if j >= 4:
                        act.wait_ge(*hg_ready.after(b, j - 4))
                    dst = hid[:, 0, :] if j == 0 else big_gelu(j)
                    A.activation(dst, PSQ[2 + j % 2], ACT.Gelu).then_inc(gelu0.sem, 1)

            def ffn1(b):
                gates(1, b)
                for n in range(16):
                    act.wait_ge(*up1_done.after(b, n))
                    if n >= 3:
                        act.wait_ge(*hh_ready.after(b, n - 3))
                    A.activation(hid[:, n % 3, :], PSQ[n % 2], ACT.Silu).then_inc(silu1.sem, 1)

            def ffn2(b):
                for j in range(4):
                    act.wait_ge(*q2_ready.after(b, j))
                    if j >= 2:
                        act.wait_ge(*h2_ready.after(b, j - 2))
                    A.activation(y01(j, 0), qlow(j), ACT.Gelu, scale=0.25)
                    A.activation(y01(j, 1), qlow(j), ACT.Gelu, scale=0.25, bias=refl[:, 6:7]).then_inc(gelu2.sem, 1)

            def ffn3(b):
                gates(2, b)
                for n in range(32):
                    act.wait_ge(*up3_done.after(b, n))
                    if n >= 4:
                        act.wait_ge(*dn3_done.after(b, n - 4))
                    A.activation(hid2[:, n % 4, :], PSQ[n % 4], ACT.Relu, bias=F3("b1")[:, n:n + 1]
                                 ).then_inc(relu3.sem, 1)

            act.wait_ge(in_first, 64)
            act.wait_ge(*consts_ready.after(0))
            A.activation(tg[:, :], g_raw[:, :], ACT.Tanh).then_inc(gates_tanh.sem, 1)
            layernorm(0, 0)
            layernorm(0, 1)
            l0_front(0)
            l0_front(1)
            l0_gather(0)
            l0_softmax(0)
            l0_gather(1)
            l0_softmax(1)
            stages = [None, ffn0, lambda b: attention(0, b), ffn1, lambda b: attention(1, b), ffn2,
                      lambda b: attention(2, b), ffn3]
            for s in range(1, 8):
                layernorm(s, 0)
                layernorm(s, 1)
                if s == 2:
                    for a in range(ATT):
                        for b in range(B):
                            kv_prepare(a, b)
                stages[s](0)
                stages[s](1)

        @block.gpsimd
        def _(pool):
            def link(ins):
                steps["pool"] += 1
                ins.then_inc(pool_step, 1)
                pool.wait_ge(pool_step, steps["pool"])

            P.memset(mean_w[:, :], 1.0 / D)
            P.memset(ones_bf[:, :], 1.0)
            P.memset(ones_row[:, :], 1.0)
            P.memset(eps_col[:, :], EPS)
            P.memset(gst[:, :], 0.0)
            P.memset(ap_[:, :, :], 0.0)
            P.memset(refl[:, 6:7], 0.25)
            P.memset(refl[:, 7:8], -1e-9)
            P.iota(loc[:, :], [[1, T]], base=0, channel_multiplier=0, allow_small_or_imprecise_dtypes=True
                   ).then_inc(consts_ready.sem, 1)
            for b in range(B):
                for u in range(U):
                    pool.wait_ge(*gw_ready.after(b, u))
                    pool.wait_ge(*qrep_ready.after(b, u // NK))
                    n = b * U + u
                    if n >= 3:
                        pool.wait_ge(*score_done.after((n - 3) // U, (n - 3) % U))
                    P.tensor_tensor(tq[:, u % 3, :], GW[:, b, u, :], qrep[:, b, u // NK, :], ALU.mult
                                    ).then_inc(tq_ready.sem, 1)
            pool.wait_ge(*out_read.after(0, B - 1))
            P.memset(V9[:, :, :, :, 8:9], 1.0).then_inc(v_ones.sem, 1)
            pool.wait_ge(in_masks, 64)
            pool.wait_ge(*pad_ready.after(0))
            for b in range(B):
                last = P.tensor_tensor(amp[:, b, :, :], am_sb[:, :, :], pad_row[:, b * M:(b + 1) * M].unsqueeze(1)
                                       .broadcast_to([128, NT, M]), ALU.add)
            last.then_inc(amp_ready.sem, 1)

            def accumulate(r, b):
                for e in range(8):
                    pool.wait_ge(*yg_ready.after(r, b, e))
                    if e == 0:
                        if b:
                            pool.wait_ge(*residual.after(3 + 4 * r, b - 1))
                        P.tensor_copy(acc, yg[:, e % 2, :]).then_inc(acc_ready.sem, 1)
                    else:
                        pool.wait_ge(*acc_ready.after(r, b, e - 1))
                        P.tensor_tensor(acc, acc, yg[:, e % 2, :], ALU.add).then_inc(acc_ready.sem, 1)

            for r in range(2):
                for b in range(B):
                    accumulate(r, b)

        @block.vector
        def _(dve):
            def link(ins):
                steps["dve"] += 1
                ins.then_inc(dve_step, 1)
                dve.wait_ge(dve_step, steps["dve"])

            def layernorm(s, b):
                dve.wait_ge(*ln_mean.after(s, b))
                V.tensor_tensor(xc[:, b, :], x[:, b, :], PSQ[7], ALU.subtract).then_inc(ln_centered.sem, 1)
                dve.wait_ge(*ln_rstd.after(s, b))
                dve.wait_ge(*ln_centered.after(s, b))
                V.tensor_tensor(xn[:, b, :], xc[:, b, :], rstd[:, :], ALU.mult).then_inc(xn_ready.sem, 1)

            def add_branch(s, b, bias, relu=False):
                dve.wait_ge(*out_done.after(s - (s > 3), b))
                V.tensor_scalar(y_tmp[:, :], PSQ[6], bias, 0.0 if relu else None, ALU.add,
                                *((ALU.max,) if relu else ())).then_inc(out_read.sem, 1)
                dve.wait_ge(*out_read.after(s, b))
                V.scalar_tensor_tensor(x[:, b, :], y_tmp[:, :], tg[:, s:s + 1], x[:, b, :], ALU.mult, ALU.add
                                       ).then_inc(residual.sem, 1)

            def constants():
                dve.wait_ge(in_first, 64)
                dve.wait_ge(*consts_ready.after(0))
                V.tensor_copy(ident_bf[:, :], C("ident"))
                V.tensor_scalar(neg_ident[:, :], C("ident"), NEG, None, ALU.mult)
                V.tensor_copy(tri_bf[:, :], C("tri"))
                V.tensor_copy(hm_bf[:, :], C("headmask")[0:96, :])
                V.tensor_copy(selB[:, :, :], C("id32")[:, 0:20].unsqueeze(2).broadcast_to([128, 20, MO]))
                V.tensor_copy(sel0[:, :, :], C("id32")[0:96, 0:16].unsqueeze(2).broadcast_to([96, 16, 64]))
                V.tensor_copy(sel1[:, :, :], C("id32")[0:96, 0:8].unsqueeze(2).broadcast_to([96, 8, 128]))
                for k in range(NK):
                    src = C("id32")[:, k:20:NK].unsqueeze(2).broadcast_to([128, HG, 32])
                    for dst, pat in ((selA, "patA"), (selW, "patW")):
                        V.tensor_tensor(dst[:, k, :].rearrange("p (h c) -> p h c", h=HG), src,
                                        C(pat).rearrange("p (h c) -> p h c", h=HG), ALU.mult)
                link(V.tensor_copy(mcnt[:, :], mif_sb[:, :]))
                link(V.tensor_reduce(Lb[:, :, 0], mcnt[:, :].rearrange("p (b m) -> p b m", b=2), AX.X, ALU.add))
                link(V.tensor_scalar(Lb[:, :, 1], Lb[:, :, 0], -1.0, float(M - 1), ALU.mult, ALU.add))
                link(V.tensor_scalar(Lb[:, :, 2], Lb[:, :, 1], -1.0, None, ALU.mult))
                link(V.tensor_tensor(Lb[:, :, 3], Lb[:, :, 1], Lb[:, :, 2], ALU.max))
                link(V.tensor_scalar(Lb[:, :, 4], Lb[:, :, 1], 0.0, None, ALU.is_ge))
                link(V.tensor_scalar(Lb[:, :, 4], Lb[:, :, 4], 2.0, -1.0, ALU.mult, ALU.add))
                link(V.reciprocal(Lb[:, :, 5], Lb[:, :, 3]))
                link(V.tensor_scalar(Lb[:, :, 6], Lb[:, :, 3], -1.0, None, ALU.mult))
                link(V.tensor_scalar(Lb[:, :, 7], Lb[:, :, 4], M / (M - 1.0), None, ALU.mult))
                dve.wait_ge(in_l0, 16)
                V.tensor_scalar(bq_s[:, :], L0("bqrep"), 0.5 / HD ** 0.5, None, ALU.mult).then_inc(dve_consts.sem, 1)

            def l0_front(b):
                dve.wait_ge(*tab_done.after(b))
                src = PSQ[0][0:MO, :].rearrange("m (s h c) -> m s h c", s=2, h=H)
                for s in range(2):
                    last = V.tensor_copy(tab[:, b, 0, :, 16 * s:16 * s + 16], src[:, s])
                link(last)
                for s in range(2):
                    last = V.tensor_tensor(tab[:, b, 1, :, 16 * s:16 * s + 16], src[:, s],
                                           tab[:, b, 0, :, 16 * s:16 * s + 16], ALU.subtract)
                last.then_inc(tab_ready.sem, 1)
                dve.wait_ge(*off_done.after(b))
                L = Lb[:, b, :]
                V.tensor_scalar(ixt, PSQ[2], L0("boff"), C("refk"), ALU.add, ALU.add).then_inc(off_read.sem, 1)
                dve.wait_ge(*off_read.after(b))
                link(V.tensor_tensor(ixt, ixt, loc[:, :], ALU.add))
                link(V.tensor_scalar(ix1, ixt, L[:, 4:5], None, ALU.mult))
                link(V.tensor_scalar(ix2, ix1, L[:, 5:6], MAGIC, ALU.mult, ALU.add))
                link(V.tensor_scalar(ix2, ix2, -MAGIC, L[:, 6:7], ALU.add, ALU.mult))
                link(V.tensor_tensor(ix1, ix1, ix2, ALU.add))
                link(V.tensor_scalar(ix2, ix1, 0.0, L[:, 3:4], ALU.is_lt, ALU.mult))
                link(V.tensor_tensor(ix1, ix1, ix2, ALU.add))
                link(V.tensor_scalar(ix1, ix1, L[:, 7:8], -0.5, ALU.mult, ALU.add))
                link(V.tensor_scalar(ix2, ix1, MAGIC, -MAGIC, ALU.add, ALU.add))
                link(V.tensor_tensor(ixt, ix2, ix1, ALU.is_gt))
                link(V.tensor_tensor(ix2, ix2, ixt, ALU.subtract))
                link(V.tensor_tensor(ix1, ix1, ix2, ALU.subtract))
                V.tensor_scalar(i0bf[:, b, :], ix2, -2.0, float(M), ALU.max, ALU.min)
                link(V.tensor_copy(w1hi[:, b, :], ix1))
                V.tensor_tensor(w1lo[:, b, :], ix1, w1hi[:, b, :], ALU.subtract).then_inc(ix_ready.sem, 1)

            def l0_gather(b):
                def one_hots(u):
                    g, k = u // NK, u % NK
                    for p in range(2):
                        n = b * U + u
                        if n >= 2:
                            dve.wait_ge(*gather_done.after((n - 2) // U, (n - 2) % U))
                        if k < 3:
                            dve.wait_ge(*ib_ready.after(b, g, k, p))
                            src = ib[:, p, :]
                        else:
                            dve.wait_ge(*bc_done.after(b, u, p))
                            src = ps[0:MO, 2 * p:2 * p + 2, :].rearrange("m a t -> m (a t)")
                        V.tensor_scalar(oh[:, u % 2, p, :], src, C("pos")[0:MO, :], None, ALU.is_equal
                                        ).then_inc(oh_ready.sem, 1)

                def weigh(u):
                    dve.wait_ge(*gather_done.after(b, u))
                    dve.wait_ge(*wf_ready.after(b, u))
                    V.tensor_tensor(GW[:, b, u, :], PSQ[4], at_wf[:, u % 2, :], ALU.mult).then_inc(gw_ready.sem, 1)

                one_hots(0)
                for u in range(U):
                    if u + 1 < U:
                        one_hots(u + 1)
                    weigh(u)

            def l0_softmax(b):
                dve.wait_ge(*score_done.after(b, U - 1))
                sc = PSQ[6][:, 0:NT * H * NK].rearrange("p (n k) -> p n k", k=NK)
                s3 = s80.rearrange("p (n k) -> p n k", k=NK)
                e3 = e80.rearrange("p (n k) -> p n k", k=NK)
                link(V.tensor_reduce(s64[:, 0, :], sc, AX.X, ALU.max, negate=True))
                V.tensor_tensor(s3, sc, s64[:, 0, :].unsqueeze(2).broadcast_to([128, NT * H, NK]), ALU.add
                                ).then_inc(s_shifted.sem, 1)
                dve.wait_ge(*s_exp.after(b))
                link(V.tensor_reduce(s64[:, 1, :], e3, AX.X, ALU.add))
                link(V.reciprocal(s64[:, 2, :], s64[:, 1, :]))
                if b:
                    dve.wait_ge(*aT_done.after(b - 1))
                for t in range(NT):
                    for g in range(G):
                        n = t * H + g * HG
                        last = V.tensor_tensor(ap_[:, t, 32 * g:32 * g + 20].rearrange("p (h k) -> p h k", k=NK),
                                               e3[:, n:n + HG, :],
                                               s64[:, 2, n:n + HG].unsqueeze(2).broadcast_to([128, HG, NK]), ALU.mult)
                last.then_inc(a_ready.sem, 1)

            def l0_back(b):
                dve.wait_ge(*aT_done.after(b))
                link(V.tensor_copy(ahi, PSQ[0]))
                V.tensor_tensor(alo, PSQ[0], ahi, ALU.subtract).then_inc(aT_ready.sem, 1)
                for u in range(U):
                    dve.wait_ge(*ab_done.after(b, u))
                    V.tensor_tensor(GW[:, b, u, :], GW[:, b, u, :], PSQ[1 + u % 3], ALU.mult
                                    ).then_inc(t2_ready.sem, 1)
                add_branch(0, b, L0("bo"))

            def kv_prepare(a, b):
                dve.wait_ge(*kf_ready.after(a, b))
                link(V.tensor_copy(kst, kf))
                link(V.tensor_tensor(kst[64:96, :], kf[64:96, :], kst[64:96, :], ALU.subtract))
                for g in range(G):
                    last = V.tensor_tensor(KB[:, a, b, g, :, :],
                                           kst[:, g * M:(g + 1) * M].unsqueeze(1).broadcast_to([96, HG, M]),
                                           hm_bf[:, :].unsqueeze(2).broadcast_to([96, HG, M]), ALU.mult)
                last.then_inc(kb_ready.sem, 1)

            def pads():
                dve.wait_ge(in_masks, 64)
                V.tensor_scalar(pad_row[:, :], mb8[:, :], NEG, None, ALU.mult)
                V.tensor_scalar(padT[:, :], mb8T[:, :], NEG, None, ALU.mult).then_inc(pad_ready.sem, 1)

            def masks():
                dve.wait_ge(in_att, 16)
                for a in range(ATT):
                    V.tensor_scalar(bqs[:, a, :], AW[a]("bq")[0:96, :], HD ** -0.5, None, ALU.mult)
                V.tensor_copy(selN[:, :, :], C("id16")[0:32, :].unsqueeze(2).broadcast_to([32, H, M])
                              ).then_inc(bqs_ready.sem, 1)

            def overwritten_keys():
                dve.wait_ge(in_ik, 32)
                V.tensor_scalar(z[:, :, :], ik_sb[:, :, :], 0.0, None, ALU.is_equal)
                V.tensor_scalar(zT[:, :], ikT_sb[:, :], 0.0, None, ALU.is_equal)
                link(V.tensor_scalar(zTf, ikT_sb[:, :], 0.0, None, ALU.is_equal))
                link(V.tensor_reduce(zany[:, 0, :], z[:, :, :], AX.X, ALU.max))
                link(V.tensor_scalar(zany[:, 1, :], zany[:, 0, :], NEG, -NEG, ALU.mult, ALU.add))
                V.tensor_scalar(zany[:, 2, :], zany[:, 1, :], 1e-9, None, ALU.max).then_inc(z_ready.sem, 1)

            def attention(a, b):
                s = 2 * a + 2
                dve.wait_ge(*qf_ready.after(a, b, G - 1))
                link(V.tensor_copy(qst[0:96, :, :], qf[0:96, :, :]))
                V.tensor_tensor(qst[32:64, :, :], qf[32:64, :, :], qst[32:64, :, :], ALU.subtract
                                ).then_inc(qst_ready.sem, 1)
                if a == 2:
                    dve.wait_ge(*u_done.after(b))
                    for t in range(NT):
                        last = V.tensor_copy(uw[:, t, :, :].rearrange("p h c -> p (h c)"),
                                             PSQ[4 + t // 2][:, (t % 2) * 144:(t % 2) * 144 + 144])
                    last.then_inc(u_read.sem, 1)
                for t in range(NT):
                    dve.wait_ge(*st_done.after(a, b, t))
                    sc = ps[:, 2:6, 0:HG * M]
                    if a == 0:
                        dve.wait_ge(*amp_ready.after(0))
                        link(V.tensor_tensor(s_tok.rearrange("p (g h m) -> p g h m", g=G, h=HG),
                                             sc.rearrange("p g (h m) -> p g h m", h=HG),
                                             amp[:, b, t, :].unsqueeze(1).unsqueeze(1).broadcast_to([128, G, HG, M]),
                                             ALU.add))
                        src = s_tok.rearrange("p (h m) -> p h m", h=H)
                    else:
                        src = sc.rearrange("p g (h m) -> p g h m", h=HG)
                    V.tensor_reduce(nmx[:, t, :] if a == 0 else nmx[:, t, :].rearrange("p (g h) -> p g h", g=G),
                                    src, AX.X, ALU.max, negate=True).then_inc(st_read.sem, 1)
                dve.wait_ge(*st_read.after(a, b, NT - 1))
                if a == 2:
                    V.tensor_tensor(nmx[:, :, :], nmx[:, :, :], zany[:, 2, :].unsqueeze(2).broadcast_to([128, NT, H]),
                                    ALU.min).then_inc(w0_shift.sem, 1)
                    dve.wait_ge(*w0_shift.after(b))
                link(V.tensor_copy(nst[:, :, 0, :], nmx[:, :, :]))
                V.tensor_tensor(nst[:, :, 1, :], nmx[:, :, :], nst[:, :, 0, :], ALU.subtract).then_inc(nst_ready.sem, 1)
                if a == 2:
                    dve.wait_ge(*w0_ready.after(b))
                    dve.wait_ge(*u_read.after(b))
                    link(V.tensor_tensor(uw[:, :, :, :].rearrange("p t h c -> p (t h) c"),
                                         uw[:, :, :, :].rearrange("p t h c -> p (t h) c"),
                                         w0z[:, :, :].rearrange("p t h -> p (t h)").unsqueeze(2)
                                         .broadcast_to([128, NT * H, 9]), ALU.mult))
                if a == 0:
                    for h in range(H):
                        dve.wait_ge(*sT_done.after(a, b, h))
                        if h >= 3:
                            dve.wait_ge(*pT_ready.after(a, b, h - 3))
                        V.tensor_tensor(bT[0:M, h % 3, :], PSQ[h % 4][0:M, :], amT_sb[:, :], ALU.add
                                        ).then_inc(bT_ready.sem, 1)
                dve.wait_ge(*pv_done.after(a, b, H - 1))
                for half in range(2):
                    o9 = PSQ[4 + half][:, 0:288].rearrange("p (n c) -> p n c", c=9)
                    if a == 2:
                        u9 = uw[:, 2 * half:2 * half + 2, :, :].rearrange("p t h c -> p (t h) c")
                        link(V.tensor_tensor(u9, u9, o9, ALU.add))
                        o9 = u9
                    rd = rden[:, 2 * half:2 * half + 2, :].rearrange("p t h -> p (t h)")
                    link(V.reciprocal(rd, o9[:, :, 8]))
                    last = V.tensor_tensor(oN[:, 2 * half:2 * half + 2, :].rearrange("p t (h d) -> p (t h) d", h=H),
                                           o9[:, :, 0:8], rd.unsqueeze(2).broadcast_to([128, 2 * H, HD]), ALU.mult)
                last.then_inc(o_norm.sem, 1)
                add_branch(s, b, AW[a]("bo"), relu=a == 1)

            def gates(r, b):
                ne, topk = GATES[r]
                dve.wait_ge(*lg_done.after(r, b))
                lp = PSQ[1][:, 0:NT * ne].rearrange("p (t e) -> p t e", t=NT)
                sh, ex, p, rank, one = (lg[:, i, :, 0:ne] for i in range(5))

                def tok(i):
                    return g4[:, i, :].unsqueeze(2).broadcast_to([128, NT, ne])

                link(V.tensor_reduce(g4[:, 0, :], lp, AX.X, ALU.max, negate=True))
                V.tensor_tensor(sh, lp, tok(0), ALU.add).then_inc(lg_shift.sem, 1)
                dve.wait_ge(*lg_exp.after(r, b))
                link(V.tensor_reduce(g4[:, 1, :], ex, AX.X, ALU.add))
                link(V.reciprocal(g4[:, 2, :], g4[:, 1, :]))
                link(V.tensor_tensor(p, ex, tok(2), ALU.mult))
                cmp1 = big[:, 0:NT * ne * ne].rearrange("p (t e j) -> p t e j", t=NT, e=ne)
                cmp2 = big2[:, 0:NT * ne * ne].rearrange("p (t e j) -> p t e j", t=NT, e=ne)
                pj = p.unsqueeze(2).broadcast_to([128, NT, ne, ne])
                pe_ = p.unsqueeze(3).broadcast_to([128, NT, ne, ne])
                tie = C("tie").rearrange("p (e j) -> p e j", e=16)[:, 0:ne, 0:ne]
                V.tensor_tensor(cmp1, pj, pe_, ALU.is_gt)
                link(V.tensor_tensor(cmp2, pj, pe_, ALU.is_equal))
                link(V.tensor_tensor(cmp2, cmp2, tie.unsqueeze(1).broadcast_to([128, NT, ne, ne]), ALU.mult))
                link(V.tensor_tensor(cmp1, cmp1, cmp2, ALU.add))
                link(V.tensor_reduce(rank, cmp1, AX.X, ALU.add))
                ga = gate[:, :, 0:ne]
                if r == 0:
                    V.scalar_tensor_tensor(ga, rank, float(topk), p, ALU.is_lt, ALU.mult).then_inc(gate_ready.sem, 1)
                elif r == 1:
                    link(V.scalar_tensor_tensor(one, rank, float(topk), p, ALU.is_lt, ALU.mult))
                    link(V.tensor_reduce(g4[:, 3, :], one, AX.X, ALU.add))
                    link(V.reciprocal(g4[:, 3, :], g4[:, 3, :]))
                    V.tensor_tensor(ga, one, tok(3), ALU.mult).then_inc(gate_ready.sem, 1)
                else:
                    V.tensor_scalar(oh12[:, b, :, 0, :], rank, 0.0, None, ALU.is_equal)
                    V.tensor_scalar(oh12[:, b, :, 1, :], rank, 1.0, None, ALU.is_equal).then_inc(oh12_ready.sem, 1)
                    dve.wait_ge(*cum_done.after(b))
                    dve.wait_ge(*oh12_ready.after(b))
                    link(V.scalar_tensor_tensor(k12[:, :, :, :].rearrange("p t c e -> p (t c e)"),
                                                PSQ[2][:, 0:NT * 16], float(CAP),
                                                oh12[:, b, :, :, :].rearrange("p t c e -> p (t c e)"),
                                                ALU.is_le, ALU.mult))
                    link(V.tensor_tensor(one, k12[:, :, 0, :], k12[:, :, 1, :], ALU.add))
                    V.tensor_tensor(ga, one, p, ALU.mult).then_inc(gate_ready.sem, 1)
                dve.wait_ge(*gT_done.after(r, b))
                link(V.tensor_copy(gst[0:ne, :], PSQ[0][0:ne, :]))
                link(V.tensor_tensor(gr1[0:ne, :], PSQ[0][0:ne, :], gst[0:ne, :], ALU.subtract))
                link(V.tensor_copy(glo[0:ne, :], gr1[0:ne, :]))
                V.tensor_copy(gst[32:32 + ne, :], glo[0:ne, :])
                V.tensor_tensor(gst[64:64 + ne, :], gr1[0:ne, :], glo[0:ne, :], ALU.subtract
                                ).then_inc(gst_ready.sem, 1)

            def expert_out(r, b, e, done, bias):
                dve.wait_ge(*done)
                if e >= 2:
                    dve.wait_ge(*acc_ready.after(r, b, e - 2))
                elif b:
                    dve.wait_ge(*acc_ready.after(r, b - 1, 6 + e))
                if bias is None:
                    ins = V.tensor_tensor(yg[:, e % 2, :], PSQ[4 + e % 2], gbc[:, e, :], ALU.mult)
                else:
                    ins = V.scalar_tensor_tensor(yg[:, e % 2, :], PSQ[4 + e % 2], bias, gbc[:, e, :], ALU.add, ALU.mult)
                ins.then_inc(yg_ready.sem, 1)

            def add_sum(r, s, b):
                dve.wait_ge(*acc_ready.after(r, b, 7))
                V.tensor_copy(g4[0:1, 0, 0:1], g4[0:1, 1, 0:1]).then_inc(out_read.sem, 1)
                V.scalar_tensor_tensor(x[:, b, :], acc, tg[:, s:s + 1], x[:, b, :], ALU.mult, ALU.add
                                       ).then_inc(residual.sem, 1)

            def ffn0(b):
                gates(0, b)
                for j in range(1, 9):
                    dve.wait_ge(*gelu0.after(b, j))
                    dve.wait_ge(*ga_done.after(b, j - 1))
                    if j >= 5:
                        dve.wait_ge(*dn0_done.after(b, j - 4))
                    V.tensor_tensor(hid2[:, j % 4, :], big_gelu(j), PSQ[4 + j % 2], ALU.mult).then_inc(hg_ready.sem, 1)
                dve.wait_ge(*out_done.after(1, b))
                V.tensor_copy(y_tmp[:, :], PSQ[6]).then_inc(out_read.sem, 1)
                dve.wait_ge(*out_read.after(1, b))
                V.scalar_tensor_tensor(x[:, b, :], y_tmp[:, :], tg[:, 1:2], x[:, b, :], ALU.mult, ALU.add
                                       ).then_inc(residual.sem, 1)

            def ffn1(b):
                gates(1, b)
                for n in range(16):
                    dve.wait_ge(*silu1.after(b, n))
                    if n >= 4:
                        dve.wait_ge(*dn1_done.after(b, n - 4))
                    V.tensor_tensor(hid2[:, n % 4, :], hid[:, n % 3, :], PSQ[2 + n % 2], ALU.mult
                                    ).then_inc(hh_ready.sem, 1)
                    if n >= 3 and n % 2:
                        e = n // 2 - 1
                        if e == 0:
                            dve.wait_ge(*gbc_ready.after(0, b, 7))
                        expert_out(0, b, e, dn1_done.after(b, 2 * e + 1), None)
                expert_out(0, b, 7, dn1_done.after(b, 15), None)
                add_sum(0, 3, b)

            def ffn2(b):
                if b == 0:
                    dve.wait_ge(in_f2, 16)
                    link(V.tensor_scalar(b2x[:, 0:1], F2("b2"), 256.0, None, ALU.mult))
                    link(V.tensor_scalar(b2x[:, 1:2], tg[:, 5:6], 1.0 / 256, None, ALU.mult))

                def quantise(j):
                    dve.wait_ge(*up2_done.after(b, j))
                    if j or b:
                        dve.wait_ge(*q2_ready.after(*((b, j - 1) if j else (b - 1, 3))))
                    if j >= 2:
                        dve.wait_ge(*h2_ready.after(b, j - 2))
                    elif b:
                        dve.wait_ge(*h2_ready.after(b - 1, j + 2))
                    n, t = hq(j), hid[:, 0, :]
                    link(V.tensor_scalar(n, PSQ[j], F2("b1")[:, j:j + 1], 256.0, ALU.add, ALU.mult))
                    link(V.tensor_scalar(n, n, MAGIC, -MAGIC, ALU.add, ALU.add))
                    link(V.tensor_scalar(t, n, -1024.0, 1024.0, ALU.max, ALU.min))
                    link(V.tensor_scalar(qt(j), t, 1.0 / 64, -63.0 / 128, ALU.mult, ALU.add))
                    if j >= 2:
                        dve.wait_ge(*gelu2.after(b, j - 2))
                    link(V.tensor_scalar(qlow(j), qt(j), MAGIC, -MAGIC, ALU.add, ALU.add))
                    V.scalar_tensor_tensor(qt(j), t, 1.0 / 64, qlow(j), ALU.mult, ALU.subtract
                                           ).then_inc(q2_ready.sem, 1)

                def interpolate(j):
                    dve.wait_ge(*gelu2.after(b, j))
                    dve.wait_ge(*q2_ready.after(b, j))
                    if j or b:
                        dve.wait_ge(*h2_ready.after(*((b, j - 1) if j else (b - 1, 3))))
                    d = hid[:, 1, :]
                    link(V.tensor_tensor(d, y01(j, 1), y01(j, 0), ALU.subtract))
                    link(V.tensor_tensor(d, d, qt(j), ALU.mult))
                    link(V.tensor_tensor(d, d, y01(j, 0), ALU.add))
                    link(V.tensor_scalar(d, d, 256.0, MAGIC, ALU.mult, ALU.add))
                    link(V.tensor_scalar(hid[:, 2, :], hq(j), -1024.0, 0.0, ALU.add, ALU.max))
                    V.scalar_tensor_tensor(hid2[:, j, :], d, -MAGIC, hid[:, 2, :], ALU.add, ALU.add
                                           ).then_inc(h2_ready.sem, 1)

                quantise(0)
                for j in range(4):
                    if j < 3:
                        quantise(j + 1)
                    interpolate(j)
                dve.wait_ge(*out_done.after(4, b))
                V.tensor_scalar(y_tmp[:, :], PSQ[6], b2x[:, 0:1], MAGIC, ALU.add, ALU.add).then_inc(out_read.sem, 1)
                dve.wait_ge(*out_read.after(5, b))
                link(V.tensor_scalar(y_tmp[:, :], y_tmp[:, :], -MAGIC, b2x[:, 1:2], ALU.add, ALU.mult))
                V.tensor_tensor(x[:, b, :], y_tmp[:, :], x[:, b, :], ALU.add).then_inc(residual.sem, 1)

            def hq(j):
                return gbc[:, 6 + j % 2, :]

            def qt(j):
                return yg[:, j % 2, :]

            def ffn3(b):
                gates(2, b)
                dve.wait_ge(*gbc_ready.after(1, b, 7))
                for e in range(8):
                    expert_out(1, b, e, dn3_done.after(b, 4 * e + 3), F3("b2")[:, e:e + 1])
                add_sum(1, 7, b)

            constants()
            dve.wait_ge(*gates_tanh.after(0))
            layernorm(0, 0)
            layernorm(0, 1)
            l0_front(0)
            l0_front(1)
            l0_gather(0)
            l0_softmax(0)
            l0_gather(1)
            l0_softmax(1)
            pads()
            l0_back(0)
            l0_back(1)
            stages = [None, ffn0, lambda b: attention(0, b), ffn1, lambda b: attention(1, b), ffn2,
                      lambda b: attention(2, b), ffn3]
            for s in range(1, 8):
                layernorm(s, 0)
                layernorm(s, 1)
                if s == 2:
                    masks()
                    for a in range(ATT):
                        for b in range(B):
                            kv_prepare(a, b)
                if s == 6:
                    overwritten_keys()
                stages[s](0)
                stages[s](1)


def kernel(**inputs):
    import numpy as np
    import concourse.bacc as _bacc
    from concourse import mybir as _mybir
    from concourse.bass_utils import run_bass_kernel_spmd as _run

    I = {k: np.asarray(v) for k, v in inputs.items()}
    f4 = np.float32

    def rowsof(a, n=128):
        return a.reshape(-1, n, a.shape[-1]).transpose(1, 0, 2).reshape(n, -1)

    def pad(a, n=128):
        return np.concatenate([a, np.zeros((n - a.shape[0],) + a.shape[1:], a.dtype)]) if a.shape[0] < n else a

    def pack(widths, **parts):
        for k, w in widths.items():
            assert parts[k].shape[1] == w, (k, parts[k].shape, w)
        return np.concatenate([pad(parts[k]) for k in widths], axis=1)

    col = lambda v: v.reshape(-1, 1)
    p = np.arange(128)
    c = np.arange(128)
    slot = (c % 32) // 8
    r = p % 32
    const = dict(
        ident=np.eye(128, dtype=f4), tri=(p[:, None] <= p[None, :]).astype(f4),
        id32=(r[:, None] == np.arange(32)).astype(f4), id16=((p % 16)[:, None] == np.arange(16)).astype(f4),
        headmask=((r // 8)[:, None] == np.arange(4)).astype(f4),
        tie=np.tile((np.arange(16)[None, :] < np.arange(16)[:, None]).reshape(1, 256), (128, 1)).astype(f4),
        patA=np.tile(np.where(slot % 2 == 1, 0.5, 0.0), (128, 1)).astype(f4),
        patW=np.tile(np.where(slot < 2, -1.0, 1.0), (128, 1)).astype(f4),
        patWb=col(np.where((p % 32) // 8 < 2, 1.0, 0.0)).astype(f4),
        refk=col(np.where(r < 20, r % NK - 3, 0)).astype(f4), pos=col(p - 1).astype(f4),
        selS=((((p % 32) // 8) % 2 == 0)[:, None] & ((p // 32)[:, None] == np.arange(4))).astype(f4))

    def grouped(w):
        return np.repeat(w.reshape(G, HG, 1, HD, -1), 4, axis=2).reshape(G * 128, -1)

    wq, wk, wv, wo = (I[f"L0_xattn_{n}"] for n in ("Wq", "Wk", "Wv", "Wo"))
    woff, boff = I["L0_xattn_Woff"], I["L0_xattn_boff"]
    woff_p = np.zeros((G, 32, D), f4)
    woff_p[:, :HG * NK] = woff.reshape(G, HG * NK, D)
    boff_p = np.zeros((G, 32), f4)
    boff_p[:, :HG * NK] = boff.reshape(G, HG * NK)
    kv = np.stack([wk.reshape(H, HD, D), wv.reshape(H, HD, D)], 1).reshape(2 * D, D)
    bkv = np.stack([I["L0_xattn_bk"].reshape(H, HD), I["L0_xattn_bv"].reshape(H, HD)], 1).reshape(1, 2 * D)
    worep = np.zeros((G, HG, 4, HD, D), f4)
    worep[:, :, 1] = wo.T.reshape(G, HG, HD, D)
    worep[:, :, 3] = wo.T.reshape(G, HG, HD, D)
    ctx = np.zeros((D, B, M + 2), f4)
    ctx[:, :, 1:M + 1] = I["ctx_1024"].transpose(2, 0, 1)
    l0 = pack(L0_W, wq=wq.T, wqrep=grouped(wq).T, woff=woff_p.reshape(128, D).T, wkv=kv.T,
              worep=rowsof(worep.reshape(G * 128, D)), ctx=ctx.reshape(D, -1), bq=col(I["L0_xattn_bq"]),
              bqrep=grouped(col(I["L0_xattn_bq"])).reshape(G, 128).T, boff=col(boff_p), bo=col(I["L0_xattn_bo"]))
    valid = np.ones((2, MO), f4)
    valid[0, 0] = 0
    valid[1, MO - 1] = 0
    rows = np.concatenate([bkv, valid.reshape(1, -1)] + [I[f"L{n}_xattn_bv"].reshape(1, -1) for n in (1, 2, 3)]
                          + [I["L3_ffn_gate_b"].reshape(1, -1)], axis=1)

    def three(w):
        return np.repeat(w.reshape(w.shape[0], G, 1, 32), 3, axis=2).reshape(w.shape[0], G * 96)

    att = []
    for n in (1, 2, 3):
        w = {k: I[f"L{n}_xattn_W{k}"] for k in "qkvo"}
        if n != 2:
            w = {k: v.T for k, v in w.items()}
        att.append(pack(ATT_W, wq=three(w["q"]), wk=three(w["k"]), wv=w["v"], wo=w["o"],
                        bq=three(I[f"L{n}_xattn_bq"].reshape(1, -1)).reshape(G, 96).T,
                        bk=three(I[f"L{n}_xattn_bk"].reshape(1, -1)).reshape(G, 96).T, bo=col(I[f"L{n}_xattn_bo"])))
    att = np.concatenate(att, axis=1)

    up = np.concatenate([I["L0_ffn_shared_up"], I["L0_ffn_routed_up"]]).reshape(18 * 64, D)
    down = np.concatenate([I["L0_ffn_shared_down"], I["L0_ffn_routed_down"]]).transpose(0, 2, 1).reshape(18 * 64, D)
    f0 = pack(F0_W, rw=I["L0_ffn_router_w"].T, up=up.T, down=rowsof(down))
    f1 = pack(F1_W, rw=I["L1_ffn_wg"].T, w1=I["L1_ffn_w1"].reshape(-1, D).T, w3=I["L1_ffn_w3"].reshape(-1, D).T,
              w2=rowsof(I["L1_ffn_w2"].transpose(0, 2, 1).reshape(-1, D)))
    f2 = pack(F2_W, w1=I["L2_ffn_w1"], w2=rowsof(I["L2_ffn_w2"]), b1=I["L2_ffn_b1"].reshape(4, 128).T,
              b2=col(I["L2_ffn_b2"]))
    f3 = pack(F3_W, rw=I["L3_ffn_gate_w"].T, b1=I["L3_ffn_b1"].reshape(32, 128).T, b2=I["L3_ffn_b2"].T)
    f3big = pack(F3_BIG, w1=I["L3_ffn_W1"].transpose(1, 0, 2).reshape(D, -1), w2=rowsof(I["L3_ffn_W2"].reshape(-1, D)))

    mbf = np.zeros((B, M, 4), np.bool_)
    mbf[:, :, 0] = I["mask_BxS2_bf0"]
    mbf = mbf.view(np.int32)[:, :, 0]
    tiles = lambda a: a.reshape(NT, 128, M).transpose(1, 0, 2)
    arrays = dict(
        xT=I["x"].reshape(B * T, D).T, g8=np.tile(np.stack([I["g_xattn"], I["g_ffn"]], 1).reshape(1, 8), (128, 1)),
        const=pack(CONST_W, **const), l0=l0, att=att, f0=f0, f1=f1, f2=f2, f3=f3, f3big=f3big, rows=rows,
        am_tok=tiles(I["fside_SxS2_0"]), am_T=I["fside_SxS2_0"].T,
        ik_tok=tiles(I["mask_SxS2_ik0"]), ik_T=I["mask_SxS2_ik0"].T,
        mif=np.tile(I["mask_BxS2_if0"].reshape(1, -1), (128, 1)),
        mbf_tok=np.tile(mbf.reshape(1, -1), (128, 1)), mbf_T=mbf.T)
    arrays = {k: np.ascontiguousarray(v) for k, v in arrays.items()}

    nc = _bacc.Bacc("TRN2", target_bir_lowering=False, num_devices=1)
    args = {k: nc.dram_tensor(k, v.shape, _mybir.dt.from_np(v.dtype), kind="ExternalInput").ap()
            for k, v in arrays.items()}
    out = nc.dram_tensor("outT", (D, B * T), _mybir.dt.from_np(np.dtype(f4)), kind="ExternalOutput").ap()
    bass_flamingo_gated_layers_kernel(nc, outT=out, **args)
    res = _run(nc, [arrays], core_ids=[0])
    return res.results[0]["outT"].T.reshape(B, T, D)
```

```python
import concourse.bass as bass
from concourse import mybir
from contextlib import ExitStack

B, T, D = 2, 512, 128
M = 77
H, HD = 16, 8
G, HG = 4, 4
NT, TT = T // 128, 128
NK = 5
MO = M + 1
ATT = 3
RING = 6
MROW = 48
POOL_HEADS = 4
GATES = ((16, 4), (8, 2), (8, 2))
CAP = 320
EPS = 1e-5
MAGIC = 12582912.0
NEG = -1e30

CONST_W = dict(ident=128, tri=128, id32=32, id16=16, keys=77, headmask=4, tie=256, signW=1,
               patWb=1, refk=1, pos=1, selS=4)
L0_W = dict(wq=128, wqrep=512, woff=128, wkv=256, worep=512, ctx=B * (M + 2), bq=1, bqrep=4, boff=1, bo=1)
ATT_W = dict(wq=128, wk=128, wv=128, wo=128, bq=1, bk=1, bo=1)
F0_W = dict(rw=16, up=1152, down=1152)
F1_W = dict(rw=8, w1=2048, w3=2048, w2=2048)
F2_W = dict(w1=512, w2=512, b1=4, b2=1)
F3_W = dict(rw=8, b1=32, b2=8)
F3_BIG = dict(w1=4096, w2=4096)
ROW_W = dict(bkv=256, valid=2 * MO, bv=ATT * 128, gb=8)


def offsets(widths):
    at, out = 0, {}
    for name, w in widths.items():
        out[name] = (at, w)
        at += w
    return out, at


class Signal:

    def __init__(self, sem, *dims):
        self.sem, self.dims = sem, dims

    def after(self, *key):
        n = 0
        for k, d in zip(key, self.dims):
            assert 0 <= k < d
            n = n * d + k
        return self.sem, n + 1


def bass_flamingo_gated_layers_kernel(nc, xT, g8, const, l0, att, f0, f1, f2, f3, f3big, rows, am_tok, am_T,
                  ik_tok, ik_T, mif, mbf_tok, mbf_T, outT):
    f32, bf16, i32 = mybir.dt.float32, mybir.dt.bfloat16, mybir.dt.int32
    ALU, ACT, AX = mybir.AluOpType, mybir.ActivationFunctionType, mybir.AxisListType
    V, A, P, E = nc.vector, nc.scalar, nc.gpsimd, nc.tensor

    with ExitStack() as ctx:
        def sb(name, shape, dt=f32):
            return ctx.enter_context(nc.sbuf_tensor(name, shape, dt))

        def signal(name, *dims):
            return Signal(ctx.enter_context(nc.semaphore(name)), *dims)

        def packed(tile, widths):
            cols, _ = offsets(widths)
            return lambda name: tile[:, cols[name][0]:cols[name][0] + cols[name][1]]

        x = sb("x", [128, B, T])
        tg = sb("tg", [128, 8])
        g_raw = sb("g_raw", [128, 8])
        const_sb = sb("const_sb", [128, offsets(CONST_W)[1]])
        C = packed(const_sb, CONST_W)
        l0_sb = sb("l0_sb", [128, offsets(L0_W)[1]])
        L0 = packed(l0_sb, L0_W)
        f0_sb = sb("f0_sb", [128, offsets(F0_W)[1]])
        F0 = packed(f0_sb, F0_W)
        f0_hi = sb("f0_hi", [128, 2 * 1152], bf16)
        f3_sb = sb("f3_sb", [128, offsets(F3_W)[1]])
        F3 = packed(f3_sb, F3_W)
        rows_sb = sb("rows_sb", [1, offsets(ROW_W)[1]])
        R = packed(rows_sb, ROW_W)
        ones_row = sb("ones_row", [1, 128])
        eps_col = sb("eps_col", [128, 1])
        mean_w = sb("mean_w", [128, 128])
        ones_bf = sb("ones_bf", [128, 128], bf16)
        ident_bf = sb("ident_bf", [128, 128], bf16)
        neg_ident = sb("neg_ident", [128, 128], bf16)
        tri_bf = sb("tri_bf", [128, 128], bf16)

        xc = sb("xc", [128, B, T])
        sq = sb("sq", [128, T])
        rstd = sb("rstd", [128, T])
        xn = sb("xn", [128, B, T])
        xn_lo = sb("xn_lo", [128, B, T], bf16)
        y_tmp = sb("y_tmp", [128, T])

        arena = sb("arena", [128, B * G * NK * T])
        GW = arena[:, :].rearrange("p (b u t) -> p b u t", b=B, u=G * NK)
        n_f3, n_f1, n_att = offsets(F3_BIG)[1], offsets(F1_W)[1], ATT * offsets(ATT_W)[1]
        f3w = arena[:, 0:n_f3]
        F3B = packed(f3w, F3_BIG)
        f1_sb = arena[:, n_f3:n_f3 + n_f1]
        F1 = packed(f1_sb, F1_W)
        att_sb = arena[:, n_f3 + n_f1:n_f3 + n_f1 + n_att].rearrange("p (a n) -> p a n", a=ATT)
        AW = [packed(att_sb[:, a, :], ATT_W) for a in range(ATT)]

        at, base = [n_f3 + n_f1 + n_att], [arena]

        def piece(n, dt=f32):
            w = n if dt == f32 else (n + 1) // 2
            assert at[0] + w <= base[0].shape[1], at[0]
            v = base[0][:, at[0]:at[0] + w]
            at[0] += w
            return v if dt == f32 else v.bitcast(dt)[:, 0:n]

        f1_hi = piece(3 * 2048, bf16)
        amp = piece(B * NT * M).rearrange("p (b t m) -> p b t m", b=B, t=NT)
        amp_lo = piece(B * NT * M, bf16).rearrange("p (b t m) -> p b t m", b=B, t=NT)
        mb8 = piece(B * M).bitcast(i32)
        pad_row = piece(B * M)
        sel_kh = piece(512, bf16)
        f3_hi = arena[:, n_f3:n_f3 + n_f3 // 2].bitcast(bf16)

        work = sb("work", [128, 10752])
        early = sb("early", [128, 7500])
        at[0], base[0] = 0, work
        qp = piece(T)
        qrep = piece(B * G * T).rearrange("p (b g t) -> p b g t", b=B, g=G)
        ixt = piece(T)
        ix1 = piece(T)
        ix2 = piece(T)
        i0bf = piece(B * T, bf16).rearrange("p (b t) -> p b t", b=B)
        w1hi = piece(B * T, bf16).rearrange("p (b t) -> p b t", b=B)
        w1lo = piece(B * T, bf16).rearrange("p (b t) -> p b t", b=B)
        at_wf = piece(2 * T).rearrange("p (r t) -> p r t", r=2)
        tq = piece(3 * T).rearrange("p (r t) -> p r t", r=3)
        ahi = piece(T, bf16)
        alo = piece(T, bf16)
        end_l0 = at[0]
        at[0] = 0
        qf = piece(T)
        q_lo = piece(T, bf16)
        qs = piece(G * T, bf16).rearrange("p (g t) -> p g t", g=G)
        wT = piece(T, bf16)
        oT = piece(T)
        den_r = piece(T)
        uT = piece(2 * T).rearrange("p (r t) -> p r t", r=2)
        pT = piece(RING * T)[0:M].rearrange("p (r t) -> p r t", r=RING)
        p_lo = piece(RING * T, bf16)[0:M].rearrange("p (r t) -> p r t", r=RING)
        nst = piece(NT * 3 * H, bf16).rearrange("p (t a h) -> p t a h", t=NT, a=3)
        at[0] = 10752 - 3 * T
        shift_hi = piece(T, bf16)
        shift_lo = piece(T, bf16)
        am_st = piece(T)
        am_sb = piece(NT * M).rearrange("p (t m) -> p t m", t=NT)
        at[0] = 0
        gbc = piece(8 * T).rearrange("p (e t) -> p e t", e=8)
        hid = piece(3 * T).rearrange("p (r t) -> p r t", r=3)
        hid2 = piece(4 * T).rearrange("p (r t) -> p r t", r=4)
        h_lo = piece(4 * T, bf16).rearrange("p (r t) -> p r t", r=4)
        gr1 = piece(T)[0:16]
        at[0] = 10752 - 3 * T
        acc = piece(T)
        yg = piece(2 * T).rearrange("p (r t) -> p r t", r=2)
        big = gbc[:, 4:6, :].rearrange("p e t -> p (e t)")
        big2 = gbc[:, 6:8, :].rearrange("p e t -> p (e t)")
        base[0], at[0] = early, 0
        loc = piece(T)
        sel_rows = piece(G * NK * 128, bf16).rearrange("p (g k c) -> p g k c", g=G, k=NK)
        tab = [[f0_sb[0:MO, 0:1024].bitcast(bf16), f0_sb[0:MO, 1024:2048].bitcast(bf16)],
               [f0_hi[0:MO, 0:2048], piece(2048, bf16)[0:MO]]]
        ib = piece(4 * T, bf16)[0:MO].rearrange("p (p2 t) -> p p2 t", p2=2)
        oh = piece(8 * T, bf16)[0:MO].rearrange("p (r p2 t) -> p r p2 t", r=2, p2=2)
        s80 = piece(NT * H * NK)
        e80 = piece(NT * H * NK)
        ap_ = piece(NT * 128).rearrange("p (t c) -> p t c", t=NT)
        mcnt = piece(2 * M)
        mif_sb = piece(2 * M).bitcast(i32)
        at[0] = 0
        kt = piece(B * H * M, bf16).rearrange("p (b h m) -> p b h m", b=B, h=H)
        v_hi = piece(B * 17 * 128, bf16)[0:M].rearrange("p (b c) -> p b c", b=B)
        v_lo = piece(B * 17 * 128, bf16)[0:M].rearrange("p (b c) -> p b c", b=B)
        f2_sb = piece(offsets(F2_W)[1])
        F2 = packed(f2_sb, F2_W)
        kf = piece(M)
        kl = piece(M, bf16)
        sel_shift = piece(H * M, bf16).rearrange("p (h m) -> p h m", h=H)
        base[0], at[0] = f0_sb, 0
        vf = sb("vf", [M, B, D])
        vf_lo = sb("vf_lo", [M, B, D], bf16)
        ik_sb = piece(NT * M).bitcast(i32).rearrange("p (t m) -> p t m", t=NT)
        ikT_sb = piece(T).bitcast(i32)
        ikT_st = piece(T)
        z = piece(NT * M, bf16).rearrange("p (t m) -> p t m", t=NT)
        zT = piece(T, bf16)[0:M]
        wst = piece(NT * 2 * H, bf16).rearrange("p (t a h) -> p t a h", t=NT, a=2)
        w0z = piece(NT * H).rearrange("p (t h) -> p t h", t=NT)
        zany = piece(3 * NT).rearrange("p (i t) -> p i t", i=3)
        base[0], at[0] = l0_sb, 0
        sel0 = piece(16 * 64, bf16)[0:96].rearrange("p (e c) -> p e c", e=16)
        sel1 = piece(8 * 128, bf16)[0:96].rearrange("p (e c) -> p e c", e=8)
        sel_qh = piece(512, bf16)
        sel_ql = piece(512, bf16)
        sel_kl = sb("sel_kl", [128, 512], bf16)[:, :]
        gst = sb("gst", [96, T], bf16)

        refl = sb("refl", [128, 8])
        bq_s = sb("bq_s", [128, 4])
        Lb = sb("Lb", [128, 2, 8])
        s64 = sb("s64", [128, 3, NT * H])

        hm_bf = sb("hm_bf", [128, HG], bf16)
        bqs = sb("bqs", [128, ATT])
        selH = sb("selH", [32, H, 8], bf16)
        nmx = sb("nmx", [128, NT, H])
        mb8T = sb("mb8T", [M, B], i32)
        padT = sb("padT", [M, B])

        glo = sb("glo", [16, T], bf16)
        lg = sb("lg", [128, 5, NT, 16])
        g4 = sb("g4", [128, 4, NT])
        oh12 = sb("oh12", [128, B, NT, 2, 8], bf16)
        k12 = sb("k12", [128, NT, 2, 8])
        gate = sb("gate", [128, NT, 16])
        b2x = sb("b2x", [128, 2])
        b1x = sb("b1x", [128, 4])

        ps = ctx.enter_context(nc.psum_tensor("ps", [128, 8, 512], f32))

        def dma_sem(name):
            return ctx.enter_context(nc.semaphore(name))

        in_first, in_l0, in_rows, in_att, in_f0, in_f1, in_f2, in_f3, in_masks, in_big, in_ik = (dma_sem(n) for n in (
            "x_and_consts_in", "layer0_weights_in", "bias_rows_in", "attention_weights_in", "ffn0_weights_in",
            "ffn1_weights_in", "ffn2_weights_in", "ffn3_biases_in", "masks_in", "ffn3_weights_in", "overwrite_mask_in"))
        out_sem = dma_sem("out_stored")
        consts_ready = signal("consts_ready", 1)
        dve_consts = signal("dve_consts", 1)
        gates_tanh = signal("gates_tanh", 1)
        dve_step = ctx.enter_context(nc.semaphore("dve_step"))
        act_step = ctx.enter_context(nc.semaphore("act_step"))
        pool_step = ctx.enter_context(nc.semaphore("pool_step"))
        steps = {"dve": 0, "act": 0, "pool": 0}

        ln_mean = signal("ln_mean", 8, B)
        ln_centered = signal("ln_centered", 8, B)
        ln_squared = signal("ln_squared", 8, B)
        ln_var = signal("ln_var", 8, B)
        ln_log = signal("ln_log", 8, B)
        ln_rstd = signal("ln_rstd", 8, B)
        xn_ready = signal("xn_ready", 8, B)
        weights0_lo = signal("weights0_lo", 1)
        weights0_hi = signal("weights0_hi", 1)
        weights1_hi = signal("weights1_hi", 3)
        weights3_hi = signal("weights3_hi", 4)
        weights1_lo = signal("weights1_lo", 3)
        weights3_lo = signal("weights3_lo", 4)
        out_done = signal("out_done", 6, B)
        out_read = signal("out_read", 8, B)
        residual = signal("residual", 8, B)

        rows_ready = signal("rows_ready", 1)
        tab_zeroed = signal("tab_zeroed", 1)
        tab_done = signal("tab_done", B)
        tab_ready = signal("tab_ready", B)
        qp_done = signal("qp_done", B)
        qp_ready = signal("qp_ready", B)
        off_done = signal("off_done", B)
        off_read = signal("off_read", B)
        qrep_done = signal("qrep_done", B, G)
        qrep_ready = signal("qrep_ready", B, G)
        ix_ready = signal("ix_ready", B)
        U = G * NK
        bc_done = signal("bc_done", B, U, 2)
        ib_ready = signal("ib_ready", B, G, NK - 1, 2)
        t2_sum = signal("t2_sum", B, G)
        t2_pair = signal("t2_pair", B, G)
        oh_ready = signal("oh_ready", B, U, 2)
        gather_done = signal("gather_done", B, U)
        wf_done = signal("wf_done", B, U)
        wf_ready = signal("wf_ready", B, U)
        gw_ready = signal("gw_ready", B, U)
        tq_ready = signal("tq_ready", B, U)
        score_done = signal("score_done", B, U)
        s_shifted = signal("s_shifted", B)
        s_exp = signal("s_exp", B)
        a_ready = signal("a_ready", B)
        aT_done = signal("aT_done", B)
        aT_ready = signal("aT_ready", B)
        ab_done = signal("ab_done", B, U)
        t2_ready = signal("t2_ready", B, U)
        t2_used = signal("t2_used", B, G)

        kf_ready = signal("kf_ready", ATT, B)
        kb_ready = signal("kb_ready", ATT, B)
        v_done = signal("v_done", ATT, B)
        v_ready = signal("v_ready", ATT, B)
        kl_ready = signal("kl_ready", ATT, B)
        ks_done = signal("ks_done", ATT, B)
        qs_done = signal("qs_done", ATT, B, G)
        qs_act = signal("qs_act", ATT, B, 2)
        qs_dve = signal("qs_dve", ATT, B, 2)
        q_done = signal("q_done", ATT, B)
        qf_ready = signal("qf_ready", ATT, B)
        qst_ready = signal("qst_ready", ATT, B)
        st_done = signal("st_done", ATT, B, NT, 2)
        st_read = signal("st_read", ATT, B, NT, 2)
        nst_ready = signal("nst_ready", ATT, B)
        nT_done = signal("nT_done", ATT, B)
        nT_ready = signal("nT_ready", ATT, B)
        sT_done = signal("sT_done", ATT, B, H)
        pT_ready = signal("pT_ready", ATT, B, H)
        p_lo_v = signal("p_lo_v", ATT, B, H - POOL_HEADS)
        p_lo_p = signal("p_lo_p", ATT, B, POOL_HEADS)
        pv_done = signal("pv_done", ATT, B, H)
        den_ready = signal("den_ready", ATT, B)
        wb_done = signal("wb_done", B)
        uw_ready = signal("uw_ready", B)
        wT_done = signal("wT_done", B)
        wT_ready = signal("wT_ready", B)
        wst_ready = signal("wst_ready", B)
        tot_ready = signal("tot_ready", B)
        o_norm = signal("o_norm", ATT, B)
        oT_done = signal("oT_done", ATT, B)
        oT_ready = signal("oT_ready", ATT, B)
        amp_ready = signal("amp_ready", 1)
        w0_shift = signal("w0_shift", B)
        w0_ready = signal("w0_ready", B)
        u_done = signal("u_done", B)
        u_read = signal("u_read", B)
        ik_filled = signal("ik_filled", 1)
        z_ready = signal("z_ready", 1)
        sel_ready = signal("sel_ready", 1)
        bqs_ready = signal("bqs_ready", 1)
        pad_ready = signal("pad_ready", 1)
        zeroed = signal("zeroed", 1)

        lg_done = signal("lg_done", 3, B)
        lg_shift = signal("lg_shift", 3, B)
        lg_exp = signal("lg_exp", 3, B)
        oh12_ready = signal("oh12_ready", B)
        cum_done = signal("cum_done", B)
        gate_ready = signal("gate_ready", 3, B)
        gT_done = signal("gT_done", 3, B)
        gst_ready = signal("gst_ready", 3, B)
        gb_done = signal("gb_done", 2, B, 8)
        gbc_ready = signal("gbc_ready", 2, B, 8)
        up0_done = signal("up0_done", B, 9)
        gelu0 = signal("gelu0", B, 9)
        ga_done = signal("ga_done", B, 8)
        hg_ready = signal("hg_ready", B, 8)
        dn0_done = signal("dn0_done", B, 8)
        lo0_v = signal("lo0_v", B, 5)
        lo0_p = signal("lo0_p", B, 4)
        lo1_v = signal("lo1_v", B, 8)
        lo1_p = signal("lo1_p", B, 8)
        lo3 = signal("lo3", B, 32)
        up1_done = signal("up1_done", B, 16)
        silu1 = signal("silu1", B, 16)
        hh_ready = signal("hh_ready", B, 16)
        dn1_done = signal("dn1_done", B, 16)
        yg_ready = signal("yg_ready", 2, B, 8)
        acc_ready = signal("acc_ready", 2, B, 8)
        up2_done = signal("up2_done", B, 4)
        h256 = signal("h256", B, 4)
        b2_ready = signal("b2_ready", 1)
        dy_ready = signal("dy_ready", B, 4)
        q2_ready = signal("q2_ready", B, 4)
        gelu2 = signal("gelu2", B, 4)
        h2_ready = signal("h2_ready", B, 4)
        up3_done = signal("up3_done", B, 32)
        relu3 = signal("relu3", B, 32)
        dn3_done = signal("dn3_done", B, 32)

        block = ctx.enter_context(nc.Block())
        PSQ = [ps[:, k, :] for k in range(8)]

        def high(ap):
            return ap.bitcast(bf16)[:, 1::2]

        def next_ln(s, b):
            return (s, 1) if b == 0 else (s + 1, 0) if s < 7 else None

        def on_pool(n):
            return n % (H // POOL_HEADS) == 1

        def p_split(a, b, n):
            k = sum(on_pool(i) for i in range(n))
            return p_lo_p.after(a, b, k) if on_pool(n) else p_lo_v.after(a, b, n - k)

        def lo_done(v, p, b, n):
            return v.after(b, n // 2) if n % 2 == 0 else p.after(b, n // 2)

        @block.sync
        def _(sp):
            sp.dma_start(x[:, :, :], xT.rearrange("p (b t) -> p b t", b=B)).then_inc(in_first, 16)
            sp.dma_start(const_sb[:, :], const).then_inc(in_first, 16)
            sp.dma_start(mif_sb[:, :], mif).then_inc(in_first, 16)
            sp.dma_start(g_raw[:, :], g8).then_inc(in_first, 16)
            sp.dma_start(l0_sb[:, :], l0).then_inc(in_l0, 16)
            sp.dma_start(rows_sb[:, :], rows).then_inc(in_rows, 16)
            sp.dma_start(f3_sb[:, :], f3).then_inc(in_f3, 16)
            sp.wait_ge(*gather_done.after(B - 1, U - 1))
            sp.dma_start(f0_sb[:, :], f0).then_inc(in_f0, 16)
            sp.wait_ge(*out_read.after(0, B - 1))
            sp.dma_start(att_sb, att.rearrange("p (a n) -> p a n", a=ATT)).then_inc(in_att, 16)
            for dst, src in ((am_sb[:, :, :], am_tok), (mb8[:, :], mbf_tok), (mb8T[:, :], mbf_T)):
                sp.dma_start(dst, src).then_inc(in_masks, 16)
            sp.dma_start(f1_sb[:, :], f1).then_inc(in_f1, 16)
            sp.wait_ge(*zeroed.after(0))
            sp.dma_start(am_st[MROW:MROW + M, :], am_T).then_inc(in_masks, 16)
            sp.dma_start(f2_sb[:, :], f2).then_inc(in_f2, 16)
            sp.dma_start(f3w, f3big).then_inc(in_big, 16)
            sp.wait_ge(*out_read.after(1, B - 1))
            sp.dma_start(ik_sb, ik_tok).then_inc(in_ik, 16)
            sp.dma_start(ikT_sb[0:M], ik_T).then_inc(in_ik, 16)
            sp.wait_ge(*ik_filled.after(0))
            sp.dma_start(ikT_st[MROW:MROW + M, :].bitcast(i32), ik_T).then_inc(in_ik, 16)
            for b in range(B):
                sp.wait_ge(*residual.after(7, b))
                sp.dma_start(outT[:, b * T:(b + 1) * T], x[:, b, :]).then_inc(out_sem, 16)
            sp.wait_ge(out_sem, 16 * B)

        @block.tensor
        def _(pe):
            def product(out, w_rest, w, r, r_rest, start=True, stop=True):
                E.matmul(out, w, high(r), start=start, stop=False)
                E.matmul(out, w, r_rest, start=False, stop=False)
                return E.matmul(out, high(w_rest), high(r), start=False, stop=stop)

            def norm_mean(s, b):
                if s == 0:
                    if b == 0:
                        pe.wait_ge(in_first, 64)
                        pe.wait_ge(*consts_ready.after(0))
                else:
                    pe.wait_ge(*residual.after(s - 1, b))
                if (s, b) != (0, 0):
                    pe.wait_ge(*ln_log.after(s if b else s - 1, 1 - b))
                E.matmul(PSQ[7], mean_w[:, :], x[:, b, :], start=True, stop=True).then_inc(ln_mean.sem, 1)

            def norm_var(s, b):
                pe.wait_ge(*ln_squared.after(s, b))
                E.matmul(PSQ[7], mean_w[:, :], sq[:, :], start=True, stop=True).then_inc(ln_var.sem, 1)

            def bank6_free(s, b):
                if (s, b) != (0, 0):
                    pe.wait_ge(*out_read.after(s if b else s - 1, 1 - b))

            def l0_front(b):
                if b:
                    pe.wait_ge(*qrep_ready.after(0, G - 1))
                    pe.wait_ge(*tab_ready.after(0))
                    pe.wait_ge(*off_read.after(0))
                else:
                    pe.wait_ge(in_l0, 16)
                    pe.wait_ge(in_rows, 16)
                for slot in range(2):
                    out = PSQ[0][0:MO, slot * 256:(slot + 1) * 256]
                    c0 = b * (M + 2) + slot
                    E.matmul(out, L0("ctx")[:, c0:c0 + MO], L0("wkv"), start=True, stop=False)
                    last = E.matmul(out, R("valid")[:, slot * MO:(slot + 1) * MO], R("bkv"), start=False, stop=True)
                last.then_inc(tab_done.sem, 1)
                pe.wait_ge(*xn_ready.after(0, b))
                E.matmul(PSQ[1], L0("wq"), xn[:, b, :], start=True, stop=True).then_inc(qp_done.sem, 1)
                pe.wait_ge(*qp_ready.after(b))
                E.matmul(PSQ[2], L0("woff"), qp, start=True, stop=True).then_inc(off_done.sem, 1)
                for g in range(G):
                    if g >= 2:
                        pe.wait_ge(*qrep_ready.after(b, g - 2))
                    E.matmul(PSQ[3 + g % 2], L0("wqrep")[:, g * 128:(g + 1) * 128], xn[:, b, :],
                             start=True, stop=True).then_inc(qrep_done.sem, 1)

            def head_rows(g, k):
                return sel_rows[:, g, k, :]

            def l0_gather(b):
                def spread(u, g, k):
                    for p in range(2):
                        if k:
                            pe.wait_ge(*ib_ready.after(b, g, k - 1, p))
                        elif u:
                            pe.wait_ge(*oh_ready.after(b, u - 1, p))
                        elif b:
                            pe.wait_ge(*oh_ready.after(b - 1, U - 1, p))
                        for i in range(2):
                            c = 32 * g + NK * (2 * p + i) + k
                            last = E.matmul(PSQ[2 * p + i][0:MO, :], ident_bf[:, c:c + 1].broadcast_to([128, MO]),
                                            i0bf[:, b, :], start=True, stop=True)
                        last.then_inc(bc_done.sem, 1)
                    if u:
                        pe.wait_ge(*wf_ready.after(b, u - 1))
                    elif b:
                        pe.wait_ge(*wf_ready.after(b - 1, U - 1))
                    E.matmul(PSQ[5], head_rows(g, k), w1hi[:, b, :], start=True, stop=False)
                    E.matmul(PSQ[5], head_rows(g, k), w1lo[:, b, :], start=False, stop=True).then_inc(wf_done.sem, 1)

                def gather(u, g, k):
                    n = b * U + u
                    if n >= 2:
                        pe.wait_ge(*gw_ready.after((n - 2) // U, (n - 2) % U))
                    pe.wait_ge(*oh_ready.after(b, u, 1))
                    out = PSQ[(4, 7)[u % 2]]
                    for part in range(2):
                        for h in range(HG):
                            c = (HG * g + h) * 128
                            last = E.matmul(out, tab[b][part][:, c:c + 128],
                                            oh[:, u % 2, h // 2, (h % 2) * T:(h % 2 + 1) * T],
                                            start=(part, h) == (0, 0), stop=(part, h) == (1, HG - 1))
                    last.then_inc(gather_done.sem, 1)

                def score(u, g, k):
                    pe.wait_ge(*tq_ready.after(b, u))
                    if u == 0 and b:
                        pe.wait_ge(*s_shifted.after(b - 1))
                    sc = PSQ[6][:, 0:NT * H * NK].rearrange("p (t h k) -> p t h k", t=NT, h=H)
                    for t in range(NT):
                        last = E.matmul(sc[:, t, HG * g:HG * g + HG, k], tq[:, u % 3, t * 128:(t + 1) * 128],
                                        C("selS"), start=True, stop=True)
                    last.then_inc(score_done.sem, 1)

                units = [(g * NK + k, g, k) for g in range(G) for k in range(NK)]
                pe.wait_ge(*ix_ready.after(B - 1))
                pe.wait_ge(*rows_ready.after(0))
                pe.wait_ge(*tab_ready.after(B - 1))
                pe.wait_ge(*qrep_ready.after(B - 1, G - 1))
                spread(*units[0])
                for n in range(U):
                    if n + 1 < U:
                        spread(*units[n + 1])
                    gather(*units[n])
                    if n:
                        score(*units[n - 1])
                score(*units[U - 1])

            def l0_back(b):
                pe.wait_ge(*a_ready.after(b))
                if b == 0:
                    pe.wait_ge(*gw_ready.after(B - 1, U - 1))
                    pe.wait_ge(*s_shifted.after(B - 1))
                else:
                    pe.wait_ge(*out_read.after(0, 0))
                for t in range(NT):
                    last = E.transpose(PSQ[0][:, t * 128:(t + 1) * 128], ap_[:, t, :], C("ident"))
                last.then_inc(aT_done.sem, 1)
                pe.wait_ge(*aT_ready.after(b))

                def project(g):
                    pe.wait_ge(*t2_sum.after(b, g))
                    last = E.matmul(PSQ[6], L0("worep")[:, g * 128:(g + 1) * 128], GW[:, b, g * NK, :],
                                    start=g == 0, stop=g == G - 1)
                    last.then_inc(*((out_done.sem, 1) if g == G - 1 else (t2_used.sem, 1)))

                for u in range(U):
                    g, k = u // NK, u % NK
                    if u >= 3:
                        pe.wait_ge(*t2_ready.after(b, u - 3))
                    for part, a_part in enumerate((ahi, alo)):
                        last = E.matmul(PSQ[1 + u % 3], head_rows(g, k), a_part, start=part == 0, stop=part == 1)
                    last.then_inc(ab_done.sem, 1)
                    if k == 3 and g:
                        project(g - 1)
                    if b == 1 and u == 6:
                        norm_mean(1, 0)
                    if b == 1 and u == 12:
                        norm_var(1, 0)
                project(G - 1)

            def kv_project(a, b):
                if (a, b) == (0, 0):
                    pe.wait_ge(in_att, 16)
                else:
                    pe.wait_ge(*kb_ready.after(*((a, b - 1) if b else (a - 1, B - 1))))
                c0 = b * (M + 2) + 1
                E.matmul(PSQ[5][:, 0:M], AW[a]("wk"), L0("ctx")[:, c0:c0 + M], start=True,
                         stop=True)
                E.matmul(PSQ[5][0:M, 128:256], L0("ctx")[:, c0:c0 + M], AW[a]("wv"), start=True, stop=False)
                E.matmul(PSQ[5][0:M, 128:256], ones_row[:, 0:M], R("bv")[:, a * 128:(a + 1) * 128],
                         start=False, stop=True).then_inc(v_done.sem, 1)

            def kv_spread(a, b):
                pe.wait_ge(*kl_ready.after(a, b))
                pe.wait_ge(*v_ready.after(a, b))
                for g in range(G):
                    out = PSQ[5][:, g * M:(g + 1) * M]
                    E.matmul(out, sel_kh[:, g * 128:(g + 1) * 128], high(kf), start=True, stop=False)
                    last = E.matmul(out, sel_kl[:, g * 128:(g + 1) * 128], kl, start=False, stop=True)
                last.then_inc(ks_done.sem, 1)

            def attention(a, b):
                s = 2 * a + 2
                pe.wait_ge(*xn_ready.after(s, b))
                if a == 1 and b == 0:
                    pe.wait_ge(*yg_ready.after(0, B - 1, 7))
                E.matmul(PSQ[0], AW[a]("wq"), xn[:, b, :], start=True, stop=True).then_inc(q_done.sem, 1)
                pe.wait_ge(*kb_ready.after(a, b))
                if (a, b) == (0, 0):
                    pe.wait_ge(*zeroed.after(0))
                    pe.wait_ge(*amp_ready.after(0))
                if a == 2:
                    pe.wait_ge(*z_ready.after(0))
                    E.matmul(PSQ[4], high(vf[:, b, :]), zT, start=True, stop=False)
                    E.matmul(PSQ[4], vf_lo[:, b, :], zT, start=False, stop=True)
                    E.matmul(PSQ[5], ones_bf[0:M, :], zT, start=True, stop=True).then_inc(u_done.sem, 1)
                pe.wait_ge(*qst_ready.after(a, b))
                for g in range(G):
                    E.matmul(PSQ[g], sel_qh[:, g * 128:(g + 1) * 128], high(qf), start=True, stop=False)
                    E.matmul(PSQ[g], sel_ql[:, g * 128:(g + 1) * 128], q_lo, start=False, stop=True
                             ).then_inc(qs_done.sem, 1)
                for t in range(NT):
                    for half in range(2):
                        if t:
                            pe.wait_ge(*st_read.after(a, b, t - 1, half))
                        else:
                            pe.wait_ge(*(qs_dve if half else qs_act).after(a, b, 1))
                        for g in (2 * half, 2 * half + 1):
                            out = PSQ[g][:, 0:HG * M]
                            last = E.matmul(out, qs[:, g, t * 128:(t + 1) * 128],
                                            kt[:, b, HG * g:HG * g + HG, :].rearrange("p h m -> p (h m)"), start=True,
                                            stop=a == 1)
                            out = out.rearrange("p (h m) -> p h m", h=HG)
                            more = []
                            if a == 0:
                                more = [(ident_bf, high(amp[:, b, t, :])), (ident_bf, amp_lo[:, b, t, :])]
                            if a == 2:
                                more = [(neg_ident, z[:, t, :])]
                            for i, (w, part) in enumerate(more):
                                last = E.matmul(out, w[:, :], part.unsqueeze(1).broadcast_to([128, HG, M]),
                                                start=False, stop=i == len(more) - 1)
                        last.then_inc(st_done.sem, 1)
                pe.wait_ge(*nst_ready.after(a, b))
                for t in range(NT):
                    last = E.matmul(PSQ[0][0:MROW, t * 128:(t + 1) * 128],
                                    nst[:, t, :, :].rearrange("p a h -> p (a h)"), ident_bf[:, :],
                                    start=True, stop=True)
                last.then_inc(nT_done.sem, 1)
                if a == 2:
                    pe.wait_ge(*wst_ready.after(b))
                    for t in range(NT):
                        last = E.matmul(PSQ[1][0:32, t * 128:(t + 1) * 128],
                                        wst[:, t, :, :].rearrange("p a h -> p (a h)"), ident_bf[:, :],
                                        start=True, stop=True)
                    last.then_inc(wT_done.sem, 1)
                    pe.wait_ge(*wT_ready.after(b))
                    E.matmul(PSQ[2], selH[:, :, :].rearrange("p h c -> p (h c)"), wT[0:32, :], start=True,
                             stop=True).then_inc(wb_done.sem, 1)
                    pe.wait_ge(*uw_ready.after(b))
                pe.wait_ge(*nT_ready.after(a, b))

                def scores_T(n):
                    if n >= 4:
                        pe.wait_ge(*pT_ready.after(a, b, n - 4))
                    out, k = PSQ[n % 4][0:M, :], MROW if a == 1 else 128
                    E.matmul(out, kt[:, b, n, :], qs[:, n // HG, :], start=True, stop=False)
                    last = E.matmul(out, sel_shift[0:k, n, :], shift_hi[0:k, :], start=False, stop=a != 0)
                    if a == 0:
                        last = E.matmul(out, sel_shift[:, n, :], shift_lo, start=False, stop=True)
                    last.then_inc(sT_done.sem, 1)

                def values(n):
                    pe.wait_ge(*p_split(a, b, n))
                    w = slice(n * 128, (n + 1) * 128)
                    out, p, first, last = PSQ[4 + n // 8], high(pT[:, n % RING, :]), n % 8 == 0, n % 8 == 7
                    E.matmul(out, v_hi[:, b, w], p, start=first, stop=False)
                    E.matmul(out, v_hi[:, b, w], p_lo[:, n % RING, :], start=False, stop=False)
                    E.matmul(out, v_lo[:, b, w], p, start=False, stop=last).then_inc(pv_done.sem, 1)

                nxt = next_ln(s, b)
                for n in range(H):
                    scores_T(n)
                    if n >= 3:
                        values(n - 3)
                    if n == 5:
                        norm_mean(*nxt)
                    if n == 13:
                        norm_var(*nxt)
                for n in range(H - 3, H):
                    values(n)
                pe.wait_ge(*o_norm.after(a, b))
                bank6_free(s, b)
                E.matmul(PSQ[6], AW[a]("wo"), oT, start=True, stop=True).then_inc(out_done.sem, 1)

            def router(r, s, b, bank, rw, bias):
                ne = GATES[r][0]
                bank6_free(s, b)
                pe.wait_ge(*xn_ready.after(s, b))
                for t in range(NT):
                    out = PSQ[bank][:, t * ne:(t + 1) * ne]
                    last = E.matmul(out, xn[:, b, t * 128:(t + 1) * 128], rw, start=True, stop=bias is None)
                    if bias is not None:
                        last = E.matmul(out, ones_row[:, :], bias, start=False, stop=True)
                last.then_inc(lg_done.sem, 1)

            def slots_taken(b, bank):
                pe.wait_ge(*oh12_ready.after(b))
                for t in range(NT):
                    out = PSQ[bank][:, t * 16:(t + 1) * 16]
                    before = [(bb, tt) for bb in range(B) for tt in range(NT) if (bb, tt) < (b, t)]
                    last = E.matmul(out, tri_bf[:, :], oh12[:, b, t, :, :].rearrange("p c e -> p (c e)"),
                                    start=True, stop=not before)
                    for n, (bb, tt) in enumerate(before):
                        last = E.matmul(out, ones_bf[:, :], oh12[:, bb, tt, :, :].rearrange("p c e -> p (c e)"),
                                        start=False, stop=n == len(before) - 1)
                last.then_inc(cum_done.sem, 1)

            def transpose_gates(r, b, bank):
                ne = GATES[r][0]
                pe.wait_ge(*gate_ready.after(r, b))
                for t in range(NT):
                    last = E.transpose(PSQ[bank][0:ne, t * 128:(t + 1) * 128], gate[:, t, 0:ne], C("ident"))
                last.then_inc(gT_done.sem, 1)

            def spread_gate(r, b, e):
                if e:
                    pe.wait_ge(*gbc_ready.after(r - 1, b, e - 1))
                else:
                    pe.wait_ge(*gst_ready.after(r, b))
                E.matmul(PSQ[6], sel1[:, e, :], gst[:, :], start=True, stop=True).then_inc(gb_done.sem, 1)

            def ffn0(b):
                if b == 0:
                    pe.wait_ge(in_f0, 16)
                    pe.wait_ge(*weights0_lo.after(0))
                router(0, 1, b, 4, F0("rw"), None)

                def up(j):
                    if j >= 2:
                        pe.wait_ge(*gelu0.after(b, j - 2))
                    product(PSQ[j % 2], F0("up")[:, j * 128:(j + 1) * 128], f0_hi[:, j * 128:(j + 1) * 128],
                            xn[:, b, :], xn_lo[:, b, :]).then_inc(up0_done.sem, 1)

                def gate_rows(j):
                    if j == 1:
                        pe.wait_ge(*gst_ready.after(0, b))
                    if j >= 3:
                        pe.wait_ge(*hg_ready.after(b, j - 3))
                    E.matmul(PSQ[2 + j % 2], sel0[:, 2 * j - 2:2 * j, :].rearrange("p a c -> p (a c)"), gst[:, :],
                             start=True, stop=True).then_inc(ga_done.sem, 1)

                def down(j):
                    pe.wait_ge(*lo_done(lo0_v, lo0_p, b, j))
                    src = hid[:, 0, :] if j == 0 else hid2[:, j % 4, :]
                    c = slice(1152 + j * 128, 1152 + (j + 1) * 128)
                    last = product(PSQ[6], F0("down")[:, j * 128:(j + 1) * 128], f0_hi[:, c], src, h_lo[:, j % 4, :],
                                   start=j == 0, stop=j == 8)
                    last.then_inc(*((out_done.sem, 1) if j == 8 else (dn0_done.sem, 1)))

                up(0)
                up(1)
                transpose_gates(0, b, 4)
                kv_project(0, b)
                for j in range(2, 9):
                    up(j)
                    if j == 3:
                        kv_spread(0, b)
                    gate_rows(j - 1)
                    if j == 2:
                        down(0)
                    if j >= 4:
                        down(j - 3)
                    if j == 4:
                        norm_mean(*next_ln(1, b))
                    if j == 7:
                        norm_var(*next_ln(1, b))
                gate_rows(8)
                down(6)
                down(7)
                down(8)

            def ffn1(b):
                if b == 0:
                    pe.wait_ge(in_f1, 16)
                    pe.wait_ge(*weights1_lo.after(2))
                router(1, 3, b, 6, F1("rw"), None)
                if b:
                    pe.wait_ge(*yg_ready.after(0, b - 1, 7))
                kv_project(1, b)

                def down(n):
                    e = n // 2
                    pe.wait_ge(*lo_done(lo1_v, lo1_p, b, n))
                    if n % 2 == 0 and e >= 2:
                        pe.wait_ge(*yg_ready.after(0, b, e - 2))
                    product(PSQ[4 + e % 2], F1("w2")[:, n * 128:(n + 1) * 128],
                            f1_hi[:, 4096 + n * 128:4096 + (n + 1) * 128], hid2[:, n % 4, :], h_lo[:, n % 4, :],
                            start=n % 2 == 0, stop=n % 2 == 1).then_inc(dn1_done.sem, 1)

                for n in range(16):
                    c = slice(n * 128, (n + 1) * 128)
                    if n >= 2:
                        pe.wait_ge(*hh_ready.after(b, n - 2))
                    product(PSQ[n % 2], F1("w1")[:, c], f1_hi[:, c], xn[:, b, :], xn_lo[:, b, :])
                    product(PSQ[2 + n % 2], F1("w3")[:, c], f1_hi[:, 2048 + n * 128:2048 + (n + 1) * 128], xn[:, b, :],
                            xn_lo[:, b, :]).then_inc(up1_done.sem, 1)
                    if n == 1:
                        transpose_gates(1, b, 6)
                    if n == 2:
                        kv_spread(1, b)
                    if n == 5:
                        pe.wait_ge(*kb_ready.after(1, b))
                    if 3 <= n < 11:
                        spread_gate(1, b, n - 3)
                    if n >= 3:
                        down(n - 3)
                    if n == 5:
                        norm_mean(*next_ln(3, b))
                    if n == 10:
                        norm_var(*next_ln(3, b))
                down(13)
                down(14)
                down(15)

            def ffn2(b):
                if b == 0:
                    pe.wait_ge(in_f2, 16)
                pe.wait_ge(*xn_ready.after(5, b))
                for j in range(4):
                    E.matmul(PSQ[j], F2("w1")[:, j * 128:(j + 1) * 128], xn[:, b, :], start=True,
                             stop=True).then_inc(up2_done.sem, 1)
                kv_project(2, b)
                norm_mean(*next_ln(5, b))
                kv_spread(2, b)
                bank6_free(5, b)
                for j in range(4):
                    if j == 1:
                        norm_var(*next_ln(5, b))
                    pe.wait_ge(*h2_ready.after(b, j))
                    last = E.matmul(PSQ[6], F2("w2")[:, j * 128:(j + 1) * 128], hid2[:, j, :], start=j == 0,
                                    stop=j == 3)
                last.then_inc(out_done.sem, 1)

            def ffn3(b):
                if b == 0:
                    pe.wait_ge(in_f3, 16)
                router(2, 7, b, 6, F3("rw"), R("gb"))
                if b == 0:
                    pe.wait_ge(in_big, 16)
                    pe.wait_ge(*weights3_lo.after(3))
                else:
                    pe.wait_ge(*yg_ready.after(1, b - 1, 7))

                def down(n):
                    e, j = n // 4, n % 4
                    pe.wait_ge(*lo3.after(b, n))
                    if j == 0 and e >= 2:
                        pe.wait_ge(*yg_ready.after(1, b, e - 2))
                    product(PSQ[4 + e % 2], F3B("w2")[:, n * 128:(n + 1) * 128],
                            f3_hi[:, 4096 + n * 128:4096 + (n + 1) * 128], hid2[:, n % 4, :], h_lo[:, n % 4, :],
                            start=j == 0, stop=j == 3).then_inc(dn3_done.sem, 1)

                for n in range(32):
                    if n >= 4:
                        pe.wait_ge(*relu3.after(b, n - 4))
                    c = slice(n * 128, (n + 1) * 128)
                    product(PSQ[n % 4], F3B("w1")[:, c], f3_hi[:, c], xn[:, b, :], xn_lo[:, b, :]
                            ).then_inc(up3_done.sem, 1)
                    if n == 2:
                        slots_taken(b, 6)
                    if n == 4:
                        transpose_gates(2, b, 6)
                    if 6 <= n < 14:
                        spread_gate(2, b, n - 6)
                    if n >= 3:
                        down(n - 3)
                    if n == 16 and b == 0:
                        norm_mean(7, 1)
                    if n == 20 and b == 0:
                        norm_var(7, 1)
                down(29)
                down(30)
                down(31)

            for b in range(B):
                norm_mean(0, b)
                norm_var(0, b)
            l0_front(0)
            l0_front(1)
            l0_gather(0)
            l0_gather(1)
            l0_back(0)
            l0_back(1)
            stages = [None, ffn0, lambda b: attention(0, b), ffn1, lambda b: attention(1, b), ffn2,
                      lambda b: attention(2, b), ffn3]
            for s in range(1, 8):
                for b in range(B):
                    stages[s](b)

        def hq(j):
            return gbc[:, 6 + j % 2, :]

        def qt(j):
            return yg[:, j % 2, :]

        def big_gelu(j):
            return gbc[:, j % 4, :]

        def y01(j, i):
            return gbc[:, 2 * (j % 2) + i, :]

        def qlow(j):
            return gbc[:, 4 + j % 2, :]

        @block.scalar
        def _(act):
            def link(ins):
                steps["act"] += 1
                ins.then_inc(act_step, 1)
                act.wait_ge(act_step, steps["act"])

            def exp_and_log():
                A.preload_act_table_set("natural_log_exp_and_others")

            def norm_square(s, b):
                act.wait_ge(*ln_centered.after(s, b))
                if (s, b) != (0, 0):
                    act.wait_ge(*ln_var.after(s if b else s - 1, 1 - b))
                A.activation(sq[:, :], xc[:, b, :], ACT.Square).then_inc(ln_squared.sem, 1)

            def norm_rstd(s, b, tables=False):
                if tables:
                    exp_and_log()
                act.wait_ge(*ln_var.after(s, b))
                if (s, b) != (0, 0):
                    act.wait_ge(*xn_ready.after(s if b else s - 1, 1 - b))
                A.activation(rstd[:, :], PSQ[7], ACT.Ln, bias=eps_col[:, :]).then_inc(ln_log.sem, 1)
                act.wait_ge(*ln_log.after(s, b))
                A.activation(rstd[:, :], rstd[:, :], ACT.Exp, scale=-0.5).then_inc(ln_rstd.sem, 1)

            S0 = 0.5 / HD ** 0.5

            def l0_front(b):
                act.wait_ge(*qp_done.after(b))
                if b:
                    act.wait_ge(*off_done.after(b - 1))
                else:
                    act.wait_ge(in_l0, 16)
                    act.wait_ge(*dve_consts.after(0))
                A.activation(qp, PSQ[1], ACT.Identity, bias=L0("bq")).then_inc(qp_ready.sem, 1)
                for g in range(G):
                    act.wait_ge(*qrep_done.after(b, g))
                    A.activation(qrep[:, b, g, :], PSQ[3 + g % 2], ACT.Identity, bias=bq_s[:, g:g + 1],
                                 scale=S0).then_inc(qrep_ready.sem, 1)

            def l0_gather(b):
                for u in range(U):
                    g, k = u // NK, u % NK
                    if k < NK - 1:
                        for p in range(2):
                            act.wait_ge(*bc_done.after(b, u, p))
                            n = b * U + u - (1 if k else 2)
                            if n >= 0:
                                act.wait_ge(*oh_ready.after(n // U, n % U, p))
                            A.activation(ib[:, p, :], ps[0:MO, 2 * p:2 * p + 2, :], ACT.Copy).then_inc(ib_ready.sem, 1)
                    act.wait_ge(*wf_done.after(b, u))
                    if u >= 2:
                        act.wait_ge(*gw_ready.after(b, u - 2))
                    elif b:
                        act.wait_ge(*gw_ready.after(b - 1, U - 2 + u))
                    A.activation(at_wf[:, u % 2, :], PSQ[5], ACT.Identity, bias=C("patWb"),
                                 scale=C("signW")).then_inc(wf_ready.sem, 1)

            def l0_softmax(b):
                act.wait_ge(*s_shifted.after(b))
                A.activation(e80, s80, ACT.Exp).then_inc(s_exp.sem, 1)

            def kv_prepare(a, b):
                act.wait_ge(*v_done.after(a, b))
                if (a, b) == (0, 0):
                    act.wait_ge(in_att, 16)
                else:
                    act.wait_ge(*kb_ready.after(*((a, b - 1) if b else (a - 1, B - 1))))
                fn = ACT.Relu if a == 1 else ACT.Identity
                A.activation(kf, PSQ[5][:, 0:M], fn, bias=AW[a]("bk")).then_inc(kf_ready.sem, 1)
                A.activation(vf[:, b, :], PSQ[5][0:M, 128:256], fn).then_inc(v_ready.sem, 1)

            def attention(a, b):
                s = 2 * a + 2
                fn = ACT.Relu if a == 1 else ACT.Identity
                if (a, b) == (0, 0):
                    act.wait_ge(*bqs_ready.after(0))
                act.wait_ge(*q_done.after(a, b))
                A.activation(qf, PSQ[0], fn, bias=bqs[:, a:a + 1], scale=HD ** -0.5).then_inc(qf_ready.sem, 1)
                for g in range(2):
                    act.wait_ge(*qs_done.after(a, b, g))
                    A.activation(qs[:, g, :], PSQ[g], ACT.Copy).then_inc(qs_act.sem, 1)
                if a == 2:
                    act.wait_ge(*u_done.after(b))
                    A.activation(uT, ps[:, 4:6, :], ACT.Copy).then_inc(u_read.sem, 1)
                    act.wait_ge(*w0_shift.after(b))
                    A.activation(w0z[:, :, :], nmx[:, :, :], ACT.Exp, bias=refl[:, 7:8]).then_inc(w0_ready.sem, 1)
                act.wait_ge(*nT_done.after(a, b))
                if (a, b) == (0, 0):
                    act.wait_ge(*pad_ready.after(0))
                A.activation(shift_hi[0:MROW, :], PSQ[0][0:MROW, :], ACT.Copy).then_inc(nT_ready.sem, 1)
                if a == 2:
                    act.wait_ge(*wT_done.after(b))
                    A.activation(wT[0:32, :], PSQ[1][0:32, :], ACT.Copy).then_inc(wT_ready.sem, 1)
                nxt = next_ln(s, b)
                for n in range(H):
                    act.wait_ge(*sT_done.after(a, b, n))
                    if n >= RING:
                        act.wait_ge(*pv_done.after(a, b, n - RING))
                    A.activation(pT[:, n % RING, :], PSQ[n % 4][0:M, :], ACT.Exp,
                                 **(dict(bias=padT[:, b:b + 1]) if a == 0 else {})).then_inc(pT_ready.sem, 1)
                    if n == 7:
                        norm_square(*nxt)
                    if n == 15:
                        norm_rstd(*nxt)
                if a == 2:
                    act.wait_ge(*tot_ready.after(b))
                else:
                    act.wait_ge(*pv_done.after(a, b, H - 1))
                if a == 2:
                    link(A.activation(den_r, uT[:, 1, :], ACT.Ln))
                else:
                    A.activation(den_r[0:64, :], PSQ[4][64:128, :], ACT.Ln)
                    link(A.activation(den_r[64:128, :], PSQ[5][0:64, :], ACT.Ln))
                A.activation(den_r, den_r, ACT.Exp, scale=-1.0).then_inc(den_ready.sem, 1)

            def router(r, b):
                ne = GATES[r][0]
                act.wait_ge(*lg_shift.after(r, b))
                A.activation(lg[:, 1, :, 0:ne], lg[:, 0, :, 0:ne], ACT.Exp).then_inc(lg_exp.sem, 1)

            def spread_gate(r, b, e):
                act.wait_ge(*gb_done.after(r - 1, b, e))
                A.activation(gbc[:, e, :], PSQ[6], ACT.Copy).then_inc(gbc_ready.sem, 1)

            def ffn0(b):
                router(0, b)
                for j in range(9):
                    if j == 2:
                        kv_prepare(0, b)
                    act.wait_ge(*up0_done.after(b, j))
                    if j >= 5:
                        act.wait_ge(*hg_ready.after(b, j - 5))
                    dst = hid[:, 0, :] if j == 0 else big_gelu(j)
                    A.activation(dst, PSQ[j % 2], ACT.Gelu).then_inc(gelu0.sem, 1)
                    if j == 5:
                        norm_square(*next_ln(1, b))
                    if b and j in (4, 6, 8):
                        i = j // 2 - 2
                        act.wait_ge(in_f1, 16)
                        A.activation(f1_hi[:, 2048 * i:2048 * (i + 1)], f1_sb[:, 8 + 2048 * i:8 + 2048 * (i + 1)],
                                     ACT.Copy).then_inc(weights1_hi.sem, 1)
                norm_rstd(*next_ln(1, b), tables=True)

            def ffn1(b):
                router(1, b)
                kv_prepare(1, b)
                for n in range(16):
                    act.wait_ge(*up1_done.after(b, n))
                    if n >= 3:
                        act.wait_ge(*hh_ready.after(b, n - 3))
                    A.activation(hid[:, n % 3, :], PSQ[n % 2], ACT.Silu).then_inc(silu1.sem, 1)
                    if 3 <= n < 11:
                        spread_gate(1, b, n - 3)
                    if n == 6:
                        norm_square(*next_ln(3, b))
                norm_rstd(*next_ln(3, b), tables=True)

            def ffn2(b):
                def scaled(j):
                    act.wait_ge(*up2_done.after(b, j))
                    if j >= 2:
                        act.wait_ge(*h2_ready.after(b, j - 2))
                    elif b:
                        act.wait_ge(*h2_ready.after(b - 1, j + 2))
                    else:
                        act.wait_ge(*b2_ready.after(0))
                    A.activation(hq(j), PSQ[j], ACT.Identity, bias=b1x[:, j:j + 1], scale=256.0
                                 ).then_inc(h256.sem, 1)

                scaled(0)
                scaled(1)
                kv_prepare(2, b)
                for j in range(4):
                    act.wait_ge(*q2_ready.after(b, j))
                    if j >= 2:
                        act.wait_ge(*h2_ready.after(b, j - 2))
                    elif b:
                        act.wait_ge(*h2_ready.after(b - 1, j + 2))
                    A.activation(y01(j, 0), qlow(j), ACT.Gelu, scale=0.25)
                    A.activation(y01(j, 1), qlow(j), ACT.Gelu, scale=0.25, bias=refl[:, 6:7]).then_inc(gelu2.sem, 1)
                    if j == 0:
                        norm_square(*next_ln(5, b))
                    if j < 2:
                        scaled(j + 2)
                    if j >= 2:
                        i = 2 * b + j - 2
                        if i == 0:
                            act.wait_ge(in_big, 16)
                            act.wait_ge(*dn1_done.after(B - 1, 15))
                        A.activation(f3_hi[:, 2048 * i:2048 * (i + 1)], f3w[:, 2048 * i:2048 * (i + 1)], ACT.Copy
                                     ).then_inc(weights3_hi.sem, 1)
                norm_rstd(*next_ln(5, b), tables=True)

            def ffn3(b):
                router(2, b)
                for n in range(32):
                    act.wait_ge(*up3_done.after(b, n))
                    if n >= 4:
                        act.wait_ge(*dn3_done.after(b, n - 4))
                    A.activation(hid2[:, n % 4, :], PSQ[n % 4], ACT.Relu, bias=F3("b1")[:, n:n + 1]
                                 ).then_inc(relu3.sem, 1)
                    if 6 <= n < 14:
                        spread_gate(2, b, n - 6)
                    if n == 17 and b == 0:
                        norm_square(7, 1)
                    if n == 21 and b == 0:
                        norm_rstd(7, 1)

            act.wait_ge(in_first, 64)
            act.wait_ge(*consts_ready.after(0))
            A.activation(tg[:, :], g_raw[:, :], ACT.Tanh).then_inc(gates_tanh.sem, 1)
            exp_and_log()
            for b in range(B):
                norm_square(0, b)
                norm_rstd(0, b)
            l0_front(0)
            l0_front(1)
            l0_gather(0)
            l0_softmax(0)
            l0_gather(1)
            l0_softmax(1)
            act.wait_ge(in_f0, 16)
            A.activation(f0_hi[:, :], f0_sb[:, 16:16 + 2304], ACT.Copy).then_inc(weights0_hi.sem, 1)
            norm_square(1, 0)
            norm_rstd(1, 0)
            stages = [None, ffn0, lambda b: attention(0, b), ffn1, lambda b: attention(1, b), ffn2,
                      lambda b: attention(2, b), ffn3]
            for s in range(1, 8):
                for b in range(B):
                    stages[s](b)

        @block.gpsimd
        def _(pool):
            def link(ins):
                steps["pool"] += 1
                ins.then_inc(pool_step, 1)
                pool.wait_ge(pool_step, steps["pool"])

            P.memset(mean_w[:, :], 1.0 / D)
            P.memset(ones_bf[:, :], 1.0)
            P.memset(ones_row[:, :], 1.0)
            P.memset(eps_col[:, :], EPS)
            P.memset(gst[:, :], 0.0)
            P.memset(ap_[:, :, :], 0.0)
            P.memset(refl[:, 6:7], 0.25)
            P.memset(refl[:, 7:8], -1e-9)
            P.iota(loc[:, :], [[1, T]], base=0, channel_multiplier=0, allow_small_or_imprecise_dtypes=True
                   ).then_inc(consts_ready.sem, 1)
            for b in range(B):
                for part in range(2):
                    last = P.memset(tab[b][part], 0.0)
            last.then_inc(tab_zeroed.sem, 1)
            pool.wait_ge(in_first, 64)
            for g in range(G):
                last = P.tensor_copy(sel_rows[:, g, :, :].rearrange("p k (h c) -> p k h c", h=HG),
                                     C("ident")[:, 32 * g:32 * g + HG * NK].rearrange("p (h k) -> p k h", h=HG)
                                     .unsqueeze(3).broadcast_to([128, NK, HG, 32]))
            last.then_inc(rows_ready.sem, 1)

            def rest(out, src, sem):
                P.tensor_tensor(out, src, high(src), ALU.subtract).then_inc(sem, 1)

            for b in range(B):
                for u in range(U):
                    pool.wait_ge(*gw_ready.after(b, u))
                    pool.wait_ge(*qrep_ready.after(b, u // NK))
                    n = b * U + u
                    if n >= 3:
                        pool.wait_ge(*score_done.after((n - 3) // U, (n - 3) % U))
                    P.tensor_tensor(tq[:, u % 3, :], GW[:, b, u, :], qrep[:, b, u // NK, :], ALU.mult
                                    ).then_inc(tq_ready.sem, 1)
            for b in range(B):
                for g in range(G):
                    u = g * NK
                    pool.wait_ge(*t2_ready.after(b, u + 1))
                    link(P.tensor_tensor(GW[:, b, u, :], GW[:, b, u, :], GW[:, b, u + 1, :], ALU.add))
                    pool.wait_ge(*t2_ready.after(b, u + 2))
                    link(P.tensor_tensor(GW[:, b, u, :], GW[:, b, u, :], GW[:, b, u + 2, :], ALU.add))
                    pool.wait_ge(*t2_pair.after(b, g))
                    P.tensor_tensor(GW[:, b, u, :], GW[:, b, u, :], GW[:, b, u + 3, :], ALU.add
                                    ).then_inc(t2_sum.sem, 1)
                if b == 0:
                    pool.wait_ge(*weights0_hi.after(0))
                    w = f0_sb[:, 16:16 + 2304]
                    P.tensor_tensor(w, w, f0_hi[:, :], ALU.subtract).then_inc(weights0_lo.sem, 1)
            pool.wait_ge(*out_read.after(0, B - 1))
            P.memset(am_st, 0.0)
            P.memset(v_lo, 0.0)
            link(P.memset(v_hi, 0.0))
            for b in range(B):
                vb = v_hi[:, b, :].rearrange("m (h c) -> m h c", c=136)
                P.memset(vb[:, 0:8, 64:72], 1.0)
                last = P.memset(vb[:, 7:15, 72:80], 1.0)
            last.then_inc(zeroed.sem, 1)

            for b in range(B):
                if b:
                    pool.wait_ge(in_masks, 64)
                    pool.wait_ge(*pad_ready.after(0))
                    for bb in range(B):
                        last = P.tensor_tensor(amp[:, bb, :, :], am_sb[:, :, :], pad_row[:, bb * M:(bb + 1) * M]
                                               .unsqueeze(1).broadcast_to([128, NT, M]), ALU.add)
                    link(last)
                    rest(amp_lo.rearrange("p b t m -> p (b t m)"), amp.rearrange("p b t m -> p (b t m)"),
                         amp_ready.sem)
                for j in range(1, 9, 2):
                    pool.wait_ge(*hg_ready.after(b, j - 1))
                    if j >= 5:
                        pool.wait_ge(*dn0_done.after(b, j - 4))
                    rest(h_lo[:, j % 4, :], hid2[:, j % 4, :], lo0_p.sem)

            def probabilities(a, b):
                for n in range(H):
                    if on_pool(n):
                        pool.wait_ge(*pT_ready.after(a, b, n))
                        if n >= RING:
                            pool.wait_ge(*pv_done.after(a, b, n - RING))
                        rest(p_lo[:, n % RING, :], pT[:, n % RING, :], p_lo_p.sem)

            def accumulate(r, b, e):
                pool.wait_ge(*yg_ready.after(r, b, e))
                if e == 0:
                    if b:
                        pool.wait_ge(*residual.after(3 + 4 * r, b - 1))
                    P.tensor_copy(acc, yg[:, e % 2, :]).then_inc(acc_ready.sem, 1)
                else:
                    pool.wait_ge(*acc_ready.after(r, b, e - 1))
                    P.tensor_tensor(acc, acc, yg[:, e % 2, :], ALU.add).then_inc(acc_ready.sem, 1)

            for i in range(3):
                pool.wait_ge(*weights1_hi.after(i))
                w = f1_sb[:, 8 + 2048 * i:8 + 2048 * (i + 1)]
                P.tensor_tensor(w, w, f1_hi[:, 2048 * i:2048 * (i + 1)], ALU.subtract).then_inc(weights1_lo.sem, 1)
            pool.wait_ge(*out_read.after(1, B - 1))
            P.memset(ikT_st, 1.0).then_inc(ik_filled.sem, 1)
            for b in range(B):
                probabilities(0, b)
            for b in range(B):
                for n in range(1, 16, 2):
                    pool.wait_ge(*hh_ready.after(b, n))
                    if n >= 4:
                        pool.wait_ge(*dn1_done.after(b, n - 4))
                    rest(h_lo[:, n % 4, :], hid2[:, n % 4, :], lo1_p.sem)
                    if n >= 5:
                        accumulate(0, b, (n - 5) // 2)
                accumulate(0, b, 6)
                accumulate(0, b, 7)
            for b in range(B):
                probabilities(1, b)
            for b in range(B):
                for j in range(4):
                    pool.wait_ge(*gelu2.after(b, j))
                    if j or b:
                        pool.wait_ge(*h2_ready.after(*((b, j - 1) if j else (b - 1, 3))))
                    pool.wait_ge(*q2_ready.after(b, j))
                    d = hid[:, 1, :]
                    link(P.tensor_tensor(d, y01(j, 1), y01(j, 0), ALU.subtract))
                    link(P.tensor_tensor(d, d, qt(j), ALU.mult))
                    P.tensor_tensor(d, d, y01(j, 0), ALU.add).then_inc(dy_ready.sem, 1)
                for i in (2 * b, 2 * b + 1):
                    pool.wait_ge(*weights3_hi.after(i))
                    w = f3w[:, 2048 * i:2048 * (i + 1)]
                    P.tensor_tensor(w, w, f3_hi[:, 2048 * i:2048 * (i + 1)], ALU.subtract
                                    ).then_inc(weights3_lo.sem, 1)
            for b in range(B):
                probabilities(2, b)
            for b in range(B):
                for e in range(8):
                    accumulate(1, b, e)

        @block.vector
        def _(dve):
            def link(ins):
                steps["dve"] += 1
                ins.then_inc(dve_step, 1)
                dve.wait_ge(dve_step, steps["dve"])

            def rest(out, src, sem=None):
                ins = V.tensor_tensor(out, src, high(src), ALU.subtract)
                if sem is not None:
                    ins.then_inc(sem, 1)
                return ins

            def norm_center(s, b):
                dve.wait_ge(*ln_mean.after(s, b))
                V.tensor_tensor(xc[:, b, :], x[:, b, :], PSQ[7], ALU.subtract).then_inc(ln_centered.sem, 1)

            def norm_scale(s, b):
                dve.wait_ge(*ln_rstd.after(s, b))
                dve.wait_ge(*ln_centered.after(s, b))
                link(V.tensor_tensor(xn[:, b, :], xc[:, b, :], rstd[:, :], ALU.mult))
                rest(xn_lo[:, b, :], xn[:, b, :], xn_ready.sem)

            def add_branch(s, b, bias, relu=False):
                dve.wait_ge(*out_done.after(s - (s > 3), b))
                V.tensor_scalar(y_tmp[:, :], PSQ[6], bias, 0.0 if relu else None, ALU.add,
                                *((ALU.max,) if relu else ())).then_inc(out_read.sem, 1)
                dve.wait_ge(*out_read.after(s, b))
                V.scalar_tensor_tensor(x[:, b, :], y_tmp[:, :], tg[:, s:s + 1], x[:, b, :], ALU.mult, ALU.add
                                       ).then_inc(residual.sem, 1)

            def constants():
                dve.wait_ge(in_first, 64)
                dve.wait_ge(*consts_ready.after(0))
                V.tensor_copy(ident_bf[:, :], C("ident"))
                V.tensor_scalar(neg_ident[:, :], C("ident"), NEG, None, ALU.mult)
                V.tensor_copy(tri_bf[:, :], C("tri"))
                V.tensor_copy(hm_bf[:, :], C("headmask"))
                V.tensor_copy(selH[:, :, :], C("id16")[0:32, :].unsqueeze(2).broadcast_to([32, H, 8]))
                link(V.tensor_copy(mcnt[:, :], mif_sb[:, :]))
                link(V.tensor_reduce(Lb[:, :, 0], mcnt[:, :].rearrange("p (b m) -> p b m", b=2), AX.X, ALU.add))
                link(V.tensor_scalar(Lb[:, :, 1], Lb[:, :, 0], -1.0, float(M - 1), ALU.mult, ALU.add))
                link(V.tensor_scalar(Lb[:, :, 2], Lb[:, :, 1], -1.0, None, ALU.mult))
                link(V.tensor_tensor(Lb[:, :, 3], Lb[:, :, 1], Lb[:, :, 2], ALU.max))
                link(V.tensor_scalar(Lb[:, :, 4], Lb[:, :, 1], 0.0, None, ALU.is_ge))
                link(V.tensor_scalar(Lb[:, :, 4], Lb[:, :, 4], 2.0, -1.0, ALU.mult, ALU.add))
                link(V.reciprocal(Lb[:, :, 5], Lb[:, :, 3]))
                link(V.tensor_scalar(Lb[:, :, 6], Lb[:, :, 3], -1.0, None, ALU.mult))
                link(V.tensor_scalar(Lb[:, :, 7], Lb[:, :, 4], M / (M - 1.0), None, ALU.mult))
                dve.wait_ge(in_l0, 16)
                V.tensor_scalar(bq_s[:, :], L0("bqrep"), 0.5 / HD ** 0.5, None, ALU.mult).then_inc(dve_consts.sem, 1)

            def l0_front(b):
                dve.wait_ge(*tab_done.after(b))
                src = PSQ[0][0:MO, :].rearrange("m (s h c) -> m s h c", s=2, h=H)
                src = src.rearrange("m s (g h) c -> m s g h c", g=G)

                def block(part, s, h):
                    return tab[b][part].rearrange("m (g h c) -> m g h c", g=G, h=HG)[
                        :, :, h, 32 * h + 16 * s:32 * h + 16 * s + 16]

                spots = [(s, h) for s in range(2) for h in range(HG)]
                if b == 0:
                    dve.wait_ge(*tab_zeroed.after(0))
                for s, h in spots:
                    last = V.tensor_copy(block(0, s, h), src[:, s, :, h, :])
                link(last)
                for s, h in spots:
                    last = V.tensor_tensor(block(1, s, h), src[:, s, :, h, :], block(0, s, h), ALU.subtract)
                last.then_inc(tab_ready.sem, 1)
                dve.wait_ge(*off_done.after(b))
                L = Lb[:, b, :]
                V.tensor_scalar(ixt, PSQ[2], L0("boff"), C("refk"), ALU.add, ALU.add).then_inc(off_read.sem, 1)
                dve.wait_ge(*off_read.after(b))
                link(V.tensor_tensor(ixt, ixt, loc[:, :], ALU.add))
                link(V.tensor_scalar(ix1, ixt, L[:, 4:5], None, ALU.mult))
                link(V.tensor_scalar(ix2, ix1, L[:, 5:6], MAGIC, ALU.mult, ALU.add))
                link(V.tensor_scalar(ix2, ix2, -MAGIC, L[:, 6:7], ALU.add, ALU.mult))
                link(V.tensor_tensor(ix1, ix1, ix2, ALU.add))
                link(V.tensor_scalar(ix2, ix1, 0.0, L[:, 3:4], ALU.is_lt, ALU.mult))
                link(V.tensor_tensor(ix1, ix1, ix2, ALU.add))
                link(V.tensor_scalar(ix1, ix1, L[:, 7:8], -0.5, ALU.mult, ALU.add))
                link(V.tensor_scalar(ix2, ix1, MAGIC, -MAGIC, ALU.add, ALU.add))
                link(V.tensor_tensor(ixt, ix2, ix1, ALU.is_gt))
                link(V.tensor_tensor(ix2, ix2, ixt, ALU.subtract))
                link(V.tensor_tensor(ix1, ix1, ix2, ALU.subtract))
                V.tensor_scalar(i0bf[:, b, :], ix2, -2.0, float(M), ALU.max, ALU.min)
                link(V.tensor_copy(w1hi[:, b, :], ix1))
                V.tensor_tensor(w1lo[:, b, :], ix1, w1hi[:, b, :], ALU.subtract).then_inc(ix_ready.sem, 1)

            def l0_gather(b):
                def one_hots(u):
                    g, k = u // NK, u % NK
                    for p in range(2):
                        n = b * U + u
                        if n >= 2:
                            dve.wait_ge(*gather_done.after((n - 2) // U, (n - 2) % U))
                        if k < NK - 1:
                            dve.wait_ge(*ib_ready.after(b, g, k, p))
                            src = ib[:, p, :]
                        else:
                            dve.wait_ge(*bc_done.after(b, u, p))
                            src = ps[0:MO, 2 * p:2 * p + 2, :].rearrange("m a t -> m (a t)")
                        V.tensor_scalar(oh[:, u % 2, p, :], src, C("pos")[0:MO, :], None, ALU.is_equal
                                        ).then_inc(oh_ready.sem, 1)

                def weigh(u):
                    dve.wait_ge(*gather_done.after(b, u))
                    dve.wait_ge(*wf_ready.after(b, u))
                    V.tensor_tensor(GW[:, b, u, :], PSQ[(4, 7)[u % 2]], at_wf[:, u % 2, :], ALU.mult).then_inc(gw_ready.sem, 1)

                one_hots(0)
                for u in range(U):
                    if u + 1 < U:
                        one_hots(u + 1)
                    weigh(u)

            def l0_softmax(b):
                dve.wait_ge(*score_done.after(b, U - 1))
                sc = PSQ[6][:, 0:NT * H * NK].rearrange("p (n k) -> p n k", k=NK)
                s3 = s80.rearrange("p (n k) -> p n k", k=NK)
                e3 = e80.rearrange("p (n k) -> p n k", k=NK)
                link(V.tensor_reduce(s64[:, 0, :], sc, AX.X, ALU.max, negate=True))
                V.tensor_tensor(s3, sc, s64[:, 0, :].unsqueeze(2).broadcast_to([128, NT * H, NK]), ALU.add
                                ).then_inc(s_shifted.sem, 1)
                dve.wait_ge(*s_exp.after(b))
                link(V.tensor_reduce(s64[:, 1, :], e3, AX.X, ALU.add))
                link(V.reciprocal(s64[:, 2, :], s64[:, 1, :]))
                link(V.tensor_scalar(s64[:, 2, :], s64[:, 2, :], 0.5, None, ALU.mult))
                if b:
                    dve.wait_ge(*aT_done.after(b - 1))
                for t in range(NT):
                    for g in range(G):
                        n = t * H + g * HG
                        last = V.tensor_tensor(ap_[:, t, 32 * g:32 * g + 20].rearrange("p (h k) -> p h k", k=NK),
                                               e3[:, n:n + HG, :],
                                               s64[:, 2, n:n + HG].unsqueeze(2).broadcast_to([128, HG, NK]), ALU.mult)
                last.then_inc(a_ready.sem, 1)

            def l0_back(b):
                dve.wait_ge(*aT_done.after(b))
                link(V.tensor_copy(ahi, PSQ[0]))
                V.tensor_tensor(alo, PSQ[0], ahi, ALU.subtract).then_inc(aT_ready.sem, 1)
                for u in range(U):
                    dve.wait_ge(*ab_done.after(b, u))
                    V.tensor_tensor(GW[:, b, u, :], GW[:, b, u, :], PSQ[1 + u % 3], ALU.mult
                                    ).then_inc(t2_ready.sem, 1)
                    if u % NK == NK - 1:
                        dve.wait_ge(*t2_ready.after(b, u))
                        V.tensor_tensor(GW[:, b, u - 1, :], GW[:, b, u - 1, :], GW[:, b, u, :], ALU.add
                                        ).then_inc(t2_pair.sem, 1)
                    if b == 1 and u == 9:
                        norm_center(1, 0)
                    if b == 1 and u == 17:
                        norm_scale(1, 0)
                add_branch(0, b, L0("bo"))

            def kv_rest(a, b):
                dve.wait_ge(*kf_ready.after(a, b))
                rest(kl, kf, kl_ready.sem)
                dve.wait_ge(*v_ready.after(a, b))
                if (a, b) == (0, 0):
                    dve.wait_ge(*zeroed.after(0))
                if a == 2:
                    rest(vf_lo[:, b, :], vf[:, b, :])
                v1, v2 = (v[:, b, :].rearrange("m (h c) -> m h c", c=136)[:, :, 0:8] for v in (v_hi, v_lo))
                src = vf[:, b, :].rearrange("m (h d) -> m h d", h=H)
                link(V.tensor_copy(v1, src))
                V.tensor_tensor(v2, src, v1, ALU.subtract)

            def kv_tables(a, b):
                dve.wait_ge(*ks_done.after(a, b))
                V.tensor_tensor(kt[:, b, :, :].rearrange("p (g h) m -> p g h m", g=G),
                                PSQ[5][:, 0:G * M].rearrange("p (g m) -> p g m", g=G).unsqueeze(2)
                                .broadcast_to([128, G, HG, M]),
                                hm_bf[:, :].unsqueeze(1).unsqueeze(3).broadcast_to([128, G, HG, M]), ALU.mult
                                ).then_inc(kb_ready.sem, 1)

            def pads():
                dve.wait_ge(in_masks, 64)
                V.tensor_scalar(pad_row[:, :], mb8[:, :], NEG, None, ALU.mult)
                V.tensor_scalar(padT[:, :], mb8T[:, :], NEG, None, ALU.mult)
                link(V.tensor_copy(shift_hi, high(am_st)))
                V.tensor_tensor(shift_lo, am_st, shift_hi, ALU.subtract).then_inc(pad_ready.sem, 1)

            def selectors():
                V.tensor_copy(sel0[:, :, :], C("id32")[0:96, 0:16].unsqueeze(2).broadcast_to([96, 16, 64]))
                V.tensor_copy(sel1[:, :, :], C("id32")[0:96, 0:8].unsqueeze(2).broadcast_to([96, 8, 128]))

                one = C("ident").rearrange("p (h d) -> p h d", d=HD).unsqueeze(2).broadcast_to([128, H, 2, HD])
                for dst, slots in ((sel_qh, slice(0, 4, 2)), (sel_ql, slice(1, 4, 2)), (sel_kh, slice(0, 2)),
                                   (sel_kl, slice(2, 4))):
                    link(V.memset(dst, 0.0))
                    last = V.tensor_copy(dst.rearrange("p (h s d) -> p h s d", h=H, s=4)[:, :, slots, :], one)
                last.then_inc(sel_ready.sem, 1)

            def masks():
                dve.wait_ge(in_att, 16)
                for a in range(ATT):
                    V.tensor_scalar(bqs[:, a:a + 1], AW[a]("bq"), HD ** -0.5, None, ALU.mult)
                V.tensor_tensor(sel_shift,
                                C("id16").unsqueeze(2).broadcast_to([128, H, M]),
                                C("keys").unsqueeze(1).broadcast_to([128, H, M]), ALU.add).then_inc(bqs_ready.sem, 1)

            def overwritten_keys():
                dve.wait_ge(in_ik, 48)
                V.tensor_scalar(z[:, :, :], ik_sb[:, :, :], 0.0, None, ALU.is_equal)
                link(V.tensor_scalar(zT, ikT_sb[0:M], 0.0, None, ALU.is_equal))
                V.tensor_scalar(shift_hi, ikT_st.bitcast(i32), 0.0, NEG, ALU.is_equal, ALU.mult)
                link(V.tensor_reduce(zany[:, 0, :], z[:, :, :], AX.X, ALU.max))
                link(V.tensor_scalar(zany[:, 1, :], zany[:, 0, :], NEG, -NEG, ALU.mult, ALU.add))
                V.tensor_scalar(zany[:, 2, :], zany[:, 1, :], 1e-9, None, ALU.max).then_inc(z_ready.sem, 1)

            def attention(a, b):
                s = 2 * a + 2
                dve.wait_ge(*qf_ready.after(a, b))
                rest(q_lo, qf, qst_ready.sem)
                for g in (2, 3):
                    dve.wait_ge(*qs_done.after(a, b, g))
                    V.tensor_copy(qs[:, g, :], PSQ[g]).then_inc(qs_dve.sem, 1)
                for t in range(NT):
                    for half in range(2):
                        dve.wait_ge(*st_done.after(a, b, t, half))
                        V.tensor_reduce(nmx[:, t, 8 * half:8 * half + 8].rearrange("p (g h) -> p g h", g=2),
                                        ps[:, 2 * half:2 * half + 2, 0:HG * M].rearrange("p g (h m) -> p g h m", h=HG),
                                        AX.X, ALU.max, negate=True).then_inc(st_read.sem, 1)
                dve.wait_ge(*st_read.after(a, b, NT - 1, 1))
                if a == 2:
                    V.tensor_tensor(nmx[:, :, :], nmx[:, :, :], zany[:, 2, :].unsqueeze(2).broadcast_to([128, NT, H]),
                                    ALU.min).then_inc(w0_shift.sem, 1)
                    dve.wait_ge(*w0_shift.after(b))
                left = s64[:, 0, :].rearrange("p (t h) -> p t h", t=NT)
                link(V.tensor_copy(nst[:, :, 0, :], nmx[:, :, :]))
                link(V.tensor_tensor(left, nmx[:, :, :], nst[:, :, 0, :], ALU.subtract))
                link(V.tensor_copy(nst[:, :, 1, :], left))
                V.tensor_tensor(nst[:, :, 2, :], left, nst[:, :, 1, :], ALU.subtract).then_inc(nst_ready.sem, 1)
                if a == 2:
                    dve.wait_ge(*w0_ready.after(b))
                    link(V.tensor_copy(wst[:, :, 0, :], w0z[:, :, :]))
                    V.tensor_tensor(wst[:, :, 1, :], w0z[:, :, :], wst[:, :, 0, :], ALU.subtract
                                    ).then_inc(wst_ready.sem, 1)
                    dve.wait_ge(*wb_done.after(b))
                    dve.wait_ge(*u_read.after(b))
                    for i in range(2):
                        last = V.tensor_tensor(uT[:, i, :], uT[:, i, :], PSQ[2], ALU.mult)
                    last.then_inc(uw_ready.sem, 1)
                nxt = next_ln(s, b)
                for n in range(H):
                    if not on_pool(n):
                        dve.wait_ge(*pT_ready.after(a, b, n))
                        if n >= RING:
                            dve.wait_ge(*pv_done.after(a, b, n - RING))
                        rest(p_lo[:, n % RING, :], pT[:, n % RING, :], p_lo_v.sem)
                    if n == 7:
                        norm_center(*nxt)
                norm_scale(*nxt)
                dve.wait_ge(*pv_done.after(a, b, H - 1))
                halves = ((slice(0, 64), slice(64, 128), 4), (slice(64, 128), slice(0, 64), 5))
                if a == 2:
                    dve.wait_ge(*uw_ready.after(b))
                    for rows, sums, bank in halves:
                        V.tensor_tensor(uT[rows, 0, :], uT[rows, 0, :], PSQ[bank][rows, :], ALU.add)
                        last = V.tensor_tensor(uT[rows, 1, :], uT[rows, 1, :], PSQ[bank][sums, :], ALU.add)
                    last.then_inc(tot_ready.sem, 1)
                    dve.wait_ge(*tot_ready.after(b))
                dve.wait_ge(*den_ready.after(a, b))
                if a == 2:
                    V.tensor_tensor(oT, uT[:, 0, :], den_r, ALU.mult).then_inc(o_norm.sem, 1)
                else:
                    for rows, _, bank in halves:
                        last = V.tensor_tensor(oT[rows, :], PSQ[bank][rows, :], den_r[rows, :], ALU.mult)
                    last.then_inc(o_norm.sem, 1)
                add_branch(s, b, AW[a]("bo"), relu=a == 1)

            def router(r, b, bank):
                ne, topk = GATES[r]
                dve.wait_ge(*lg_done.after(r, b))
                lp = PSQ[bank][:, 0:NT * ne].rearrange("p (t e) -> p t e", t=NT)
                sh, ex, p, rank, one = (lg[:, i, :, 0:ne] for i in range(5))

                def tok(i):
                    return g4[:, i, :].unsqueeze(2).broadcast_to([128, NT, ne])

                link(V.tensor_reduce(g4[:, 0, :], lp, AX.X, ALU.max, negate=True))
                V.tensor_tensor(sh, lp, tok(0), ALU.add).then_inc(lg_shift.sem, 1)
                dve.wait_ge(*lg_exp.after(r, b))
                link(V.tensor_reduce(g4[:, 1, :], ex, AX.X, ALU.add))
                link(V.reciprocal(g4[:, 2, :], g4[:, 1, :]))
                link(V.tensor_tensor(p, ex, tok(2), ALU.mult))
                cmp1 = big[:, 0:NT * ne * ne].rearrange("p (t e j) -> p t e j", t=NT, e=ne)
                cmp2 = big2[:, 0:NT * ne * ne].rearrange("p (t e j) -> p t e j", t=NT, e=ne)
                pj = p.unsqueeze(2).broadcast_to([128, NT, ne, ne])
                pe_ = p.unsqueeze(3).broadcast_to([128, NT, ne, ne])
                tie = C("tie").rearrange("p (e j) -> p e j", e=16)[:, 0:ne, 0:ne]
                V.tensor_tensor(cmp1, pj, pe_, ALU.is_gt)
                link(V.tensor_tensor(cmp2, pj, pe_, ALU.is_equal))
                link(V.tensor_tensor(cmp2, cmp2, tie.unsqueeze(1).broadcast_to([128, NT, ne, ne]), ALU.mult))
                link(V.tensor_tensor(cmp1, cmp1, cmp2, ALU.add))
                link(V.tensor_reduce(rank, cmp1, AX.X, ALU.add))
                ga = gate[:, :, 0:ne]
                if r == 0:
                    V.scalar_tensor_tensor(ga, rank, float(topk), p, ALU.is_lt, ALU.mult).then_inc(gate_ready.sem, 1)
                elif r == 1:
                    link(V.scalar_tensor_tensor(one, rank, float(topk), p, ALU.is_lt, ALU.mult))
                    link(V.tensor_reduce(g4[:, 3, :], one, AX.X, ALU.add))
                    link(V.reciprocal(g4[:, 3, :], g4[:, 3, :]))
                    V.tensor_tensor(ga, one, tok(3), ALU.mult).then_inc(gate_ready.sem, 1)
                else:
                    V.tensor_scalar(oh12[:, b, :, 0, :], rank, 0.0, None, ALU.is_equal)
                    V.tensor_scalar(oh12[:, b, :, 1, :], rank, 1.0, None, ALU.is_equal).then_inc(oh12_ready.sem, 1)

            def capacity(b):
                dve.wait_ge(*cum_done.after(b))
                dve.wait_ge(*oh12_ready.after(b))
                one, p = lg[:, 4, :, 0:8], lg[:, 2, :, 0:8]
                link(V.scalar_tensor_tensor(k12[:, :, :, :].rearrange("p t c e -> p (t c e)"),
                                            PSQ[6][:, 0:NT * 16], float(CAP),
                                            oh12[:, b, :, :, :].rearrange("p t c e -> p (t c e)"),
                                            ALU.is_le, ALU.mult))
                link(V.tensor_tensor(one, k12[:, :, 0, :], k12[:, :, 1, :], ALU.add))
                V.tensor_tensor(gate[:, :, 0:8], one, p, ALU.mult).then_inc(gate_ready.sem, 1)

            def gate_parts(r, b, bank):
                ne = GATES[r][0]
                dve.wait_ge(*gT_done.after(r, b))
                link(V.tensor_copy(gst[0:ne, :], PSQ[bank][0:ne, :]))
                link(V.tensor_tensor(gr1[0:ne, :], PSQ[bank][0:ne, :], gst[0:ne, :], ALU.subtract))
                link(V.tensor_copy(glo[0:ne, :], gr1[0:ne, :]))
                V.tensor_copy(gst[32:32 + ne, :], glo[0:ne, :])
                V.tensor_tensor(gst[64:64 + ne, :], gr1[0:ne, :], glo[0:ne, :], ALU.subtract
                                ).then_inc(gst_ready.sem, 1)

            def expert_out(r, b, e, done, bias):
                dve.wait_ge(*done)
                dve.wait_ge(*gbc_ready.after(r, b, e))
                if e >= 2:
                    dve.wait_ge(*acc_ready.after(r, b, e - 2))
                elif b:
                    dve.wait_ge(*acc_ready.after(r, b - 1, 6 + e))
                if bias is None:
                    ins = V.tensor_tensor(yg[:, e % 2, :], PSQ[4 + e % 2], gbc[:, e, :], ALU.mult)
                else:
                    ins = V.scalar_tensor_tensor(yg[:, e % 2, :], PSQ[4 + e % 2], bias, gbc[:, e, :], ALU.add, ALU.mult)
                ins.then_inc(yg_ready.sem, 1)

            def add_sum(r, s, b):
                dve.wait_ge(*acc_ready.after(r, b, 7))
                V.memset(zany[0:1, 0, 0:1], 0.0).then_inc(out_read.sem, 1)
                V.scalar_tensor_tensor(x[:, b, :], acc, tg[:, s:s + 1], x[:, b, :], ALU.mult, ALU.add
                                       ).then_inc(residual.sem, 1)

            def ffn0(b):
                router(0, b, 4)
                gate_parts(0, b, 4)
                for j in range(9):
                    if j == 0:
                        dve.wait_ge(*gelu0.after(b, 0))
                        rest(h_lo[:, 0, :], hid[:, 0, :], lo0_v.sem)
                        if b == 0:
                            masks()
                        kv_rest(0, b)
                        if b == 0:
                            pads()
                        continue
                    dve.wait_ge(*gelu0.after(b, j))
                    dve.wait_ge(*ga_done.after(b, j - 1))
                    if j >= 4:
                        dve.wait_ge(*dn0_done.after(b, j - 4))
                    V.tensor_tensor(hid2[:, j % 4, :], big_gelu(j), PSQ[2 + j % 2], ALU.mult).then_inc(hg_ready.sem, 1)
                    if j % 2 == 0:
                        dve.wait_ge(*hg_ready.after(b, j - 1))
                        rest(h_lo[:, j % 4, :], hid2[:, j % 4, :], lo0_v.sem)
                    if j == 1:
                        kv_tables(0, b)
                    if j == 5:
                        norm_center(*next_ln(1, b))
                dve.wait_ge(*out_done.after(1, b))
                V.tensor_copy(y_tmp[:, :], PSQ[6]).then_inc(out_read.sem, 1)
                dve.wait_ge(*out_read.after(1, b))
                V.scalar_tensor_tensor(x[:, b, :], y_tmp[:, :], tg[:, 1:2], x[:, b, :], ALU.mult, ALU.add
                                       ).then_inc(residual.sem, 1)
                norm_scale(*next_ln(1, b))

            def ffn1(b):
                router(1, b, 6)
                for n in range(16):
                    dve.wait_ge(*silu1.after(b, n))
                    if n >= 4:
                        dve.wait_ge(*dn1_done.after(b, n - 4))
                    V.tensor_tensor(hid2[:, n % 4, :], hid[:, n % 3, :], PSQ[2 + n % 2], ALU.mult
                                    ).then_inc(hh_ready.sem, 1)
                    if n % 2 == 0:
                        dve.wait_ge(*hh_ready.after(b, n))
                        rest(h_lo[:, n % 4, :], hid2[:, n % 4, :], lo1_v.sem)
                    if n == 0:
                        kv_rest(1, b)
                    if n == 1:
                        gate_parts(1, b, 6)
                    if n == 2:
                        kv_tables(1, b)
                    if n >= 5 and n % 2:
                        e = (n - 5) // 2
                        expert_out(0, b, e, dn1_done.after(b, 2 * e + 1), None)
                    if n == 6:
                        norm_center(*next_ln(3, b))
                expert_out(0, b, 6, dn1_done.after(b, 13), None)
                expert_out(0, b, 7, dn1_done.after(b, 15), None)
                norm_scale(*next_ln(3, b))
                add_sum(0, 3, b)

            def ffn2(b):
                if b == 0:
                    dve.wait_ge(in_f2, 16)
                    link(V.tensor_scalar(b2x[:, 0:1], F2("b2"), 256.0, None, ALU.mult))
                    link(V.tensor_scalar(b2x[:, 1:2], tg[:, 5:6], 1.0 / 256, None, ALU.mult))
                    V.tensor_scalar(b1x[:, :], F2("b1"), 256.0, None, ALU.mult).then_inc(b2_ready.sem, 1)

                def quantise(j):
                    dve.wait_ge(*h256.after(b, j))
                    if j or b:
                        dve.wait_ge(*q2_ready.after(*((b, j - 1) if j else (b - 1, 3))))
                    n, t = hq(j), hid[:, 0, :]
                    link(V.tensor_scalar(n, n, MAGIC, -MAGIC, ALU.add, ALU.add))
                    link(V.tensor_scalar(t, n, -1024.0, 1024.0, ALU.max, ALU.min))
                    link(V.tensor_scalar(qt(j), t, 1.0 / 64, -63.0 / 128, ALU.mult, ALU.add))
                    if j >= 2:
                        dve.wait_ge(*dy_ready.after(b, j - 2))
                    link(V.tensor_scalar(qlow(j), qt(j), MAGIC, -MAGIC, ALU.add, ALU.add))
                    V.scalar_tensor_tensor(qt(j), t, 1.0 / 64, qlow(j), ALU.mult, ALU.subtract
                                           ).then_inc(q2_ready.sem, 1)

                def interpolate(j):
                    dve.wait_ge(*dy_ready.after(b, j))
                    if j:
                        dve.wait_ge(*h2_ready.after(b, j - 1))
                    d = hid[:, 1, :]
                    link(V.tensor_scalar(d, d, 256.0, MAGIC, ALU.mult, ALU.add))
                    link(V.tensor_scalar(hid[:, 2, :], hq(j), -1024.0, 0.0, ALU.add, ALU.max))
                    V.scalar_tensor_tensor(hid2[:, j, :], d, -MAGIC, hid[:, 2, :], ALU.add, ALU.add
                                           ).then_inc(h2_ready.sem, 1)

                quantise(0)
                kv_rest(2, b)
                for j in range(4):
                    if j == 1:
                        kv_tables(2, b)
                    if j < 3:
                        quantise(j + 1)
                    if j == 0:
                        norm_center(*next_ln(5, b))
                    interpolate(j)
                dve.wait_ge(*out_done.after(4, b))
                V.tensor_scalar(y_tmp[:, :], PSQ[6], b2x[:, 0:1], MAGIC, ALU.add, ALU.add).then_inc(out_read.sem, 1)
                dve.wait_ge(*out_read.after(5, b))
                link(V.tensor_scalar(y_tmp[:, :], y_tmp[:, :], -MAGIC, b2x[:, 1:2], ALU.add, ALU.mult))
                V.tensor_tensor(x[:, b, :], y_tmp[:, :], x[:, b, :], ALU.add).then_inc(residual.sem, 1)
                norm_scale(*next_ln(5, b))

            def ffn3(b):
                router(2, b, 6)
                for n in range(32):
                    dve.wait_ge(*relu3.after(b, n))
                    rest(h_lo[:, n % 4, :], hid2[:, n % 4, :], lo3.sem)
                    if n == 1:
                        capacity(b)
                    if n == 3:
                        gate_parts(2, b, 6)
                    if n >= 7 and n % 4 == 3:
                        e = n // 4 - 1
                        expert_out(1, b, e, dn3_done.after(b, 4 * e + 3), F3("b2")[:, e:e + 1])
                    if n == 16 and b == 0:
                        norm_center(7, 1)
                    if n == 23 and b == 0:
                        norm_scale(7, 1)
                expert_out(1, b, 7, dn3_done.after(b, 31), F3("b2")[:, 7:8])
                add_sum(1, 7, b)

            constants()
            dve.wait_ge(*gates_tanh.after(0))
            for b in range(B):
                norm_center(0, b)
                norm_scale(0, b)
            l0_front(0)
            l0_front(1)
            l0_gather(0)
            l0_softmax(0)
            l0_gather(1)
            l0_softmax(1)
            l0_back(0)
            l0_back(1)
            selectors()
            stages = [None, ffn0, lambda b: attention(0, b), ffn1, lambda b: attention(1, b), ffn2,
                      lambda b: attention(2, b), ffn3]
            for s in range(1, 8):
                if s == 6:
                    overwritten_keys()
                for b in range(B):
                    stages[s](b)


def kernel(**inputs):
    import numpy as np
    import concourse.bacc as _bacc
    from concourse import mybir as _mybir
    from concourse.bass_utils import run_bass_kernel_spmd as _run

    I = {k: np.asarray(v) for k, v in inputs.items()}
    f4 = np.float32

    def rowsof(a, n=128):
        return a.reshape(-1, n, a.shape[-1]).transpose(1, 0, 2).reshape(n, -1)

    def pad(a, n=128):
        return np.concatenate([a, np.zeros((n - a.shape[0],) + a.shape[1:], a.dtype)]) if a.shape[0] < n else a

    def pack(widths, **parts):
        for k, w in widths.items():
            assert parts[k].shape[1] == w, (k, parts[k].shape, w)
        return np.concatenate([pad(parts[k]) for k in widths], axis=1)

    col = lambda v: v.reshape(-1, 1)
    p = np.arange(128)
    r = p % 32
    const = dict(
        ident=np.eye(128, dtype=f4), tri=(p[:, None] <= p[None, :]).astype(f4),
        id32=(r[:, None] == np.arange(32)).astype(f4), id16=(((p % 16)[:, None] == np.arange(16)) & (p < 48)[:, None]).astype(f4),
        keys=((p - 48)[:, None] == np.arange(M)).astype(f4),
        headmask=((p // 32)[:, None] == np.arange(4)).astype(f4),
        tie=np.tile((np.arange(16)[None, :] < np.arange(16)[:, None]).reshape(1, 256), (128, 1)).astype(f4),
        signW=col(np.where(r // 8 < 2, -1.0, 1.0)).astype(f4),
        patWb=col(np.where((p % 32) // 8 < 2, 1.0, 0.0)).astype(f4),
        refk=col(np.where(r < 20, r % NK - 3, 0)).astype(f4), pos=col(p - 1).astype(f4),
        selS=((((p % 32) // 8) % 2 == 0)[:, None] & ((p // 32)[:, None] == np.arange(4))).astype(f4))

    def grouped(w):
        return np.repeat(w.reshape(G, HG, 1, HD, -1), 4, axis=2).reshape(G * 128, -1)

    wq, wk, wv, wo = (I[f"L0_xattn_{n}"] for n in ("Wq", "Wk", "Wv", "Wo"))
    woff, boff = I["L0_xattn_Woff"], I["L0_xattn_boff"]
    woff_p = np.zeros((G, 32, D), f4)
    woff_p[:, :HG * NK] = woff.reshape(G, HG * NK, D)
    boff_p = np.zeros((G, 32), f4)
    boff_p[:, :HG * NK] = boff.reshape(G, HG * NK)
    kv = np.stack([wk.reshape(H, HD, D), wv.reshape(H, HD, D)], 1).reshape(2 * D, D)
    bkv = np.stack([I["L0_xattn_bk"].reshape(H, HD), I["L0_xattn_bv"].reshape(H, HD)], 1).reshape(1, 2 * D)
    worep = np.zeros((G, HG, 4, HD, D), f4)
    worep[:, :, 1] = wo.T.reshape(G, HG, HD, D)
    worep[:, :, 3] = wo.T.reshape(G, HG, HD, D)
    ctx = np.zeros((D, B, M + 2), f4)
    ctx[:, :, 1:M + 1] = I["ctx_1024"].transpose(2, 0, 1)
    l0 = pack(L0_W, wq=wq.T, wqrep=grouped(wq).T, woff=woff_p.reshape(128, D).T, wkv=kv.T,
              worep=rowsof(worep.reshape(G * 128, D)), ctx=ctx.reshape(D, -1), bq=col(I["L0_xattn_bq"]),
              bqrep=grouped(col(I["L0_xattn_bq"])).reshape(G, 128).T, boff=col(boff_p), bo=col(I["L0_xattn_bo"]))
    valid = np.ones((2, MO), f4)
    valid[0, 0] = 0
    valid[1, MO - 1] = 0
    rows = np.concatenate([bkv, valid.reshape(1, -1)] + [I[f"L{n}_xattn_bv"].reshape(1, -1) for n in (1, 2, 3)]
                          + [I["L3_ffn_gate_b"].reshape(1, -1)], axis=1)

    att = []
    for n in (1, 2, 3):
        w = {k: I[f"L{n}_xattn_W{k}"] for k in "qkvo"}
        if n != 2:
            w = {k: v.T for k, v in w.items()}
        att.append(pack(ATT_W, wq=w["q"], wk=w["k"], wv=w["v"], wo=w["o"],
                        **{f"b{k}": col(I[f"L{n}_xattn_b{k}"]) for k in "qko"}))
    att = np.concatenate(att, axis=1)

    up = np.concatenate([I["L0_ffn_shared_up"], I["L0_ffn_routed_up"]]).reshape(18 * 64, D)
    down = np.concatenate([I["L0_ffn_shared_down"], I["L0_ffn_routed_down"]]).transpose(0, 2, 1).reshape(18 * 64, D)
    f0 = pack(F0_W, rw=I["L0_ffn_router_w"].T, up=up.T, down=rowsof(down))
    f1 = pack(F1_W, rw=I["L1_ffn_wg"].T, w1=I["L1_ffn_w1"].reshape(-1, D).T, w3=I["L1_ffn_w3"].reshape(-1, D).T,
              w2=rowsof(I["L1_ffn_w2"].transpose(0, 2, 1).reshape(-1, D)))
    f2 = pack(F2_W, w1=I["L2_ffn_w1"], w2=rowsof(I["L2_ffn_w2"]), b1=I["L2_ffn_b1"].reshape(4, 128).T,
              b2=col(I["L2_ffn_b2"]))
    f3 = pack(F3_W, rw=I["L3_ffn_gate_w"].T, b1=I["L3_ffn_b1"].reshape(32, 128).T, b2=I["L3_ffn_b2"].T)
    f3big = pack(F3_BIG, w1=I["L3_ffn_W1"].transpose(1, 0, 2).reshape(D, -1), w2=rowsof(I["L3_ffn_W2"].reshape(-1, D)))

    mbf = np.zeros((B, M, 4), np.bool_)
    mbf[:, :, 0] = I["mask_BxS2_bf0"]
    mbf = mbf.view(np.int32)[:, :, 0]
    tiles = lambda a: a.reshape(NT, 128, M).transpose(1, 0, 2)
    arrays = dict(
        xT=I["x"].reshape(B * T, D).T, g8=np.tile(np.stack([I["g_xattn"], I["g_ffn"]], 1).reshape(1, 8), (128, 1)),
        const=pack(CONST_W, **const), l0=l0, att=att, f0=f0, f1=f1, f2=f2, f3=f3, f3big=f3big, rows=rows,
        am_tok=tiles(I["fside_SxS2_0"]), am_T=I["fside_SxS2_0"].T,
        ik_tok=tiles(I["mask_SxS2_ik0"]), ik_T=I["mask_SxS2_ik0"].T,
        mif=np.tile(I["mask_BxS2_if0"].reshape(1, -1), (128, 1)),
        mbf_tok=np.tile(mbf.reshape(1, -1), (128, 1)), mbf_T=mbf.T)
    arrays = {k: np.ascontiguousarray(v) for k, v in arrays.items()}

    nc = _bacc.Bacc("TRN2", target_bir_lowering=False, num_devices=1)
    args = {k: nc.dram_tensor(k, v.shape, _mybir.dt.from_np(v.dtype), kind="ExternalInput").ap()
            for k, v in arrays.items()}
    out = nc.dram_tensor("outT", (D, B * T), _mybir.dt.from_np(np.dtype(f4)), kind="ExternalOutput").ap()
    bass_flamingo_gated_layers_kernel(nc, outT=out, **args)
    res = _run(nc, [arrays], core_ids=[0])
    return res.results[0]["outT"].T.reshape(B, T, D)
```

```python
import concourse.bass as bass
from concourse import mybir
from contextlib import ExitStack

B, T, D = 2, 512, 128
M = 77
H, HD = 16, 8
G, HG = 4, 4
NT, TT = T // 128, 128
NK = 5
MO = M + 1
ATT = 3
RING = 6
MROW = 48
POOL_HEADS = 6
GATES = ((16, 4), (8, 2), (8, 2))
CAP = 320
EPS = 1e-5
MAGIC = 12582912.0
NEG = -1e30

CONST_W = dict(ident=128, tri=128, id32=32, id16=16, keys=77, headmask=4, tie=256, signW=1,
               patWb=1, refk=1, pos=1, selS=4)
L0_W = dict(wq=128, wqrep=512, woff=128, wkv=256, worep=512, ctx=B * (M + 2), bq=1, bqrep=4, boff=1, bo=1)
ATT_W = dict(wq=128, wk=128, wv=128, wo=128, bq=1, bk=1, bo=1)
F0_W = dict(rw=16, up=1152, down=1152)
F1_W = dict(rw=8, w1=2048, w3=2048, w2=2048)
F2_W = dict(w1=512, w2=512, b1=4, b2=1)
F3_W = dict(rw=8, b1=32, b2=8)
F3_BIG = dict(w1=4096, w2=4096)
ROW_W = dict(bkv=256, valid=2 * MO, bv=ATT * 128, gb=8)


def offsets(widths):
    at, out = 0, {}
    for name, w in widths.items():
        out[name] = (at, w)
        at += w
    return out, at


class Signal:

    def __init__(self, sem, *dims):
        self.sem, self.dims = sem, dims

    def after(self, *key):
        n = 0
        for k, d in zip(key, self.dims):
            assert 0 <= k < d
            n = n * d + k
        return self.sem, n + 1


def bass_flamingo_gated_layers_kernel(nc, xT, g8, const, l0, att, f0, f1, f2, f3, f3big, rows, am_tok, am_T,
                  ik_tok, ik_T, mif, mbf_tok, mbf_T, outT):
    f32, bf16, i32 = mybir.dt.float32, mybir.dt.bfloat16, mybir.dt.int32
    ALU, ACT, AX = mybir.AluOpType, mybir.ActivationFunctionType, mybir.AxisListType
    V, A, P, E = nc.vector, nc.scalar, nc.gpsimd, nc.tensor

    with ExitStack() as ctx:
        def sb(name, shape, dt=f32):
            return ctx.enter_context(nc.sbuf_tensor(name, shape, dt))

        def signal(name, *dims):
            return Signal(ctx.enter_context(nc.semaphore(name)), *dims)

        def packed(tile, widths):
            cols, _ = offsets(widths)
            return lambda name: tile[:, cols[name][0]:cols[name][0] + cols[name][1]]

        x = sb("x", [128, B, T])
        tg = sb("tg", [128, 8])
        g_raw = sb("g_raw", [128, 8])
        const_sb = sb("const_sb", [128, offsets(CONST_W)[1]])
        C = packed(const_sb, CONST_W)
        l0_sb = sb("l0_sb", [128, offsets(L0_W)[1]])
        L0 = packed(l0_sb, L0_W)
        f0_sb = sb("f0_sb", [128, offsets(F0_W)[1]])
        F0 = packed(f0_sb, F0_W)
        f0_hi = sb("f0_hi", [128, 2 * 1152], bf16)
        f3_sb = sb("f3_sb", [128, offsets(F3_W)[1]])
        F3 = packed(f3_sb, F3_W)
        rows_sb = sb("rows_sb", [1, offsets(ROW_W)[1]])
        R = packed(rows_sb, ROW_W)
        ones_row = sb("ones_row", [1, 128])
        eps_col = sb("eps_col", [128, 1])
        mean_w = sb("mean_w", [128, 128])
        ones_bf = sb("ones_bf", [128, 128], bf16)
        ident_bf = sb("ident_bf", [128, 128], bf16)
        neg_ident = sb("neg_ident", [128, 128], bf16)
        tri_bf = sb("tri_bf", [128, 128], bf16)

        xc = sb("xc", [128, B, T])
        sq = sb("sq", [128, T])
        rstd = sb("rstd", [128, T])
        xn = sb("xn", [128, B, T])
        xn_lo = sb("xn_lo", [128, B, T], bf16)
        y_tmp = sb("y_tmp", [128, T])

        arena = sb("arena", [128, B * G * NK * T])
        GW = arena[:, :].rearrange("p (b u t) -> p b u t", b=B, u=G * NK)
        n_f3, n_f1, n_att = offsets(F3_BIG)[1], offsets(F1_W)[1], ATT * offsets(ATT_W)[1]
        f3w = arena[:, 0:n_f3]
        F3B = packed(f3w, F3_BIG)
        f1_sb = arena[:, n_f3:n_f3 + n_f1]
        F1 = packed(f1_sb, F1_W)
        att_sb = arena[:, n_f3 + n_f1:n_f3 + n_f1 + n_att].rearrange("p (a n) -> p a n", a=ATT)
        AW = [packed(att_sb[:, a, :], ATT_W) for a in range(ATT)]

        at, base = [n_f3 + n_f1 + n_att], [arena]

        def piece(n, dt=f32):
            w = n if dt == f32 else (n + 1) // 2
            assert at[0] + w <= base[0].shape[1], at[0]
            v = base[0][:, at[0]:at[0] + w]
            at[0] += w
            return v if dt == f32 else v.bitcast(dt)[:, 0:n]

        f1_hi = piece(3 * 2048, bf16)
        amp = piece(B * NT * M).rearrange("p (b t m) -> p b t m", b=B, t=NT)
        amp_lo = piece(B * NT * M, bf16).rearrange("p (b t m) -> p b t m", b=B, t=NT)
        mb8 = piece(B * M).bitcast(i32)
        pad_row = piece(B * M)
        sel_kh = piece(512, bf16)
        f3_hi = arena[:, n_f3:n_f3 + n_f3 // 2].bitcast(bf16)

        work = sb("work", [128, 10752])
        early = sb("early", [128, 7500])
        at[0], base[0] = 0, work
        qp = piece(T)
        qrep = piece(B * G * T).rearrange("p (b g t) -> p b g t", b=B, g=G)
        ixt = piece(T)
        ix1 = piece(T)
        ix2 = piece(T)
        i0bf = piece(B * T, bf16).rearrange("p (b t) -> p b t", b=B)
        w1hi = piece(B * T, bf16).rearrange("p (b t) -> p b t", b=B)
        w1lo = piece(B * T, bf16).rearrange("p (b t) -> p b t", b=B)
        at_wf = piece(2 * T).rearrange("p (r t) -> p r t", r=2)
        tq = piece(3 * T).rearrange("p (r t) -> p r t", r=3)
        ahi = piece(T, bf16)
        alo = piece(T, bf16)
        tq_lo = [qp[:, 0:T // 2].bitcast(bf16), qp[:, T // 2:T].bitcast(bf16), ahi]
        at[0] = 0
        qf = piece(T)
        q_lo = piece(T, bf16)
        qs = [piece(G * T, bf16).rearrange("p (g t) -> p g t", g=G)]
        wT = piece(T, bf16)
        oT = piece(T)
        den_r = piece(T)
        uT = piece(2 * T).rearrange("p (r t) -> p r t", r=2)
        pT = piece(RING * T)[0:M].rearrange("p (r t) -> p r t", r=RING)
        p_lo = piece(RING * T, bf16)[0:M].rearrange("p (r t) -> p r t", r=RING)
        nst = piece(B * NT * 3 * H, bf16).rearrange("p (b t a h) -> p b t a h", b=B, t=NT, a=3)
        at[0] = 10752 - 3 * T
        shift_hi = piece(T, bf16)
        shift_lo = piece(T, bf16)
        am_st = piece(T)
        am_sb = piece(NT * M).rearrange("p (t m) -> p t m", t=NT)
        at[0] = 10752 - 2 * T
        qs.append(piece(G * T, bf16).rearrange("p (g t) -> p g t", g=G))
        at[0] = 0
        gbc = piece(8 * T).rearrange("p (e t) -> p e t", e=8)
        hid = piece(3 * T).rearrange("p (r t) -> p r t", r=3)
        hid2 = piece(4 * T).rearrange("p (r t) -> p r t", r=4)
        h_lo = piece(4 * T, bf16).rearrange("p (r t) -> p r t", r=4)
        spare = piece(T)
        gr1 = spare[0:16]
        at[0] = 10752 - 3 * T
        acc = piece(T)
        yg = piece(2 * T).rearrange("p (r t) -> p r t", r=2)
        big = gbc[:, 4:6, :].rearrange("p e t -> p (e t)")
        big2 = gbc[:, 6:8, :].rearrange("p e t -> p (e t)")
        base[0], at[0] = early, 0
        loc = piece(T)
        sel_rows = piece(G * NK * 128, bf16).rearrange("p (g k c) -> p g k c", g=G, k=NK)
        tab = [[f0_sb[0:MO, 0:1024].bitcast(bf16), f0_sb[0:MO, 1024:2048].bitcast(bf16)],
               [f0_hi[0:MO, 0:2048], piece(2048, bf16)[0:MO]]]
        ib = piece(4 * T, bf16)[0:MO].rearrange("p (p2 t) -> p p2 t", p2=2)
        oh = piece(8 * T, bf16)[0:MO].rearrange("p (r p2 t) -> p r p2 t", r=2, p2=2)
        s80 = piece(NT * H * NK)
        e80 = piece(NT * H * NK)
        ap_ = piece(NT * 128).rearrange("p (t c) -> p t c", t=NT)
        mcnt = piece(2 * M)
        mif_sb = piece(2 * M).bitcast(i32)
        at[0] = 0
        kt = piece(B * H * M, bf16).rearrange("p (b h m) -> p b h m", b=B, h=H)
        v_hi = piece(B * 17 * 128, bf16)[0:M].rearrange("p (b c) -> p b c", b=B)
        v_lo = piece(B * 17 * 128, bf16)[0:M].rearrange("p (b c) -> p b c", b=B)
        f2_sb = piece(offsets(F2_W)[1])
        F2 = packed(f2_sb, F2_W)
        kf = piece(M)
        kl = piece(M, bf16)
        sel_shift = piece(H * M, bf16).rearrange("p (h m) -> p h m", h=H)
        nmx = piece(B * NT * H).rearrange("p (b t h) -> p b t h", b=B, t=NT)
        base[0], at[0] = f0_sb, 0
        vf = sb("vf", [M, B, D])
        vf_lo = sb("vf_lo", [M, B, D], bf16)
        ik_sb = piece(NT * M).bitcast(i32).rearrange("p (t m) -> p t m", t=NT)
        ikT_sb = piece(T).bitcast(i32)
        ikT_st = piece(T)
        z = piece(NT * M, bf16).rearrange("p (t m) -> p t m", t=NT)
        zT = piece(T, bf16)[0:M]
        wst = piece(NT * 2 * H, bf16).rearrange("p (t a h) -> p t a h", t=NT, a=2)
        w0z = piece(NT * H).rearrange("p (t h) -> p t h", t=NT)
        zany = piece(3 * NT).rearrange("p (i t) -> p i t", i=3)
        base[0], at[0] = l0_sb, 0
        sel0 = piece(16 * 64, bf16)[0:96].rearrange("p (e c) -> p e c", e=16)
        sel1 = piece(8 * 128, bf16)[0:96].rearrange("p (e c) -> p e c", e=8)
        sel_qh = piece(512, bf16)
        sel_ql = piece(512, bf16)
        sel_kl = sb("sel_kl", [128, 512], bf16)[:, :]
        gst = sb("gst", [96, T], bf16)

        refl = sb("refl", [128, 8])
        bq_s = sb("bq_s", [128, 4])
        Lb = sb("Lb", [128, 2, 8])
        s64 = sb("s64", [128, 3, NT * H])

        hm_bf = sb("hm_bf", [128, HG], bf16)
        bqs = sb("bqs", [128, ATT])
        selS_bf = sb("selS_bf", [128, HG], bf16)
        selH = sb("selH", [32, H, 8], bf16)
        mb8T = sb("mb8T", [M, B], i32)
        padT = sb("padT", [M, B])

        glo = sb("glo", [16, T], bf16)
        lg = sb("lg", [128, 5, NT, 16])
        g4 = sb("g4", [128, 4, NT])
        oh12 = sb("oh12", [128, B, NT, 2, 8], bf16)
        k12 = sb("k12", [128, NT, 2, 8])
        gate = sb("gate", [128, NT, 16])
        b2x = sb("b2x", [128, 2])
        b1x = sb("b1x", [128, 4])

        ps = ctx.enter_context(nc.psum_tensor("ps", [128, 8, 512], f32))

        def dma_sem(name):
            return ctx.enter_context(nc.semaphore(name))

        in_first, in_l0, in_rows, in_att, in_f0, in_f1, in_f2, in_f3, in_masks, in_big, in_ik = (dma_sem(n) for n in (
            "x_and_consts_in", "layer0_weights_in", "bias_rows_in", "attention_weights_in", "ffn0_weights_in",
            "ffn1_weights_in", "ffn2_weights_in", "ffn3_biases_in", "masks_in", "ffn3_weights_in", "overwrite_mask_in"))
        out_sem = dma_sem("out_stored")
        consts_ready = signal("consts_ready", 1)
        dve_consts = signal("dve_consts", 1)
        gates_tanh = signal("gates_tanh", 1)
        dve_step = ctx.enter_context(nc.semaphore("dve_step"))
        act_step = ctx.enter_context(nc.semaphore("act_step"))
        pool_step = ctx.enter_context(nc.semaphore("pool_step"))
        steps = {"dve": 0, "act": 0, "pool": 0}

        ln_mean = signal("ln_mean", 8, B)
        ln_centered = signal("ln_centered", 8, B)
        ln_squared = signal("ln_squared", 8, B)
        ln_var = signal("ln_var", 8, B)
        ln_log = signal("ln_log", 8, B)
        ln_rstd = signal("ln_rstd", 8, B)
        xn_ready = signal("xn_ready", 8, B)
        weights0_lo = signal("weights0_lo", 1)
        weights0_hi = signal("weights0_hi", 1)
        weights1_hi = signal("weights1_hi", 3)
        weights3_hi = signal("weights3_hi", 4)
        weights1_lo = signal("weights1_lo", 3)
        weights3_lo = signal("weights3_lo", 8)
        out_done = signal("out_done", 6, B)
        out_read = signal("out_read", 8, B)
        residual = signal("residual", 8, B)

        rows_ready = signal("rows_ready", 1)
        tab_zeroed = signal("tab_zeroed", 1)
        tab_done = signal("tab_done", B)
        tab_ready = signal("tab_ready", B)
        qp_done = signal("qp_done", B)
        qp_ready = signal("qp_ready", B)
        off_done = signal("off_done", B)
        off_read = signal("off_read", B)
        qrep_done = signal("qrep_done", B, G)
        qrep_ready = signal("qrep_ready", B, G)
        ix_ready = signal("ix_ready", B)
        U = G * NK
        bc_done = signal("bc_done", B, U, 2)
        ib_ready = signal("ib_ready", B, G, NK - 1, 2)
        t2_sum = signal("t2_sum", B, G)
        t2_pair = signal("t2_pair", B, G)
        oh_ready = signal("oh_ready", B, U, 2)
        gather_done = signal("gather_done", B, U)
        wf_done = signal("wf_done", B, U)
        wf_ready = signal("wf_ready", B, U)
        gw_ready = signal("gw_ready", B, U)
        tq_ready = signal("tq_ready", B, U)
        tq_rest = signal("tq_rest", B, U)
        score_done = signal("score_done", B, U)
        s_shifted = signal("s_shifted", B)
        s_exp = signal("s_exp", B)
        a_ready = signal("a_ready", B)
        aT_done = signal("aT_done", B)
        aT_ready = signal("aT_ready", B)
        ab_done = signal("ab_done", B, U)
        t2_ready = signal("t2_ready", B, U)
        t2_used = signal("t2_used", B, G)

        kf_ready = signal("kf_ready", ATT, B)
        kb_ready = signal("kb_ready", ATT, B)
        v_done = signal("v_done", ATT, B)
        v_ready = signal("v_ready", ATT, B)
        kl_ready = signal("kl_ready", ATT, B)
        ks_done = signal("ks_done", ATT, B)
        qs_done = signal("qs_done", ATT, B, G)
        qs_act = signal("qs_act", ATT, B, 2)
        qs_dve = signal("qs_dve", ATT, B, 2)
        q_done = signal("q_done", ATT, B)
        qf_ready = signal("qf_ready", ATT, B)
        qst_ready = signal("qst_ready", ATT, B)
        st_done = signal("st_done", ATT, B, NT * G)
        st_read = signal("st_read", ATT, B, NT * G)
        nst_ready = signal("nst_ready", ATT, B)
        nT_done = signal("nT_done", ATT, B)
        nT_ready = signal("nT_ready", ATT, B)
        sT_done = signal("sT_done", ATT, B, H)
        pT_ready = signal("pT_ready", ATT, B, H)
        p_lo_v = signal("p_lo_v", ATT, B, H - POOL_HEADS)
        p_lo_p = signal("p_lo_p", ATT, B, POOL_HEADS)
        pv_done = signal("pv_done", ATT, B, H)
        den_ready = signal("den_ready", ATT, B)
        wb_done = signal("wb_done", B)
        uw_ready = signal("uw_ready", B)
        wT_done = signal("wT_done", B)
        wT_ready = signal("wT_ready", B)
        wst_ready = signal("wst_ready", B)
        tot_ready = signal("tot_ready", B)
        o_norm = signal("o_norm", ATT, B)
        amp_ready = signal("amp_ready", 1)
        w0_shift = signal("w0_shift", B)
        w0_ready = signal("w0_ready", B)
        u_done = signal("u_done", B)
        u_read = signal("u_read", B)
        ik_filled = signal("ik_filled", 1)
        z_ready = signal("z_ready", 1)
        sel_ready = signal("sel_ready", 1)
        bqs_ready = signal("bqs_ready", 1)
        pad_ready = signal("pad_ready", 1)
        zeroed = signal("zeroed", 1)

        lg_done = signal("lg_done", 3, B)
        lg_shift = signal("lg_shift", 3, B)
        lg_exp = signal("lg_exp", 3, B)
        oh12_ready = signal("oh12_ready", B)
        cum_done = signal("cum_done", B)
        gate_ready = signal("gate_ready", 3, B)
        gT_done = signal("gT_done", 3, B)
        gst_ready = signal("gst_ready", 3, B)
        gb_done = signal("gb_done", 2, B, 8)
        gbc_ready = signal("gbc_ready", 2, B, 8)
        up0_done = signal("up0_done", B, 9)
        gelu0 = signal("gelu0", B, 9)
        ga_done = signal("ga_done", B, 8)
        hg_ready = signal("hg_ready", B, 8)
        dn0_done = signal("dn0_done", B, 8)
        lo0_v = signal("lo0_v", B, 5)
        lo0_p = signal("lo0_p", B, 4)
        lo1_v = signal("lo1_v", B, 8)
        lo1_p = signal("lo1_p", B, 8)
        lo3 = signal("lo3", B, 32)
        up1_done = signal("up1_done", B, 16)
        silu1 = signal("silu1", B, 16)
        hh_ready = signal("hh_ready", B, 16)
        dn1_done = signal("dn1_done", B, 16)
        yg_ready = signal("yg_ready", 2, B, 8)
        acc_ready = signal("acc_ready", 2, B, 8)
        up2_done = signal("up2_done", B, 4)
        h256 = signal("h256", B, 4)
        b2_ready = signal("b2_ready", 1)
        dy_ready = signal("dy_ready", B, 4)
        q2_ready = signal("q2_ready", B, 4)
        gelu2 = signal("gelu2", B, 4)
        h2_ready = signal("h2_ready", B, 4)
        up3_done = signal("up3_done", B, 32)
        relu3 = signal("relu3", B, 32)
        dn3_done = signal("dn3_done", B, 32)

        block = ctx.enter_context(nc.Block())
        PSQ = [ps[:, k, :] for k in range(8)]

        def high(ap):
            return ap.bitcast(bf16)[:, 1::2]

        def next_ln(s, b):
            return (s, 1) if b == 0 else (s + 1, 0) if s < 7 else None

        def on_pool(n):
            return n % 8 in (1, 4, 6)

        def p_split(a, b, n):
            k = sum(on_pool(i) for i in range(n))
            return p_lo_p.after(a, b, k) if on_pool(n) else p_lo_v.after(a, b, n - k)

        def lo_done(v, p, b, n):
            return v.after(b, n // 2) if n % 2 == 0 else p.after(b, n // 2)

        def lgt(r, b):
            if (r, b) == (0, 1):
                return hid[:, 1, 0:5 * NT * 16].rearrange("p (i t e) -> p i t e", i=5, t=NT)
            return lg[:, :, :, :]

        def gates_of(r, b):
            if (r, b) == (0, 1):
                return hid[:, 1, 5 * NT * 16:6 * NT * 16].rearrange("p (t e) -> p t e", t=NT)
            return gate[:, :, :]

        def hq(b, j):
            if b == 0:
                return hid2[:, j, :]
            return (h_lo[:, 0:2, :].rearrange("p r t -> p (r t)").bitcast(f32),
                    h_lo[:, 2:4, :].rearrange("p r t -> p (r t)").bitcast(f32), hid[:, 1, :], spare)[j]

        def score_bank(b, u):
            return PSQ[(3, 6)[u % 2] if b else (3, 6, 0, 1)[u % 4]]

        def between(j):
            return gbc[:, 6 + j % 2, :]

        def qt(j):
            return yg[:, j % 2, :]

        def big_gelu(j):
            return gbc[:, j % 4, :]

        def y01(j, i):
            return gbc[:, 2 * (j % 2) + i, :]

        def qlow(j):
            return gbc[:, 4 + j % 2, :]

        @block.sync
        def _(sp):
            sp.dma_start(x[:, :, :], xT.rearrange("p (b t) -> p b t", b=B)).then_inc(in_first, 16)
            sp.dma_start(const_sb[:, :], const).then_inc(in_first, 16)
            sp.dma_start(mif_sb[:, :], mif).then_inc(in_first, 16)
            sp.dma_start(g_raw[:, :], g8).then_inc(in_first, 16)
            sp.dma_start(l0_sb[:, :], l0).then_inc(in_l0, 16)
            sp.dma_start(rows_sb[:, :], rows).then_inc(in_rows, 16)
            sp.dma_start(f3_sb[:, :], f3).then_inc(in_f3, 16)
            sp.wait_ge(*gather_done.after(B - 1, U - 1))
            sp.dma_start(f0_sb[:, :], f0).then_inc(in_f0, 16)
            sp.wait_ge(*out_read.after(0, B - 1))
            sp.dma_start(att_sb, att.rearrange("p (a n) -> p a n", a=ATT)).then_inc(in_att, 16)
            for dst, src in ((am_sb[:, :, :], am_tok), (mb8[:, :], mbf_tok), (mb8T[:, :], mbf_T)):
                sp.dma_start(dst, src).then_inc(in_masks, 16)
            sp.dma_start(f1_sb[:, :], f1).then_inc(in_f1, 16)
            sp.wait_ge(*zeroed.after(0))
            sp.dma_start(am_st[MROW:MROW + M, :], am_T).then_inc(in_masks, 16)
            sp.dma_start(f2_sb[:, :], f2).then_inc(in_f2, 16)
            sp.dma_start(f3w, f3big).then_inc(in_big, 16)
            sp.wait_ge(*out_read.after(1, B - 1))
            sp.dma_start(ik_sb, ik_tok).then_inc(in_ik, 16)
            sp.dma_start(ikT_sb[0:M], ik_T).then_inc(in_ik, 16)
            sp.wait_ge(*ik_filled.after(0))
            sp.dma_start(ikT_st[MROW:MROW + M, :].bitcast(i32), ik_T).then_inc(in_ik, 16)
            for b in range(B):
                sp.wait_ge(*residual.after(7, b))
                sp.dma_start(outT[:, b * T:(b + 1) * T], x[:, b, :]).then_inc(out_sem, 16)
            sp.wait_ge(out_sem, 16 * B)

        @block.tensor
        def _(pe):
            def product(out, w_rest, w, r, r_rest, start=True, stop=True):
                E.matmul(out, w, high(r), start=start, stop=False)
                E.matmul(out, w, r_rest, start=False, stop=False)
                return E.matmul(out, high(w_rest), high(r), start=False, stop=stop)

            def norm_mean(s, b):
                if s == 0:
                    if b == 0:
                        pe.wait_ge(in_first, 64)
                        pe.wait_ge(*consts_ready.after(0))
                else:
                    pe.wait_ge(*residual.after(s - 1, b))
                if (s, b) != (0, 0):
                    pe.wait_ge(*ln_log.after(s if b else s - 1, 1 - b))
                E.matmul(PSQ[7], mean_w[:, :], x[:, b, :], start=True, stop=True).then_inc(ln_mean.sem, 1)

            def norm_var(s, b):
                pe.wait_ge(*ln_squared.after(s, b))
                E.matmul(PSQ[7], mean_w[:, :], sq[:, :], start=True, stop=True).then_inc(ln_var.sem, 1)

            def bank6_free(s, b):
                if (s, b) != (0, 0):
                    pe.wait_ge(*out_read.after(s if b else s - 1, 1 - b))

            def l0_front(b):
                if b:
                    pe.wait_ge(*qrep_ready.after(0, G - 1))
                    pe.wait_ge(*tab_ready.after(0))
                    pe.wait_ge(*off_read.after(0))
                else:
                    pe.wait_ge(in_l0, 16)
                    pe.wait_ge(in_rows, 16)
                for slot in range(2):
                    out = PSQ[0][0:MO, slot * 256:(slot + 1) * 256]
                    c0 = b * (M + 2) + slot
                    E.matmul(out, L0("ctx")[:, c0:c0 + MO], L0("wkv"), start=True, stop=False)
                    last = E.matmul(out, R("valid")[:, slot * MO:(slot + 1) * MO], R("bkv"), start=False, stop=True)
                last.then_inc(tab_done.sem, 1)
                if b == 0:
                    norm_mean(0, 1)
                pe.wait_ge(*xn_ready.after(0, b))
                E.matmul(PSQ[1], L0("wq"), xn[:, b, :], start=True, stop=True).then_inc(qp_done.sem, 1)
                pe.wait_ge(*qp_ready.after(b))
                E.matmul(PSQ[2], L0("woff"), qp, start=True, stop=True).then_inc(off_done.sem, 1)
                if b == 0:
                    norm_var(0, 1)
                for g in range(G):
                    if g >= 2:
                        pe.wait_ge(*qrep_ready.after(b, g - 2))
                    E.matmul(PSQ[3 + g % 2], L0("wqrep")[:, g * 128:(g + 1) * 128], xn[:, b, :],
                             start=True, stop=True).then_inc(qrep_done.sem, 1)

            def head_rows(g, k):
                return sel_rows[:, g, k, :]

            def l0_gather():
                def spread(b, u, g, k):
                    for p in range(2):
                        if k:
                            pe.wait_ge(*ib_ready.after(b, g, k - 1, p))
                        elif u:
                            pe.wait_ge(*oh_ready.after(b, u - 1, p))
                        elif b:
                            pe.wait_ge(*oh_ready.after(b - 1, U - 1, p))
                        for i in range(2):
                            c = 32 * g + NK * (2 * p + i) + k
                            last = E.matmul(PSQ[2 * p + i][0:MO, :], ident_bf[:, c:c + 1].broadcast_to([128, MO]),
                                            i0bf[:, b, :], start=True, stop=True)
                        last.then_inc(bc_done.sem, 1)
                    if u:
                        pe.wait_ge(*wf_ready.after(b, u - 1))
                    elif b:
                        pe.wait_ge(*wf_ready.after(b - 1, U - 1))
                    E.matmul(PSQ[5], head_rows(g, k), w1hi[:, b, :], start=True, stop=False)
                    E.matmul(PSQ[5], head_rows(g, k), w1lo[:, b, :], start=False, stop=True).then_inc(wf_done.sem, 1)

                def gather(b, u, g, k):
                    n = b * U + u
                    if n >= 2:
                        pe.wait_ge(*gw_ready.after((n - 2) // U, (n - 2) % U))
                    pe.wait_ge(*oh_ready.after(b, u, 1))
                    out = PSQ[(4, 7)[u % 2]]
                    for part in range(2):
                        for h in range(HG):
                            c = (HG * g + h) * 128
                            last = E.matmul(out, tab[b][part][:, c:c + 128],
                                            oh[:, u % 2, h // 2, (h % 2) * T:(h % 2 + 1) * T],
                                            start=(part, h) == (0, 0), stop=(part, h) == (1, HG - 1))
                    last.then_inc(gather_done.sem, 1)

                def score(b, u, g, k):
                    pe.wait_ge(*tq_rest.after(b, u))
                    if u == 0 and b:
                        pe.wait_ge(*s_shifted.after(b - 1))
                    sc = PSQ[6][:, 0:NT * H * NK].rearrange("p (t h k) -> p t h k", t=NT, h=H)
                    for t in range(NT):
                        out, c = sc[:, t, HG * g:HG * g + HG, k], slice(t * 128, (t + 1) * 128)
                        E.matmul(out, high(tq[:, u % 3, c]), selS_bf[:, :], start=True, stop=False)
                        last = E.matmul(out, tq_lo[u % 3][:, c], selS_bf[:, :], start=False, stop=True)
                    last.then_inc(score_done.sem, 1)

                units = [(b, g * NK + k, g, k) for b in range(B) for g in range(G) for k in range(NK)]
                pe.wait_ge(*ix_ready.after(0))
                pe.wait_ge(*off_read.after(B - 1))
                pe.wait_ge(*rows_ready.after(0))
                pe.wait_ge(*tab_ready.after(B - 1))
                pe.wait_ge(*qrep_ready.after(B - 1, G - 1))
                spread(*units[0])
                for n in range(B * U):
                    if n + 1 == U:
                        pe.wait_ge(*ix_ready.after(1))
                    if n + 1 < B * U:
                        spread(*units[n + 1])
                    gather(*units[n])
                    if n:
                        score(*units[n - 1])
                score(*units[B * U - 1])

            def l0_back(b):
                pe.wait_ge(*a_ready.after(b))
                if b == 0:
                    pe.wait_ge(*gw_ready.after(B - 1, U - 1))
                    pe.wait_ge(*s_shifted.after(B - 1))
                else:
                    pe.wait_ge(*out_read.after(0, 0))
                for t in range(NT):
                    last = E.transpose(PSQ[0][:, t * 128:(t + 1) * 128], ap_[:, t, :], C("ident"))
                last.then_inc(aT_done.sem, 1)
                pe.wait_ge(*aT_ready.after(b))

                def project(g):
                    pe.wait_ge(*t2_sum.after(b, g))
                    last = E.matmul(PSQ[6], L0("worep")[:, g * 128:(g + 1) * 128], GW[:, b, g * NK, :],
                                    start=g == 0, stop=g == G - 1)
                    last.then_inc(*((out_done.sem, 1) if g == G - 1 else (t2_used.sem, 1)))

                for u in range(U):
                    g, k = u // NK, u % NK
                    if u >= 5:
                        pe.wait_ge(*t2_ready.after(b, u - 5))
                    for part, a_part in enumerate((ahi, alo)):
                        last = E.matmul(PSQ[1 + u % 5], head_rows(g, k), a_part, start=part == 0, stop=part == 1)
                    last.then_inc(ab_done.sem, 1)
                    if k == 3 and g:
                        project(g - 1)
                    if b == 1 and u == 6:
                        norm_mean(1, 0)
                    if b == 1 and u == 12:
                        norm_var(1, 0)
                project(G - 1)

            def kv_project(a, b):
                if (a, b) == (0, 0):
                    pe.wait_ge(in_att, 16)
                else:
                    pe.wait_ge(*kb_ready.after(*((a, b - 1) if b else (a - 1, B - 1))))
                c0 = b * (M + 2) + 1
                E.matmul(PSQ[5][:, 0:M], AW[a]("wk"), L0("ctx")[:, c0:c0 + M], start=True,
                         stop=True)
                E.matmul(PSQ[5][0:M, 128:256], L0("ctx")[:, c0:c0 + M], AW[a]("wv"), start=True, stop=False)
                E.matmul(PSQ[5][0:M, 128:256], ones_row[:, 0:M], R("bv")[:, a * 128:(a + 1) * 128],
                         start=False, stop=True).then_inc(v_done.sem, 1)

            def kv_spread(a, b):
                pe.wait_ge(*kl_ready.after(a, b))
                pe.wait_ge(*v_ready.after(a, b))
                for g in range(G):
                    out = PSQ[5][:, g * M:(g + 1) * M]
                    E.matmul(out, sel_kh[:, g * 128:(g + 1) * 128], high(kf), start=True, stop=False)
                    last = E.matmul(out, sel_kl[:, g * 128:(g + 1) * 128], kl, start=False, stop=True)
                last.then_inc(ks_done.sem, 1)

            def project_q(a, b):
                s = 2 * a + 2
                pe.wait_ge(*xn_ready.after(s, b))
                if b == 0:
                    if a == 1:
                        pe.wait_ge(*yg_ready.after(0, B - 1, 7))
                    bank6_free(s, 0)
                E.matmul(PSQ[3], AW[a]("wq"), xn[:, b, :], start=True, stop=True).then_inc(q_done.sem, 1)
                pe.wait_ge(*kb_ready.after(a, b))
                if (a, b) == (0, 0):
                    pe.wait_ge(*zeroed.after(0))
                    pe.wait_ge(*amp_ready.after(0))
                if a == 2:
                    pe.wait_ge(*z_ready.after(0))

            def spread_q(a, b, g):
                if g < 2:
                    pe.wait_ge(*qst_ready.after(a, b))
                else:
                    pe.wait_ge(*(qs_dve if g % 2 else qs_act).after(a, b, 0))
                out = PSQ[(3, 6)[g % 2]]
                E.matmul(out, sel_qh[:, g * 128:(g + 1) * 128], high(qf), start=True, stop=False)
                E.matmul(out, sel_ql[:, g * 128:(g + 1) * 128], q_lo, start=False, stop=True).then_inc(qs_done.sem, 1)

            def scores(a, b, u):
                t, g = u // G, u % G
                banks = 2 if b else 4
                if u >= banks:
                    pe.wait_ge(*st_read.after(a, b, u - banks))
                else:
                    pe.wait_ge(*qs_act.after(a, b, 1))
                    pe.wait_ge(*qs_dve.after(a, b, 1))
                out = score_bank(b, u)[:, 0:HG * M]
                last = E.matmul(out, qs[b][:, g, t * 128:(t + 1) * 128],
                                kt[:, b, HG * g:HG * g + HG, :].rearrange("p h m -> p (h m)"), start=True, stop=a == 1)
                more = []
                if a == 0:
                    more = [(ident_bf, high(amp[:, b, t, :])), (ident_bf, amp_lo[:, b, t, :])]
                if a == 2:
                    more = [(neg_ident, z[:, t, :])]
                for i, (w, part) in enumerate(more):
                    last = E.matmul(out.rearrange("p (h m) -> p h m", h=HG), w[:, :],
                                    part.unsqueeze(1).broadcast_to([128, HG, M]),
                                    start=False, stop=i == len(more) - 1)
                last.then_inc(st_done.sem, 1)

            def shift_rows(a, b):
                pe.wait_ge(*nst_ready.after(a, b))
                for t in range(NT):
                    last = E.matmul(PSQ[3][0:MROW, t * 128:(t + 1) * 128],
                                    nst[:, b, t, :, :].rearrange("p a h -> p (a h)"), ident_bf[:, :],
                                    start=True, stop=True)
                last.then_inc(nT_done.sem, 1)
                if a == 2:
                    E.matmul(PSQ[4], high(vf[:, b, :]), zT, start=True, stop=False)
                    E.matmul(PSQ[4], vf_lo[:, b, :], zT, start=False, stop=True)
                    E.matmul(PSQ[5], ones_bf[0:M, :], zT, start=True, stop=True).then_inc(u_done.sem, 1)
                    pe.wait_ge(*wst_ready.after(b))
                    for t in range(NT):
                        last = E.matmul(PSQ[6][0:32, t * 128:(t + 1) * 128],
                                        wst[:, t, :, :].rearrange("p a h -> p (a h)"), ident_bf[:, :],
                                        start=True, stop=True)
                    last.then_inc(wT_done.sem, 1)
                pe.wait_ge(*nT_ready.after(a, b))

            def spread_overwritten(b):
                pe.wait_ge(*wT_ready.after(b))
                E.matmul(PSQ[3], selH[:, :, :].rearrange("p h c -> p (h c)"), wT[0:32, :], start=True,
                         stop=True).then_inc(wb_done.sem, 1)

            def scores_T(a, b, n):
                m = b * H + n
                if m >= 3:
                    pe.wait_ge(*pT_ready.after(a, (m - 3) // H, (m - 3) % H))
                out, k = PSQ[m % 3][0:M, :], MROW if a == 1 else 128
                E.matmul(out, kt[:, b, n, :], qs[b][:, n // HG, :], start=True, stop=False)
                last = E.matmul(out, sel_shift[0:k, n, :], shift_hi[0:k, :], start=False, stop=a != 0)
                if a == 0:
                    last = E.matmul(out, sel_shift[:, n, :], shift_lo, start=False, stop=True)
                last.then_inc(sT_done.sem, 1)

            def values(a, b, n):
                pe.wait_ge(*p_split(a, b, n))
                w = slice(n * 128, (n + 1) * 128)
                out, p, first, last = PSQ[4 + n // 8], high(pT[:, n % RING, :]), n % 8 == 0, n % 8 == 7
                E.matmul(out, v_hi[:, b, w], p, start=first, stop=False)
                E.matmul(out, v_hi[:, b, w], p_lo[:, n % RING, :], start=False, stop=False)
                E.matmul(out, v_lo[:, b, w], p, start=False, stop=last).then_inc(pv_done.sem, 1)

            def project_out(a, b):
                pe.wait_ge(*o_norm.after(a, b))
                pe.wait_ge(*st_read.after(a, B - 1, NT * G - 1))
                bank6_free(2 * a + 2, b)
                E.matmul(PSQ[6], AW[a]("wo"), oT, start=True, stop=True).then_inc(out_done.sem, 1)

            def attention(a):
                s = 2 * a + 2
                project_q(a, 0)
                norm_mean(s, 1)
                for g in range(G):
                    spread_q(a, 0, g)
                for u in range(NT * G):
                    scores(a, 0, u)
                    if u == 7:
                        norm_var(s, 1)
                shift_rows(a, 0)
                for n in range(H):
                    scores_T(a, 0, n)
                    if a == 2 and n == 1:
                        spread_overwritten(0)
                    if n == (2 if a == 2 else 1):
                        if a == 2:
                            pe.wait_ge(*uw_ready.after(0))
                            pe.wait_ge(*u_read.after(0))
                        project_q(a, 1)
                    if n in (4, 5):
                        spread_q(a, 1, 2 * n - 8)
                        spread_q(a, 1, 2 * n - 7)
                    if 6 <= n < 14:
                        scores(a, 1, 2 * n - 12)
                        scores(a, 1, 2 * n - 11)
                    if n >= 3:
                        values(a, 0, n - 3)
                for n in range(H - 3, H):
                    values(a, 0, n)
                if a == 2:
                    project_out(a, 0)
                shift_rows(a, 1)
                for n in range(H):
                    scores_T(a, 1, n)
                    if a == 2 and n == 1:
                        spread_overwritten(1)
                        pe.wait_ge(*u_read.after(1))
                    if n == 2 and a != 2:
                        project_out(a, 0)
                    if n >= 3:
                        values(a, 1, n - 3)
                    if n == 5:
                        norm_mean(s + 1, 0)
                    if n == 13:
                        norm_var(s + 1, 0)
                for n in range(H - 3, H):
                    values(a, 1, n)
                if a == 0:
                    pe.wait_ge(*pT_ready.after(a, 1, H - 1))
                    ffn1_up(0, 0)
                    ffn1_up(0, 1)
                if a == 1:
                    pe.wait_ge(*pT_ready.after(a, 1, H - 1))
                    ffn2_up(0)
                if a == 2:
                    pe.wait_ge(*pT_ready.after(a, 1, H - 1))
                    for n in range(3):
                        ffn3_up(0, n)
                project_out(a, 1)

            def router(r, s, b, bank, rw, bias):
                ne = GATES[r][0]
                if (r, b) != (0, 1):
                    bank6_free(s, b)
                pe.wait_ge(*xn_ready.after(s, b))
                c0 = NT * ne if (r, b) == (0, 1) else 0
                for t in range(NT):
                    out = PSQ[bank][:, c0 + t * ne:c0 + (t + 1) * ne]
                    last = E.matmul(out, xn[:, b, t * 128:(t + 1) * 128], rw, start=True, stop=bias is None)
                    if bias is not None:
                        last = E.matmul(out, ones_row[:, :], bias, start=False, stop=True)
                last.then_inc(lg_done.sem, 1)

            def slots_taken(b, bank):
                pe.wait_ge(*oh12_ready.after(b))
                for t in range(NT):
                    out = PSQ[bank][:, t * 16:(t + 1) * 16]
                    before = [(bb, tt) for bb in range(B) for tt in range(NT) if (bb, tt) < (b, t)]
                    last = E.matmul(out, tri_bf[:, :], oh12[:, b, t, :, :].rearrange("p c e -> p (c e)"),
                                    start=True, stop=not before)
                    for n, (bb, tt) in enumerate(before):
                        last = E.matmul(out, ones_bf[:, :], oh12[:, bb, tt, :, :].rearrange("p c e -> p (c e)"),
                                        start=False, stop=n == len(before) - 1)
                last.then_inc(cum_done.sem, 1)

            def transpose_gates(r, b, bank):
                ne = GATES[r][0]
                pe.wait_ge(*gate_ready.after(r, b))
                for t in range(NT):
                    last = E.transpose(PSQ[bank][0:ne, t * 128:(t + 1) * 128], gates_of(r, b)[:, t, 0:ne], C("ident"))
                last.then_inc(gT_done.sem, 1)

            def spread_gate(r, b, e):
                if e:
                    pe.wait_ge(*gbc_ready.after(r - 1, b, e - 1))
                else:
                    pe.wait_ge(*gst_ready.after(r, b))
                E.matmul(PSQ[6], sel1[:, e, :], gst[:, :], start=True, stop=True).then_inc(gb_done.sem, 1)

            def ffn0(b):
                if b == 0:
                    pe.wait_ge(in_f0, 16)
                    pe.wait_ge(*weights0_lo.after(0))
                    router(0, 1, 0, 4, F0("rw"), None)
                    norm_mean(1, 1)
                else:
                    bank6_free(1, 1)

                def up(j):
                    if j >= 2:
                        pe.wait_ge(*gelu0.after(b, j - 2))
                    product(PSQ[j % 2], F0("up")[:, j * 128:(j + 1) * 128], f0_hi[:, j * 128:(j + 1) * 128],
                            xn[:, b, :], xn_lo[:, b, :]).then_inc(up0_done.sem, 1)

                def gate_rows(j):
                    if j == 1:
                        pe.wait_ge(*gst_ready.after(0, b))
                    if j >= 3:
                        pe.wait_ge(*hg_ready.after(b, j - 3))
                    E.matmul(PSQ[2 + j % 2], sel0[:, 2 * j - 2:2 * j, :].rearrange("p a c -> p (a c)"), gst[:, :],
                             start=True, stop=True).then_inc(ga_done.sem, 1)

                def down(j):
                    pe.wait_ge(*lo_done(lo0_v, lo0_p, b, j))
                    src = hid[:, 0, :] if j == 0 else hid2[:, j % 4, :]
                    c = slice(1152 + j * 128, 1152 + (j + 1) * 128)
                    last = product(PSQ[6], F0("down")[:, j * 128:(j + 1) * 128], f0_hi[:, c], src, h_lo[:, j % 4, :],
                                   start=j == 0, stop=j == 8)
                    last.then_inc(*((out_done.sem, 1) if j == 8 else (dn0_done.sem, 1)))

                up(0)
                if b == 0:
                    norm_var(1, 1)
                up(1)
                if b == 0:
                    router(0, 1, 1, 4, F0("rw"), None)
                    pe.wait_ge(*lg_shift.after(0, 1))
                transpose_gates(0, b, 4)
                kv_project(0, b)
                for j in range(2, 9):
                    up(j)
                    if j == 3:
                        kv_spread(0, b)
                    gate_rows(j - 1)
                    if j == 2:
                        down(0)
                    if j >= 4:
                        down(j - 3)
                    if b and j == 4:
                        norm_mean(2, 0)
                    if b and j == 7:
                        norm_var(2, 0)
                gate_rows(8)
                down(6)
                down(7)
                down(8)

            def ffn1_up(b, n):
                if (b, n) == (0, 0):
                    pe.wait_ge(in_f1, 16)
                    pe.wait_ge(*weights1_lo.after(2))
                    pe.wait_ge(*xn_ready.after(3, 0))
                if n >= 2:
                    pe.wait_ge(*hh_ready.after(b, n - 2))
                c = slice(n * 128, (n + 1) * 128)
                product(PSQ[n % 2], F1("w1")[:, c], f1_hi[:, c], xn[:, b, :], xn_lo[:, b, :])
                product(PSQ[2 + n % 2], F1("w3")[:, c], f1_hi[:, 2048 + n * 128:2048 + (n + 1) * 128], xn[:, b, :],
                        xn_lo[:, b, :]).then_inc(up1_done.sem, 1)

            def ffn1(b):
                router(1, 3, b, 6, F1("rw"), None)
                if b:
                    pe.wait_ge(*yg_ready.after(0, b - 1, 7))
                kv_project(1, b)

                def down(n):
                    e = n // 2
                    pe.wait_ge(*lo_done(lo1_v, lo1_p, b, n))
                    if n % 2 == 0 and e >= 2:
                        pe.wait_ge(*yg_ready.after(0, b, e - 2))
                    product(PSQ[4 + e % 2], F1("w2")[:, n * 128:(n + 1) * 128],
                            f1_hi[:, 4096 + n * 128:4096 + (n + 1) * 128], hid2[:, n % 4, :], h_lo[:, n % 4, :],
                            start=n % 2 == 0, stop=n % 2 == 1).then_inc(dn1_done.sem, 1)

                for n in range(16):
                    if b or n >= 2:
                        ffn1_up(b, n)
                    if n == 1:
                        transpose_gates(1, b, 6)
                    if n == 2:
                        kv_spread(1, b)
                    if n == 5:
                        pe.wait_ge(*kb_ready.after(1, b))
                    if 3 <= n < 11:
                        spread_gate(1, b, n - 3)
                    if n >= 3:
                        down(n - 3)
                    if n == 5:
                        norm_mean(*next_ln(3, b))
                    if n == 10:
                        norm_var(*next_ln(3, b))
                down(13)
                down(14)
                down(15)

            def ffn2_up(b):
                if b == 0:
                    pe.wait_ge(in_f2, 16)
                pe.wait_ge(*xn_ready.after(5, b))
                for j in range(4):
                    if b:
                        pe.wait_ge(*h256.after(0, j))
                    E.matmul(PSQ[j], F2("w1")[:, j * 128:(j + 1) * 128], xn[:, b, :], start=True,
                             stop=True).then_inc(up2_done.sem, 1)

            def ffn2_down(b, j):
                if j == 0:
                    bank6_free(5, b)
                pe.wait_ge(*h2_ready.after(b, j))
                last = E.matmul(PSQ[6], F2("w2")[:, j * 128:(j + 1) * 128], hq(b, j), start=j == 0, stop=j == 3)
                if j == 3:
                    last.then_inc(out_done.sem, 1)

            def ffn2():
                norm_mean(5, 1)
                kv_project(2, 0)
                norm_var(5, 1)
                kv_spread(2, 0)
                ffn2_up(1)
                kv_project(2, 1)
                for j in range(4):
                    ffn2_down(0, j)
                norm_mean(6, 0)
                kv_spread(2, 1)
                ffn2_down(1, 0)
                ffn2_down(1, 1)
                norm_var(6, 0)
                ffn2_down(1, 2)
                ffn2_down(1, 3)

            def ffn3_up(b, n):
                if (b, n) == (0, 0):
                    pe.wait_ge(in_big, 16)
                    pe.wait_ge(*weights3_lo.after(7))
                    pe.wait_ge(*xn_ready.after(7, 0))
                if n >= 4:
                    pe.wait_ge(*relu3.after(b, n - 4))
                c = slice(n * 128, (n + 1) * 128)
                product(PSQ[n % 4], F3B("w1")[:, c], f3_hi[:, c], xn[:, b, :], xn_lo[:, b, :]
                        ).then_inc(up3_done.sem, 1)

            def ffn3(b):
                if b == 0:
                    pe.wait_ge(in_f3, 16)
                router(2, 7, b, 6, F3("rw"), R("gb"))
                if b:
                    pe.wait_ge(*yg_ready.after(1, b - 1, 7))

                def down(n):
                    e, j = n // 4, n % 4
                    pe.wait_ge(*lo3.after(b, n))
                    if j == 0 and e >= 2:
                        pe.wait_ge(*yg_ready.after(1, b, e - 2))
                    product(PSQ[4 + e % 2], F3B("w2")[:, n * 128:(n + 1) * 128],
                            f3_hi[:, 4096 + n * 128:4096 + (n + 1) * 128], hid2[:, n % 4, :], h_lo[:, n % 4, :],
                            start=j == 0, stop=j == 3).then_inc(dn3_done.sem, 1)

                for n in range(32):
                    if b or n >= 3:
                        ffn3_up(b, n)
                    if n == 2:
                        slots_taken(b, 6)
                    if n == 4:
                        transpose_gates(2, b, 6)
                    if 6 <= n < 14:
                        spread_gate(2, b, n - 6)
                    if n >= 3:
                        down(n - 3)
                    if n == 16 and b == 0:
                        norm_mean(7, 1)
                    if n == 20 and b == 0:
                        norm_var(7, 1)
                down(29)
                down(30)
                down(31)

            norm_mean(0, 0)
            norm_var(0, 0)
            l0_front(0)
            l0_front(1)
            l0_gather()
            l0_back(0)
            l0_back(1)
            for a, ffn in ((0, ffn0), (1, ffn1)):
                ffn(0)
                ffn(1)
                attention(a)
            ffn2()
            attention(2)
            ffn3(0)
            ffn3(1)

        @block.scalar
        def _(act):
            def link(ins):
                steps["act"] += 1
                ins.then_inc(act_step, 1)
                act.wait_ge(act_step, steps["act"])

            def exp_and_log():
                A.preload_act_table_set("natural_log_exp_and_others")

            def norm_square(s, b):
                act.wait_ge(*ln_centered.after(s, b))
                if (s, b) != (0, 0):
                    act.wait_ge(*ln_var.after(s if b else s - 1, 1 - b))
                A.activation(sq[:, :], xc[:, b, :], ACT.Square).then_inc(ln_squared.sem, 1)

            def norm_rstd(s, b, tables=False):
                if tables:
                    exp_and_log()
                act.wait_ge(*ln_var.after(s, b))
                if (s, b) != (0, 0):
                    act.wait_ge(*xn_ready.after(s if b else s - 1, 1 - b))
                A.activation(rstd[:, :], PSQ[7], ACT.Ln, bias=eps_col[:, :]).then_inc(ln_log.sem, 1)
                act.wait_ge(*ln_log.after(s, b))
                A.activation(rstd[:, :], rstd[:, :], ACT.Exp, scale=-0.5).then_inc(ln_rstd.sem, 1)

            S0 = 0.5 / HD ** 0.5

            def l0_front(b):
                act.wait_ge(*qp_done.after(b))
                if b:
                    act.wait_ge(*off_done.after(b - 1))
                else:
                    act.wait_ge(in_l0, 16)
                    act.wait_ge(*dve_consts.after(0))
                A.activation(qp, PSQ[1], ACT.Identity, bias=L0("bq")).then_inc(qp_ready.sem, 1)
                if b == 0:
                    norm_square(0, 1)
                    norm_rstd(0, 1)
                for g in range(G):
                    act.wait_ge(*qrep_done.after(b, g))
                    A.activation(qrep[:, b, g, :], PSQ[3 + g % 2], ACT.Identity, bias=bq_s[:, g:g + 1],
                                 scale=S0).then_inc(qrep_ready.sem, 1)

            def l0_gather(b):
                for u in range(U):
                    g, k = u // NK, u % NK
                    if k < NK - 1:
                        for p in range(2):
                            act.wait_ge(*bc_done.after(b, u, p))
                            n = b * U + u - (1 if k else 2)
                            if n >= 0:
                                act.wait_ge(*oh_ready.after(n // U, n % U, p))
                            A.activation(ib[:, p, :], ps[0:MO, 2 * p:2 * p + 2, :], ACT.Copy).then_inc(ib_ready.sem, 1)
                    act.wait_ge(*wf_done.after(b, u))
                    if u >= 2:
                        act.wait_ge(*gw_ready.after(b, u - 2))
                    elif b:
                        act.wait_ge(*gw_ready.after(b - 1, U - 2 + u))
                    A.activation(at_wf[:, u % 2, :], PSQ[5], ACT.Identity, bias=C("patWb"),
                                 scale=C("signW")).then_inc(wf_ready.sem, 1)
                    if b and u == 2:
                        l0_softmax(0)

            def l0_softmax(b):
                act.wait_ge(*s_shifted.after(b))
                A.activation(e80, s80, ACT.Exp).then_inc(s_exp.sem, 1)

            def kv_prepare(a, b):
                act.wait_ge(*v_done.after(a, b))
                if (a, b) == (0, 0):
                    act.wait_ge(in_att, 16)
                else:
                    act.wait_ge(*kb_ready.after(*((a, b - 1) if b else (a - 1, B - 1))))
                fn = ACT.Relu if a == 1 else ACT.Identity
                A.activation(kf, PSQ[5][:, 0:M], fn, bias=AW[a]("bk")).then_inc(kf_ready.sem, 1)
                A.activation(vf[:, b, :], PSQ[5][0:M, 128:256], fn).then_inc(v_ready.sem, 1)

            def queries(a, b):
                fn = ACT.Relu if a == 1 else ACT.Identity
                if (a, b) == (0, 0):
                    act.wait_ge(*bqs_ready.after(0))
                act.wait_ge(*q_done.after(a, b))
                if b:
                    act.wait_ge(*qs_done.after(a, 0, G - 1))
                A.activation(qf, PSQ[3], fn, bias=bqs[:, a:a + 1], scale=HD ** -0.5).then_inc(qf_ready.sem, 1)

            def queries_spread(a, b, i):
                if (a, b, i) == (0, 1, 0):
                    act.wait_ge(*pad_ready.after(0))
                    act.wait_ge(*amp_ready.after(0))
                act.wait_ge(*qs_done.after(a, b, 2 * i))
                A.activation(qs[b][:, 2 * i, :], PSQ[3], ACT.Copy).then_inc(qs_act.sem, 1)

            def shift_rows(a, b):
                if a == 2:
                    act.wait_ge(*w0_shift.after(b))
                    A.activation(w0z[:, :, :], nmx[:, b, :, :], ACT.Exp, bias=refl[:, 7:8]).then_inc(w0_ready.sem, 1)
                act.wait_ge(*nT_done.after(a, b))
                if (a, b) == (0, 0):
                    act.wait_ge(*pad_ready.after(0))
                if b:
                    act.wait_ge(*sT_done.after(a, 0, H - 1))
                A.activation(shift_hi[0:MROW, :], PSQ[3][0:MROW, :], ACT.Copy).then_inc(nT_ready.sem, 1)
                if a == 2:
                    act.wait_ge(*u_done.after(b))
                    A.activation(uT, ps[:, 4:6, :], ACT.Copy).then_inc(u_read.sem, 1)
                    act.wait_ge(*wT_done.after(b))
                    A.activation(wT[0:32, :], PSQ[6][0:32, :], ACT.Copy).then_inc(wT_ready.sem, 1)

            def probabilities(a, b, n):
                act.wait_ge(*sT_done.after(a, b, n))
                if n >= RING:
                    act.wait_ge(*pv_done.after(a, b, n - RING))
                A.activation(pT[:, n % RING, :], PSQ[(b * H + n) % 3][0:M, :], ACT.Exp,
                             **(dict(bias=padT[:, b:b + 1]) if a == 0 else {})).then_inc(pT_ready.sem, 1)

            def inverse_sums(a, b):
                if a == 2:
                    act.wait_ge(*tot_ready.after(b))
                    link(A.activation(den_r, uT[:, 1, :], ACT.Ln))
                else:
                    act.wait_ge(*pv_done.after(a, b, H - 1))
                    if b:
                        act.wait_ge(*o_norm.after(a, 0))
                    A.activation(den_r[0:64, :], PSQ[4][64:128, :], ACT.Ln)
                    link(A.activation(den_r[64:128, :], PSQ[5][0:64, :], ACT.Ln))
                A.activation(den_r, den_r, ACT.Exp, scale=-1.0).then_inc(den_ready.sem, 1)

            def weights3_rounded(i):
                A.activation(f3_hi[:, 2048 * i:2048 * (i + 1)], f3w[:, 2048 * i:2048 * (i + 1)], ACT.Copy
                             ).then_inc(weights3_hi.sem, 1)

            def attention(a):
                s = 2 * a + 2
                queries(a, 0)
                queries_spread(a, 0, 0)
                queries_spread(a, 0, 1)
                if a == 1:
                    act.wait_ge(in_big, 16)
                    act.wait_ge(*dn1_done.after(B - 1, 15))
                    weights3_rounded(0)
                norm_square(s, 1)
                norm_rstd(s, 1)
                if a == 1:
                    for i in range(1, 4):
                        weights3_rounded(i)
                shift_rows(a, 0)
                for n in range(H):
                    probabilities(a, 0, n)
                    if n == (2 if a == 2 else 1):
                        queries(a, 1)
                    if n in (4, 5):
                        queries_spread(a, 1, n - 4)
                if a == 2:
                    inverse_sums(a, 0)
                shift_rows(a, 1)
                if a != 2:
                    inverse_sums(a, 0)
                for n in range(H):
                    probabilities(a, 1, n)
                    if n == 7:
                        norm_square(s + 1, 0)
                norm_rstd(s + 1, 0)
                inverse_sums(a, 1)

            def router(r, b):
                ne = GATES[r][0]
                act.wait_ge(*lg_shift.after(r, b))
                tile = lgt(r, b)
                A.activation(tile[:, 1, :, 0:ne], tile[:, 0, :, 0:ne], ACT.Exp).then_inc(lg_exp.sem, 1)

            def spread_gate(r, b, e):
                act.wait_ge(*gb_done.after(r - 1, b, e))
                A.activation(gbc[:, e, :], PSQ[6], ACT.Copy).then_inc(gbc_ready.sem, 1)

            def ffn0(b):
                if b == 0:
                    router(0, 0)
                    norm_square(1, 1)
                    norm_rstd(1, 1)
                    router(0, 1)
                for j in range(9):
                    if j == 2:
                        kv_prepare(0, b)
                    act.wait_ge(*up0_done.after(b, j))
                    if j >= 5:
                        act.wait_ge(*hg_ready.after(b, j - 5))
                    dst = hid[:, 0, :] if j == 0 else big_gelu(j)
                    A.activation(dst, PSQ[j % 2], ACT.Gelu).then_inc(gelu0.sem, 1)
                    if b and j == 5:
                        norm_square(2, 0)
                    if b and j in (4, 6, 8):
                        i = j // 2 - 2
                        act.wait_ge(in_f1, 16)
                        A.activation(f1_hi[:, 2048 * i:2048 * (i + 1)], f1_sb[:, 8 + 2048 * i:8 + 2048 * (i + 1)],
                                     ACT.Copy).then_inc(weights1_hi.sem, 1)
                if b:
                    norm_rstd(2, 0, tables=True)

            def ffn1(b):
                router(1, b)
                kv_prepare(1, b)
                for n in range(16):
                    act.wait_ge(*up1_done.after(b, n))
                    if n >= 3:
                        act.wait_ge(*hh_ready.after(b, n - 3))
                    A.activation(hid[:, n % 3, :], PSQ[n % 2], ACT.Silu).then_inc(silu1.sem, 1)
                    if 3 <= n < 11:
                        spread_gate(1, b, n - 3)
                    if n == 6:
                        norm_square(*next_ln(3, b))
                norm_rstd(*next_ln(3, b), tables=True)

            def ffn2():
                def scaled(b):
                    for j in range(4):
                        act.wait_ge(*up2_done.after(b, j))
                        if (b, j) == (0, 0):
                            act.wait_ge(*b2_ready.after(0))
                        A.activation(hq(b, j), PSQ[j], ACT.Identity, bias=b1x[:, j:j + 1], scale=256.0
                                     ).then_inc(h256.sem, 1)

                scaled(0)
                kv_prepare(2, 0)
                norm_square(5, 1)
                norm_rstd(5, 1)
                for m in range(8):
                    b, j = m // 4, m % 4
                    act.wait_ge(*q2_ready.after(b, j))
                    if m >= 2:
                        act.wait_ge(*dy_ready.after((m - 2) // 4, (m - 2) % 4))
                    A.activation(y01(j, 0), qlow(j), ACT.Gelu, scale=0.25)
                    A.activation(y01(j, 1), qlow(j), ACT.Gelu, scale=0.25, bias=refl[:, 6:7]).then_inc(gelu2.sem, 1)
                    if m == 2:
                        scaled(1)
                    if m == 4:
                        kv_prepare(2, 1)
                    if m == 6:
                        norm_square(6, 0)
                norm_rstd(6, 0, tables=True)

            def ffn3(b):
                router(2, b)
                for n in range(32):
                    act.wait_ge(*up3_done.after(b, n))
                    if n >= 4:
                        act.wait_ge(*dn3_done.after(b, n - 4))
                    A.activation(hid2[:, n % 4, :], PSQ[n % 4], ACT.Relu, bias=F3("b1")[:, n:n + 1]
                                 ).then_inc(relu3.sem, 1)
                    if 6 <= n < 14:
                        spread_gate(2, b, n - 6)
                    if n == 17 and b == 0:
                        norm_square(7, 1)
                    if n == 21 and b == 0:
                        norm_rstd(7, 1)

            act.wait_ge(in_first, 64)
            act.wait_ge(*consts_ready.after(0))
            A.activation(tg[:, :], g_raw[:, :], ACT.Tanh).then_inc(gates_tanh.sem, 1)
            exp_and_log()
            norm_square(0, 0)
            norm_rstd(0, 0)
            l0_front(0)
            l0_front(1)
            l0_gather(0)
            l0_gather(1)
            l0_softmax(1)
            act.wait_ge(in_f0, 16)
            A.activation(f0_hi[:, :], f0_sb[:, 16:16 + 2304], ACT.Copy).then_inc(weights0_hi.sem, 1)
            norm_square(1, 0)
            norm_rstd(1, 0)
            for a, ffn in ((0, ffn0), (1, ffn1)):
                ffn(0)
                ffn(1)
                attention(a)
            ffn2()
            attention(2)
            ffn3(0)
            ffn3(1)

        @block.gpsimd
        def _(pool):
            def link(ins):
                steps["pool"] += 1
                ins.then_inc(pool_step, 1)
                pool.wait_ge(pool_step, steps["pool"])

            P.memset(mean_w[:, :], 1.0 / D)
            P.memset(ones_bf[:, :], 1.0)
            P.memset(ones_row[:, :], 1.0)
            P.memset(eps_col[:, :], EPS)
            P.memset(gst[:, :], 0.0)
            P.memset(ap_[:, :, :], 0.0)
            P.memset(refl[:, 6:7], 0.25)
            P.memset(refl[:, 7:8], -1e-9)
            P.iota(loc[:, :], [[1, T]], base=0, channel_multiplier=0, allow_small_or_imprecise_dtypes=True
                   ).then_inc(consts_ready.sem, 1)
            for b in range(B):
                for part in range(2):
                    last = P.memset(tab[b][part], 0.0)
            last.then_inc(tab_zeroed.sem, 1)
            pool.wait_ge(in_first, 64)
            for g in range(G):
                last = P.tensor_copy(sel_rows[:, g, :, :].rearrange("p k (h c) -> p k h c", h=HG),
                                     C("ident")[:, 32 * g:32 * g + HG * NK].rearrange("p (h k) -> p k h", h=HG)
                                     .unsqueeze(3).broadcast_to([128, NK, HG, 32]))
            last.then_inc(rows_ready.sem, 1)

            def rest(out, src, sem):
                P.tensor_tensor(out, src, high(src), ALU.subtract).then_inc(sem, 1)

            for b in range(B):
                for u in range(U):
                    pool.wait_ge(*gw_ready.after(b, u))
                    pool.wait_ge(*qrep_ready.after(b, u // NK))
                    n = b * U + u
                    if n >= 3:
                        pool.wait_ge(*score_done.after((n - 3) // U, (n - 3) % U))
                    P.tensor_tensor(tq[:, u % 3, :], GW[:, b, u, :], qrep[:, b, u // NK, :], ALU.mult
                                    ).then_inc(tq_ready.sem, 1)
                    pool.wait_ge(*tq_ready.after(b, u))
                    rest(tq_lo[u % 3], tq[:, u % 3, :], tq_rest.sem)
            for b in range(B):
                for g in range(G):
                    u = g * NK
                    pool.wait_ge(*t2_ready.after(b, u + 1))
                    link(P.tensor_tensor(GW[:, b, u, :], GW[:, b, u, :], GW[:, b, u + 1, :], ALU.add))
                    pool.wait_ge(*t2_ready.after(b, u + 2))
                    link(P.tensor_tensor(GW[:, b, u, :], GW[:, b, u, :], GW[:, b, u + 2, :], ALU.add))
                    pool.wait_ge(*t2_pair.after(b, g))
                    P.tensor_tensor(GW[:, b, u, :], GW[:, b, u, :], GW[:, b, u + 3, :], ALU.add
                                    ).then_inc(t2_sum.sem, 1)
                if b == 0:
                    pool.wait_ge(*weights0_hi.after(0))
                    w = f0_sb[:, 16:16 + 2304]
                    P.tensor_tensor(w, w, f0_hi[:, :], ALU.subtract).then_inc(weights0_lo.sem, 1)
            pool.wait_ge(*out_read.after(0, B - 1))
            P.memset(am_st, 0.0)
            P.memset(v_lo, 0.0)
            link(P.memset(v_hi, 0.0))
            for b in range(B):
                vb = v_hi[:, b, :].rearrange("m (h c) -> m h c", c=136)
                P.memset(vb[:, 0:8, 64:72], 1.0)
                last = P.memset(vb[:, 7:15, 72:80], 1.0)
            last.then_inc(zeroed.sem, 1)

            for b in range(B):
                if b:
                    pool.wait_ge(in_masks, 64)
                    pool.wait_ge(*pad_ready.after(0))
                    for bb in range(B):
                        last = P.tensor_tensor(amp[:, bb, :, :], am_sb[:, :, :], pad_row[:, bb * M:(bb + 1) * M]
                                               .unsqueeze(1).broadcast_to([128, NT, M]), ALU.add)
                    link(last)
                    rest(amp_lo.rearrange("p b t m -> p (b t m)"), amp.rearrange("p b t m -> p (b t m)"),
                         amp_ready.sem)
                for j in range(1, 9, 2):
                    pool.wait_ge(*hg_ready.after(b, j - 1))
                    if j >= 5:
                        pool.wait_ge(*dn0_done.after(b, j - 4))
                    rest(h_lo[:, j % 4, :], hid2[:, j % 4, :], lo0_p.sem)

            def probabilities(a, b):
                for n in range(H):
                    if on_pool(n):
                        pool.wait_ge(*pT_ready.after(a, b, n))
                        if n >= RING:
                            pool.wait_ge(*pv_done.after(a, b, n - RING))
                        rest(p_lo[:, n % RING, :], pT[:, n % RING, :], p_lo_p.sem)
                    if a == 1 and n in (1, 6, 9, 14):
                        i = 4 * b + (1, 6, 9, 14).index(n)
                        pool.wait_ge(*weights3_hi.after(i // 2))
                        w = f3w[:, 1024 * i:1024 * (i + 1)]
                        P.tensor_tensor(w, w, f3_hi[:, 1024 * i:1024 * (i + 1)], ALU.subtract
                                        ).then_inc(weights3_lo.sem, 1)

            def accumulate(r, b, e):
                pool.wait_ge(*yg_ready.after(r, b, e))
                if e == 0:
                    if b:
                        pool.wait_ge(*residual.after(3 + 4 * r, b - 1))
                    P.tensor_copy(acc, yg[:, e % 2, :]).then_inc(acc_ready.sem, 1)
                else:
                    pool.wait_ge(*acc_ready.after(r, b, e - 1))
                    P.tensor_tensor(acc, acc, yg[:, e % 2, :], ALU.add).then_inc(acc_ready.sem, 1)

            for i in range(3):
                pool.wait_ge(*weights1_hi.after(i))
                w = f1_sb[:, 8 + 2048 * i:8 + 2048 * (i + 1)]
                P.tensor_tensor(w, w, f1_hi[:, 2048 * i:2048 * (i + 1)], ALU.subtract).then_inc(weights1_lo.sem, 1)
            pool.wait_ge(*out_read.after(1, B - 1))
            P.memset(ikT_st, 1.0).then_inc(ik_filled.sem, 1)
            for b in range(B):
                probabilities(0, b)
            for b in range(B):
                for n in range(1, 16, 2):
                    pool.wait_ge(*hh_ready.after(b, n))
                    if n >= 4:
                        pool.wait_ge(*dn1_done.after(b, n - 4))
                    rest(h_lo[:, n % 4, :], hid2[:, n % 4, :], lo1_p.sem)
                    if n >= 5:
                        accumulate(0, b, (n - 5) // 2)
                accumulate(0, b, 6)
                accumulate(0, b, 7)
            for b in range(B):
                probabilities(1, b)
            for m in range(8):
                b, j = m // 4, m % 4
                pool.wait_ge(*gelu2.after(b, j))
                if m >= 2:
                    pool.wait_ge(*h2_ready.after((m - 2) // 4, (m - 2) % 4))
                pool.wait_ge(*q2_ready.after(b, j))
                d = between(j)
                link(P.tensor_tensor(d, y01(j, 1), y01(j, 0), ALU.subtract))
                link(P.tensor_tensor(d, d, qt(j), ALU.mult))
                P.tensor_tensor(d, d, y01(j, 0), ALU.add).then_inc(dy_ready.sem, 1)
            for b in range(B):
                probabilities(2, b)
            for b in range(B):
                for e in range(8):
                    accumulate(1, b, e)

        @block.vector
        def _(dve):
            def link(ins):
                steps["dve"] += 1
                ins.then_inc(dve_step, 1)
                dve.wait_ge(dve_step, steps["dve"])

            def rest(out, src, sem=None):
                ins = V.tensor_tensor(out, src, high(src), ALU.subtract)
                if sem is not None:
                    ins.then_inc(sem, 1)
                return ins

            def norm_center(s, b):
                dve.wait_ge(*ln_mean.after(s, b))
                V.tensor_tensor(xc[:, b, :], x[:, b, :], PSQ[7], ALU.subtract).then_inc(ln_centered.sem, 1)

            def norm_scale(s, b):
                dve.wait_ge(*ln_rstd.after(s, b))
                dve.wait_ge(*ln_centered.after(s, b))
                link(V.tensor_tensor(xn[:, b, :], xc[:, b, :], rstd[:, :], ALU.mult))
                rest(xn_lo[:, b, :], xn[:, b, :], xn_ready.sem)

            def add_branch(s, b, bias, relu=False):
                dve.wait_ge(*out_done.after(s - (s > 3), b))
                V.tensor_scalar(y_tmp[:, :], PSQ[6], bias, 0.0 if relu else None, ALU.add,
                                *((ALU.max,) if relu else ())).then_inc(out_read.sem, 1)
                dve.wait_ge(*out_read.after(s, b))
                V.scalar_tensor_tensor(x[:, b, :], y_tmp[:, :], tg[:, s:s + 1], x[:, b, :], ALU.mult, ALU.add
                                       ).then_inc(residual.sem, 1)

            def constants():
                dve.wait_ge(in_first, 64)
                dve.wait_ge(*consts_ready.after(0))
                V.tensor_copy(ident_bf[:, :], C("ident"))
                V.tensor_scalar(neg_ident[:, :], C("ident"), NEG, None, ALU.mult)
                V.tensor_copy(tri_bf[:, :], C("tri"))
                V.tensor_copy(hm_bf[:, :], C("headmask"))
                V.tensor_copy(selS_bf[:, :], C("selS"))
                V.tensor_copy(selH[:, :, :], C("id16")[0:32, :].unsqueeze(2).broadcast_to([32, H, 8]))
                link(V.tensor_copy(mcnt[:, :], mif_sb[:, :]))
                link(V.tensor_reduce(Lb[:, :, 0], mcnt[:, :].rearrange("p (b m) -> p b m", b=2), AX.X, ALU.add))
                link(V.tensor_scalar(Lb[:, :, 1], Lb[:, :, 0], -1.0, float(M - 1), ALU.mult, ALU.add))
                link(V.tensor_scalar(Lb[:, :, 2], Lb[:, :, 1], -1.0, None, ALU.mult))
                link(V.tensor_tensor(Lb[:, :, 3], Lb[:, :, 1], Lb[:, :, 2], ALU.max))
                link(V.tensor_scalar(Lb[:, :, 4], Lb[:, :, 1], 0.0, None, ALU.is_ge))
                link(V.tensor_scalar(Lb[:, :, 4], Lb[:, :, 4], 2.0, -1.0, ALU.mult, ALU.add))
                link(V.reciprocal(Lb[:, :, 5], Lb[:, :, 3]))
                link(V.tensor_scalar(Lb[:, :, 6], Lb[:, :, 3], -1.0, None, ALU.mult))
                link(V.tensor_scalar(Lb[:, :, 7], Lb[:, :, 4], M / (M - 1.0), None, ALU.mult))
                dve.wait_ge(in_l0, 16)
                V.tensor_scalar(bq_s[:, :], L0("bqrep"), 0.5 / HD ** 0.5, None, ALU.mult).then_inc(dve_consts.sem, 1)

            def l0_table(b):
                dve.wait_ge(*tab_done.after(b))
                src = PSQ[0][0:MO, :].rearrange("m (s h c) -> m s h c", s=2, h=H)
                src = src.rearrange("m s (g h) c -> m s g h c", g=G)

                def block(part, s, h):
                    return tab[b][part].rearrange("m (g h c) -> m g h c", g=G, h=HG)[
                        :, :, h, 32 * h + 16 * s:32 * h + 16 * s + 16]

                spots = [(s, h) for s in range(2) for h in range(HG)]
                if b == 0:
                    dve.wait_ge(*tab_zeroed.after(0))
                for s, h in spots:
                    last = V.tensor_copy(block(0, s, h), src[:, s, :, h, :])
                link(last)
                for s, h in spots:
                    last = V.tensor_tensor(block(1, s, h), src[:, s, :, h, :], block(0, s, h), ALU.subtract)
                last.then_inc(tab_ready.sem, 1)
            def positions(b, part):
                L = Lb[:, b, :]
                if part == 0:
                    dve.wait_ge(*off_done.after(b))
                    V.tensor_scalar(ixt, PSQ[2], L0("boff"), C("refk"), ALU.add, ALU.add).then_inc(off_read.sem, 1)
                elif part == 1:
                    dve.wait_ge(*off_read.after(b))
                    link(V.tensor_tensor(ixt, ixt, loc[:, :], ALU.add))
                    link(V.tensor_scalar(ix1, ixt, L[:, 4:5], None, ALU.mult))
                elif part == 2:
                    link(V.tensor_scalar(ix2, ix1, L[:, 5:6], MAGIC, ALU.mult, ALU.add))
                    link(V.tensor_scalar(ix2, ix2, -MAGIC, L[:, 6:7], ALU.add, ALU.mult))
                elif part == 3:
                    link(V.tensor_tensor(ix1, ix1, ix2, ALU.add))
                    link(V.tensor_scalar(ix2, ix1, 0.0, L[:, 3:4], ALU.is_lt, ALU.mult))
                elif part == 4:
                    link(V.tensor_tensor(ix1, ix1, ix2, ALU.add))
                    link(V.tensor_scalar(ix1, ix1, L[:, 7:8], -0.5, ALU.mult, ALU.add))
                elif part == 5:
                    link(V.tensor_scalar(ix2, ix1, MAGIC, -MAGIC, ALU.add, ALU.add))
                    link(V.tensor_tensor(ixt, ix2, ix1, ALU.is_gt))
                elif part == 6:
                    link(V.tensor_tensor(ix2, ix2, ixt, ALU.subtract))
                    link(V.tensor_tensor(ix1, ix1, ix2, ALU.subtract))
                else:
                    V.tensor_scalar(i0bf[:, b, :], ix2, -2.0, float(M), ALU.max, ALU.min)
                    link(V.tensor_copy(w1hi[:, b, :], ix1))
                    V.tensor_tensor(w1lo[:, b, :], ix1, w1hi[:, b, :], ALU.subtract).then_inc(ix_ready.sem, 1)

            def l0_gather(b):
                def one_hots(u):
                    g, k = u // NK, u % NK
                    for p in range(2):
                        n = b * U + u
                        if n >= 2:
                            dve.wait_ge(*gather_done.after((n - 2) // U, (n - 2) % U))
                        if k < NK - 1:
                            dve.wait_ge(*ib_ready.after(b, g, k, p))
                            src = ib[:, p, :]
                        else:
                            dve.wait_ge(*bc_done.after(b, u, p))
                            src = ps[0:MO, 2 * p:2 * p + 2, :].rearrange("m a t -> m (a t)")
                        V.tensor_scalar(oh[:, u % 2, p, :], src, C("pos")[0:MO, :], None, ALU.is_equal
                                        ).then_inc(oh_ready.sem, 1)

                def weigh(u):
                    dve.wait_ge(*gather_done.after(b, u))
                    dve.wait_ge(*wf_ready.after(b, u))
                    V.tensor_tensor(GW[:, b, u, :], PSQ[(4, 7)[u % 2]], at_wf[:, u % 2, :], ALU.mult).then_inc(gw_ready.sem, 1)

                one_hots(0)
                for u in range(U):
                    if u + 1 < U:
                        one_hots(u + 1)
                    weigh(u)
                    if b and u == 0:
                        l0_shift(0)
                    if b and u == 3:
                        l0_softmax(0)
                    if b == 0 and 1 <= u <= 7:
                        positions(1, u)

            def l0_shift(b):
                dve.wait_ge(*score_done.after(b, U - 1))
                sc = PSQ[6][:, 0:NT * H * NK].rearrange("p (n k) -> p n k", k=NK)
                s3 = s80.rearrange("p (n k) -> p n k", k=NK)
                link(V.tensor_reduce(s64[:, 0, :], sc, AX.X, ALU.max, negate=True))
                V.tensor_tensor(s3, sc, s64[:, 0, :].unsqueeze(2).broadcast_to([128, NT * H, NK]), ALU.add
                                ).then_inc(s_shifted.sem, 1)

            def l0_softmax(b):
                dve.wait_ge(*s_exp.after(b))
                e3 = e80.rearrange("p (n k) -> p n k", k=NK)
                link(V.tensor_reduce(s64[:, 1, :], e3, AX.X, ALU.add))
                link(V.reciprocal(s64[:, 2, :], s64[:, 1, :]))
                link(V.tensor_scalar(s64[:, 2, :], s64[:, 2, :], 0.5, None, ALU.mult))
                if b:
                    dve.wait_ge(*aT_done.after(b - 1))
                for t in range(NT):
                    for g in range(G):
                        n = t * H + g * HG
                        last = V.tensor_tensor(ap_[:, t, 32 * g:32 * g + 20].rearrange("p (h k) -> p h k", k=NK),
                                               e3[:, n:n + HG, :],
                                               s64[:, 2, n:n + HG].unsqueeze(2).broadcast_to([128, HG, NK]), ALU.mult)
                last.then_inc(a_ready.sem, 1)

            def l0_back(b):
                dve.wait_ge(*aT_done.after(b))
                link(V.tensor_copy(ahi, PSQ[0]))
                V.tensor_tensor(alo, PSQ[0], ahi, ALU.subtract).then_inc(aT_ready.sem, 1)
                for u in range(U):
                    dve.wait_ge(*ab_done.after(b, u))
                    V.tensor_tensor(GW[:, b, u, :], GW[:, b, u, :], PSQ[1 + u % 5], ALU.mult
                                    ).then_inc(t2_ready.sem, 1)
                    if u % NK == NK - 1:
                        dve.wait_ge(*t2_ready.after(b, u))
                        V.tensor_tensor(GW[:, b, u - 1, :], GW[:, b, u - 1, :], GW[:, b, u, :], ALU.add
                                        ).then_inc(t2_pair.sem, 1)
                    if b == 1 and u == 9:
                        norm_center(1, 0)
                    if b == 1 and u == 17:
                        norm_scale(1, 0)
                add_branch(0, b, L0("bo"))

            def kv_rest(a, b):
                dve.wait_ge(*kf_ready.after(a, b))
                rest(kl, kf, kl_ready.sem)
                dve.wait_ge(*v_ready.after(a, b))
                if (a, b) == (0, 0):
                    dve.wait_ge(*zeroed.after(0))
                if a == 2:
                    rest(vf_lo[:, b, :], vf[:, b, :])
                v1, v2 = (v[:, b, :].rearrange("m (h c) -> m h c", c=136)[:, :, 0:8] for v in (v_hi, v_lo))
                src = vf[:, b, :].rearrange("m (h d) -> m h d", h=H)
                link(V.tensor_copy(v1, src))
                V.tensor_tensor(v2, src, v1, ALU.subtract)

            def kv_tables(a, b):
                dve.wait_ge(*ks_done.after(a, b))
                V.tensor_tensor(kt[:, b, :, :].rearrange("p (g h) m -> p g h m", g=G),
                                PSQ[5][:, 0:G * M].rearrange("p (g m) -> p g m", g=G).unsqueeze(2)
                                .broadcast_to([128, G, HG, M]),
                                hm_bf[:, :].unsqueeze(1).unsqueeze(3).broadcast_to([128, G, HG, M]), ALU.mult
                                ).then_inc(kb_ready.sem, 1)

            def pads():
                dve.wait_ge(in_masks, 64)
                V.tensor_scalar(pad_row[:, :], mb8[:, :], NEG, None, ALU.mult)
                V.tensor_scalar(padT[:, :], mb8T[:, :], NEG, None, ALU.mult)
                link(V.tensor_copy(shift_hi, high(am_st)))
                V.tensor_tensor(shift_lo, am_st, shift_hi, ALU.subtract).then_inc(pad_ready.sem, 1)

            def selectors():
                V.tensor_copy(sel0[:, :, :], C("id32")[0:96, 0:16].unsqueeze(2).broadcast_to([96, 16, 64]))
                V.tensor_copy(sel1[:, :, :], C("id32")[0:96, 0:8].unsqueeze(2).broadcast_to([96, 8, 128]))

                one = C("ident").rearrange("p (h d) -> p h d", d=HD).unsqueeze(2).broadcast_to([128, H, 2, HD])
                for dst, slots in ((sel_qh, slice(0, 4, 2)), (sel_ql, slice(1, 4, 2)), (sel_kh, slice(0, 2)),
                                   (sel_kl, slice(2, 4))):
                    link(V.memset(dst, 0.0))
                    last = V.tensor_copy(dst.rearrange("p (h s d) -> p h s d", h=H, s=4)[:, :, slots, :], one)
                last.then_inc(sel_ready.sem, 1)

            def ffn2_scales():
                dve.wait_ge(in_f2, 16)
                link(V.tensor_scalar(b2x[:, 0:1], F2("b2"), 256.0, None, ALU.mult))
                link(V.tensor_scalar(b2x[:, 1:2], tg[:, 5:6], 1.0 / 256, None, ALU.mult))
                V.tensor_scalar(b1x[:, :], F2("b1"), 256.0, None, ALU.mult).then_inc(b2_ready.sem, 1)

            def masks():
                dve.wait_ge(in_att, 16)
                for a in range(ATT):
                    V.tensor_scalar(bqs[:, a:a + 1], AW[a]("bq"), HD ** -0.5, None, ALU.mult)
                V.tensor_tensor(sel_shift,
                                C("id16").unsqueeze(2).broadcast_to([128, H, M]),
                                C("keys").unsqueeze(1).broadcast_to([128, H, M]), ALU.add).then_inc(bqs_ready.sem, 1)

            def overwritten_keys():
                dve.wait_ge(in_ik, 48)
                V.tensor_scalar(z[:, :, :], ik_sb[:, :, :], 0.0, None, ALU.is_equal)
                link(V.tensor_scalar(zT, ikT_sb[0:M], 0.0, None, ALU.is_equal))
                V.tensor_scalar(shift_hi, ikT_st.bitcast(i32), 0.0, NEG, ALU.is_equal, ALU.mult)
                link(V.tensor_reduce(zany[:, 0, :], z[:, :, :], AX.X, ALU.max))
                link(V.tensor_scalar(zany[:, 1, :], zany[:, 0, :], NEG, -NEG, ALU.mult, ALU.add))
                V.tensor_scalar(zany[:, 2, :], zany[:, 1, :], 1e-9, None, ALU.max).then_inc(z_ready.sem, 1)

            def queries_spread(a, b, i):
                dve.wait_ge(*qs_done.after(a, b, 2 * i + 1))
                if (a, b, i) == (0, 1, 0):
                    dve.wait_ge(*amp_ready.after(0))
                V.tensor_copy(qs[b][:, 2 * i + 1, :], PSQ[6]).then_inc(qs_dve.sem, 1)

            def maxima(a, b, u):
                t, g = u // G, u % G
                dve.wait_ge(*st_done.after(a, b, u))
                V.tensor_reduce(nmx[:, b, t, HG * g:HG * g + HG],
                                score_bank(b, u)[:, 0:HG * M].rearrange("p (h m) -> p h m", h=HG),
                                AX.X, ALU.max, negate=True).then_inc(st_read.sem, 1)

            def maxima_parts(a, b):
                dve.wait_ge(*st_read.after(a, b, NT * G - 1))
                top = nmx[:, b, :, :]
                if a == 2:
                    V.tensor_tensor(top, top, zany[:, 2, :].unsqueeze(2).broadcast_to([128, NT, H]), ALU.min
                                    ).then_inc(w0_shift.sem, 1)
                    dve.wait_ge(*w0_shift.after(b))
                left = s64[:, 0, :].rearrange("p (t h) -> p t h", t=NT)
                parts = nst[:, b, :, :, :]
                link(V.tensor_copy(parts[:, :, 0, :], top))
                link(V.tensor_tensor(left, top, parts[:, :, 0, :], ALU.subtract))
                link(V.tensor_copy(parts[:, :, 1, :], left))
                V.tensor_tensor(parts[:, :, 2, :], left, parts[:, :, 1, :], ALU.subtract).then_inc(nst_ready.sem, 1)

            def overwritten_weights(b):
                dve.wait_ge(*w0_ready.after(b))
                link(V.tensor_copy(wst[:, :, 0, :], w0z[:, :, :]))
                V.tensor_tensor(wst[:, :, 1, :], w0z[:, :, :], wst[:, :, 0, :], ALU.subtract
                                ).then_inc(wst_ready.sem, 1)

            def weigh_overwritten(b):
                dve.wait_ge(*wb_done.after(b))
                dve.wait_ge(*u_read.after(b))
                for i in range(2):
                    last = V.tensor_tensor(uT[:, i, :], uT[:, i, :], PSQ[3], ALU.mult)
                last.then_inc(uw_ready.sem, 1)

            def probability_rest(a, b, n):
                if not on_pool(n):
                    dve.wait_ge(*pT_ready.after(a, b, n))
                    if n >= RING:
                        dve.wait_ge(*pv_done.after(a, b, n - RING))
                    rest(p_lo[:, n % RING, :], pT[:, n % RING, :], p_lo_v.sem)

            def normalise(a, b):
                dve.wait_ge(*pv_done.after(a, b, H - 1))
                halves = ((slice(0, 64), slice(64, 128), 4), (slice(64, 128), slice(0, 64), 5))
                if a == 2:
                    dve.wait_ge(*uw_ready.after(b))
                    for rows, sums, bank in halves:
                        V.tensor_tensor(uT[rows, 0, :], uT[rows, 0, :], PSQ[bank][rows, :], ALU.add)
                        last = V.tensor_tensor(uT[rows, 1, :], uT[rows, 1, :], PSQ[bank][sums, :], ALU.add)
                    last.then_inc(tot_ready.sem, 1)
                    dve.wait_ge(*tot_ready.after(b))
                dve.wait_ge(*den_ready.after(a, b))
                if a == 2:
                    V.tensor_tensor(oT, uT[:, 0, :], den_r, ALU.mult).then_inc(o_norm.sem, 1)
                else:
                    for rows, _, bank in halves:
                        last = V.tensor_tensor(oT[rows, :], PSQ[bank][rows, :], den_r[rows, :], ALU.mult)
                    last.then_inc(o_norm.sem, 1)

            def attention(a):
                s = 2 * a + 2
                dve.wait_ge(*qf_ready.after(a, 0))
                rest(q_lo, qf, qst_ready.sem)
                norm_center(s, 1)
                queries_spread(a, 0, 0)
                queries_spread(a, 0, 1)
                for u in range(NT * G):
                    maxima(a, 0, u)
                maxima_parts(a, 0)
                if a == 2:
                    overwritten_weights(0)
                norm_scale(s, 1)
                for n in range(H):
                    probability_rest(a, 0, n)
                    if a == 2 and n == 0:
                        weigh_overwritten(0)
                    if n == 2:
                        dve.wait_ge(*qf_ready.after(a, 1))
                        rest(q_lo, qf, qst_ready.sem)
                    if n in (4, 5):
                        queries_spread(a, 1, n - 4)
                    if 6 <= n < 14:
                        maxima(a, 1, 2 * n - 12)
                        maxima(a, 1, 2 * n - 11)
                maxima_parts(a, 1)
                normalise(a, 0)
                add_branch(s, 0, AW[a]("bo"), relu=a == 1)
                if a == 2:
                    overwritten_weights(1)
                for n in range(H):
                    probability_rest(a, 1, n)
                    if a == 2 and n == 0:
                        weigh_overwritten(1)
                    if n == 7:
                        norm_center(s + 1, 0)
                norm_scale(s + 1, 0)
                normalise(a, 1)
                add_branch(s, 1, AW[a]("bo"), relu=a == 1)

            def router(r, b, bank, parts=range(5)):
                ne, topk = GATES[r]
                sh, ex, p, rank, one = (lgt(r, b)[:, i, :, 0:ne] for i in range(5))
                cmp1 = big[:, 0:NT * ne * ne].rearrange("p (t e j) -> p t e j", t=NT, e=ne)
                cmp2 = big2[:, 0:NT * ne * ne].rearrange("p (t e j) -> p t e j", t=NT, e=ne)

                def tok(i):
                    return g4[:, i, :].unsqueeze(2).broadcast_to([128, NT, ne])

                if 0 in parts:
                    dve.wait_ge(*lg_done.after(r, b))
                    c0 = NT * ne if (r, b) == (0, 1) else 0
                    lp = PSQ[bank][:, c0:c0 + NT * ne].rearrange("p (t e) -> p t e", t=NT)
                    link(V.tensor_reduce(g4[:, 0, :], lp, AX.X, ALU.max, negate=True))
                    V.tensor_tensor(sh, lp, tok(0), ALU.add).then_inc(lg_shift.sem, 1)
                if 1 in parts:
                    dve.wait_ge(*lg_exp.after(r, b))
                    link(V.tensor_reduce(g4[:, 1, :], ex, AX.X, ALU.add))
                    link(V.reciprocal(g4[:, 2, :], g4[:, 1, :]))
                    link(V.tensor_tensor(p, ex, tok(2), ALU.mult))
                    pj = p.unsqueeze(2).broadcast_to([128, NT, ne, ne])
                    pe_ = p.unsqueeze(3).broadcast_to([128, NT, ne, ne])
                    V.tensor_tensor(cmp1, pj, pe_, ALU.is_gt)
                    link(V.tensor_tensor(cmp2, pj, pe_, ALU.is_equal))
                if 2 in parts:
                    tie = C("tie").rearrange("p (e j) -> p e j", e=16)[:, 0:ne, 0:ne]
                    link(V.tensor_tensor(cmp2, cmp2, tie.unsqueeze(1).broadcast_to([128, NT, ne, ne]), ALU.mult))
                if 3 in parts:
                    link(V.tensor_tensor(cmp1, cmp1, cmp2, ALU.add))
                if 4 not in parts:
                    return
                link(V.tensor_reduce(rank, cmp1, AX.X, ALU.add))
                ga = gates_of(r, b)[:, :, 0:ne]
                if r == 0:
                    V.scalar_tensor_tensor(ga, rank, float(topk), p, ALU.is_lt, ALU.mult).then_inc(gate_ready.sem, 1)
                elif r == 1:
                    link(V.scalar_tensor_tensor(one, rank, float(topk), p, ALU.is_lt, ALU.mult))
                    link(V.tensor_reduce(g4[:, 3, :], one, AX.X, ALU.add))
                    link(V.reciprocal(g4[:, 3, :], g4[:, 3, :]))
                    V.tensor_tensor(ga, one, tok(3), ALU.mult).then_inc(gate_ready.sem, 1)
                else:
                    V.tensor_scalar(oh12[:, b, :, 0, :], rank, 0.0, None, ALU.is_equal)
                    V.tensor_scalar(oh12[:, b, :, 1, :], rank, 1.0, None, ALU.is_equal).then_inc(oh12_ready.sem, 1)

            def capacity(b):
                dve.wait_ge(*cum_done.after(b))
                dve.wait_ge(*oh12_ready.after(b))
                one, p = lg[:, 4, :, 0:8], lg[:, 2, :, 0:8]
                link(V.scalar_tensor_tensor(k12[:, :, :, :].rearrange("p t c e -> p (t c e)"),
                                            PSQ[6][:, 0:NT * 16], float(CAP),
                                            oh12[:, b, :, :, :].rearrange("p t c e -> p (t c e)"),
                                            ALU.is_le, ALU.mult))
                link(V.tensor_tensor(one, k12[:, :, 0, :], k12[:, :, 1, :], ALU.add))
                V.tensor_tensor(gate[:, :, 0:8], one, p, ALU.mult).then_inc(gate_ready.sem, 1)

            def gate_parts(r, b, bank):
                ne = GATES[r][0]
                dve.wait_ge(*gT_done.after(r, b))
                link(V.tensor_copy(gst[0:ne, :], PSQ[bank][0:ne, :]))
                link(V.tensor_tensor(gr1[0:ne, :], PSQ[bank][0:ne, :], gst[0:ne, :], ALU.subtract))
                link(V.tensor_copy(glo[0:ne, :], gr1[0:ne, :]))
                V.tensor_copy(gst[32:32 + ne, :], glo[0:ne, :])
                V.tensor_tensor(gst[64:64 + ne, :], gr1[0:ne, :], glo[0:ne, :], ALU.subtract
                                ).then_inc(gst_ready.sem, 1)

            def expert_out(r, b, e, done, bias):
                dve.wait_ge(*done)
                dve.wait_ge(*gbc_ready.after(r, b, e))
                if e >= 2:
                    dve.wait_ge(*acc_ready.after(r, b, e - 2))
                elif b:
                    dve.wait_ge(*acc_ready.after(r, b - 1, 6 + e))
                if bias is None:
                    ins = V.tensor_tensor(yg[:, e % 2, :], PSQ[4 + e % 2], gbc[:, e, :], ALU.mult)
                else:
                    ins = V.scalar_tensor_tensor(yg[:, e % 2, :], PSQ[4 + e % 2], bias, gbc[:, e, :], ALU.add, ALU.mult)
                ins.then_inc(yg_ready.sem, 1)

            def add_sum(r, s, b):
                dve.wait_ge(*acc_ready.after(r, b, 7))
                V.memset(zany[0:1, 0, 0:1], 0.0).then_inc(out_read.sem, 1)
                V.scalar_tensor_tensor(x[:, b, :], acc, tg[:, s:s + 1], x[:, b, :], ALU.mult, ALU.add
                                       ).then_inc(residual.sem, 1)

            def ffn0(b):
                if b == 0:
                    router(0, 0, 4, (0,))
                    norm_center(1, 1)
                    router(0, 0, 4, (1,))
                    norm_scale(1, 1)
                    router(0, 0, 4, (2,))
                    router(0, 1, 4, (0,))
                    router(0, 0, 4, (3, 4))
                gate_parts(0, b, 4)
                for j in range(9):
                    if j == 0:
                        dve.wait_ge(*gelu0.after(b, 0))
                        rest(h_lo[:, 0, :], hid[:, 0, :], lo0_v.sem)
                        if b == 0:
                            masks()
                        kv_rest(0, b)
                        if b == 0:
                            pads()
                            ffn2_scales()
                        continue
                    dve.wait_ge(*gelu0.after(b, j))
                    dve.wait_ge(*ga_done.after(b, j - 1))
                    if j >= 4:
                        dve.wait_ge(*dn0_done.after(b, j - 4))
                    V.tensor_tensor(hid2[:, j % 4, :], big_gelu(j), PSQ[2 + j % 2], ALU.mult).then_inc(hg_ready.sem, 1)
                    if j % 2 == 0:
                        dve.wait_ge(*hg_ready.after(b, j - 1))
                        rest(h_lo[:, j % 4, :], hid2[:, j % 4, :], lo0_v.sem)
                    if j == 1:
                        kv_tables(0, b)
                    if b == 0 and j in (2, 4, 6, 8):
                        router(0, 1, 4, (j // 2,))
                    if b and j == 5:
                        norm_center(2, 0)
                dve.wait_ge(*out_done.after(1, b))
                V.tensor_copy(y_tmp[:, :], PSQ[6]).then_inc(out_read.sem, 1)
                dve.wait_ge(*out_read.after(1, b))
                V.scalar_tensor_tensor(x[:, b, :], y_tmp[:, :], tg[:, 1:2], x[:, b, :], ALU.mult, ALU.add
                                       ).then_inc(residual.sem, 1)
                if b:
                    norm_scale(2, 0)

            def ffn1(b):
                router(1, b, 6)
                for n in range(16):
                    dve.wait_ge(*silu1.after(b, n))
                    if n >= 4:
                        dve.wait_ge(*dn1_done.after(b, n - 4))
                    V.tensor_tensor(hid2[:, n % 4, :], hid[:, n % 3, :], PSQ[2 + n % 2], ALU.mult
                                    ).then_inc(hh_ready.sem, 1)
                    if n % 2 == 0:
                        dve.wait_ge(*hh_ready.after(b, n))
                        rest(h_lo[:, n % 4, :], hid2[:, n % 4, :], lo1_v.sem)
                    if n == 0:
                        kv_rest(1, b)
                    if n == 1:
                        gate_parts(1, b, 6)
                    if n == 2:
                        kv_tables(1, b)
                    if n >= 5 and n % 2:
                        e = (n - 5) // 2
                        expert_out(0, b, e, dn1_done.after(b, 2 * e + 1), None)
                    if n == 6:
                        norm_center(*next_ln(3, b))
                expert_out(0, b, 6, dn1_done.after(b, 13), None)
                expert_out(0, b, 7, dn1_done.after(b, 15), None)
                norm_scale(*next_ln(3, b))
                add_sum(0, 3, b)

            def ffn2():
                def quantise(m):
                    b, j = m // 4, m % 4
                    dve.wait_ge(*h256.after(b, j))
                    if m:
                        dve.wait_ge(*q2_ready.after((m - 1) // 4, (m - 1) % 4))
                    n, t = hq(b, j), hid[:, 0, :]
                    link(V.tensor_scalar(n, n, MAGIC, -MAGIC, ALU.add, ALU.add))
                    link(V.tensor_scalar(t, n, -1024.0, 1024.0, ALU.max, ALU.min))
                    if m >= 2:
                        dve.wait_ge(*dy_ready.after((m - 2) // 4, (m - 2) % 4))
                    link(V.tensor_scalar(qt(j), t, 1.0 / 64, -63.0 / 128, ALU.mult, ALU.add))
                    link(V.tensor_scalar(qlow(j), qt(j), MAGIC, -MAGIC, ALU.add, ALU.add))
                    V.scalar_tensor_tensor(qt(j), t, 1.0 / 64, qlow(j), ALU.mult, ALU.subtract
                                           ).then_inc(q2_ready.sem, 1)

                def interpolate(m):
                    b, j = m // 4, m % 4
                    dve.wait_ge(*dy_ready.after(b, j))
                    d = between(j)
                    link(V.tensor_scalar(d, d, 256.0, MAGIC, ALU.mult, ALU.add))
                    link(V.tensor_scalar(hid[:, 2, :], hq(b, j), -1024.0, 0.0, ALU.add, ALU.max))
                    V.scalar_tensor_tensor(hq(b, j), d, -MAGIC, hid[:, 2, :], ALU.add, ALU.add
                                           ).then_inc(h2_ready.sem, 1)

                def finish(b):
                    dve.wait_ge(*out_done.after(4, b))
                    V.tensor_scalar(y_tmp[:, :], PSQ[6], b2x[:, 0:1], MAGIC, ALU.add, ALU.add).then_inc(out_read.sem, 1)
                    dve.wait_ge(*out_read.after(5, b))
                    link(V.tensor_scalar(y_tmp[:, :], y_tmp[:, :], -MAGIC, b2x[:, 1:2], ALU.add, ALU.mult))
                    V.tensor_tensor(x[:, b, :], y_tmp[:, :], x[:, b, :], ALU.add).then_inc(residual.sem, 1)

                quantise(0)
                norm_center(5, 1)
                kv_rest(2, 0)
                quantise(1)
                kv_tables(2, 0)
                norm_scale(5, 1)
                for m in range(8):
                    if m < 6:
                        quantise(m + 2)
                    interpolate(m)
                    if m == 3:
                        overwritten_keys()
                    if m == 4:
                        finish(0)
                    if m == 5:
                        kv_rest(2, 1)
                        norm_center(6, 0)
                    if m == 6:
                        kv_tables(2, 1)
                norm_scale(6, 0)
                finish(1)

            def ffn3(b):
                router(2, b, 6)
                for n in range(32):
                    dve.wait_ge(*relu3.after(b, n))
                    rest(h_lo[:, n % 4, :], hid2[:, n % 4, :], lo3.sem)
                    if n == 1:
                        capacity(b)
                    if n == 3:
                        gate_parts(2, b, 6)
                    if n >= 7 and n % 4 == 3:
                        e = n // 4 - 1
                        expert_out(1, b, e, dn3_done.after(b, 4 * e + 3), F3("b2")[:, e:e + 1])
                    if n == 16 and b == 0:
                        norm_center(7, 1)
                    if n == 23 and b == 0:
                        norm_scale(7, 1)
                expert_out(1, b, 7, dn3_done.after(b, 31), F3("b2")[:, 7:8])
                add_sum(1, 7, b)

            constants()
            dve.wait_ge(*gates_tanh.after(0))
            norm_center(0, 0)
            l0_table(0)
            norm_scale(0, 0)
            norm_center(0, 1)
            for part in range(3):
                positions(0, part)
            norm_scale(0, 1)
            for part in range(3, 8):
                positions(0, part)
            l0_table(1)
            positions(1, 0)
            l0_gather(0)
            l0_gather(1)
            l0_shift(1)
            l0_softmax(1)
            l0_back(0)
            l0_back(1)
            selectors()
            for a, ffn in ((0, ffn0), (1, ffn1)):
                ffn(0)
                ffn(1)
                attention(a)
            ffn2()
            attention(2)
            ffn3(0)
            ffn3(1)


def kernel(**inputs):
    import numpy as np
    import concourse.bacc as _bacc
    from concourse import mybir as _mybir
    from concourse.bass_utils import run_bass_kernel_spmd as _run

    I = {k: np.asarray(v) for k, v in inputs.items()}
    f4 = np.float32

    def rowsof(a, n=128):
        return a.reshape(-1, n, a.shape[-1]).transpose(1, 0, 2).reshape(n, -1)

    def pad(a, n=128):
        return np.concatenate([a, np.zeros((n - a.shape[0],) + a.shape[1:], a.dtype)]) if a.shape[0] < n else a

    def pack(widths, **parts):
        for k, w in widths.items():
            assert parts[k].shape[1] == w, (k, parts[k].shape, w)
        return np.concatenate([pad(parts[k]) for k in widths], axis=1)

    col = lambda v: v.reshape(-1, 1)
    p = np.arange(128)
    r = p % 32
    const = dict(
        ident=np.eye(128, dtype=f4), tri=(p[:, None] <= p[None, :]).astype(f4),
        id32=(r[:, None] == np.arange(32)).astype(f4), id16=(((p % 16)[:, None] == np.arange(16)) & (p < 48)[:, None]).astype(f4),
        keys=((p - 48)[:, None] == np.arange(M)).astype(f4),
        headmask=((p // 32)[:, None] == np.arange(4)).astype(f4),
        tie=np.tile((np.arange(16)[None, :] < np.arange(16)[:, None]).reshape(1, 256), (128, 1)).astype(f4),
        signW=col(np.where(r // 8 < 2, -1.0, 1.0)).astype(f4),
        patWb=col(np.where((p % 32) // 8 < 2, 1.0, 0.0)).astype(f4),
        refk=col(np.where(r < 20, r % NK - 3, 0)).astype(f4), pos=col(p - 1).astype(f4),
        selS=((((p % 32) // 8) % 2 == 0)[:, None] & ((p // 32)[:, None] == np.arange(4))).astype(f4))

    def grouped(w):
        return np.repeat(w.reshape(G, HG, 1, HD, -1), 4, axis=2).reshape(G * 128, -1)

    wq, wk, wv, wo = (I[f"L0_xattn_{n}"] for n in ("Wq", "Wk", "Wv", "Wo"))
    woff, boff = I["L0_xattn_Woff"], I["L0_xattn_boff"]
    woff_p = np.zeros((G, 32, D), f4)
    woff_p[:, :HG * NK] = woff.reshape(G, HG * NK, D)
    boff_p = np.zeros((G, 32), f4)
    boff_p[:, :HG * NK] = boff.reshape(G, HG * NK)
    kv = np.stack([wk.reshape(H, HD, D), wv.reshape(H, HD, D)], 1).reshape(2 * D, D)
    bkv = np.stack([I["L0_xattn_bk"].reshape(H, HD), I["L0_xattn_bv"].reshape(H, HD)], 1).reshape(1, 2 * D)
    worep = np.zeros((G, HG, 4, HD, D), f4)
    worep[:, :, 1] = wo.T.reshape(G, HG, HD, D)
    worep[:, :, 3] = wo.T.reshape(G, HG, HD, D)
    ctx = np.zeros((D, B, M + 2), f4)
    ctx[:, :, 1:M + 1] = I["ctx_1024"].transpose(2, 0, 1)
    l0 = pack(L0_W, wq=wq.T, wqrep=grouped(wq).T, woff=woff_p.reshape(128, D).T, wkv=kv.T,
              worep=rowsof(worep.reshape(G * 128, D)), ctx=ctx.reshape(D, -1), bq=col(I["L0_xattn_bq"]),
              bqrep=grouped(col(I["L0_xattn_bq"])).reshape(G, 128).T, boff=col(boff_p), bo=col(I["L0_xattn_bo"]))
    valid = np.ones((2, MO), f4)
    valid[0, 0] = 0
    valid[1, MO - 1] = 0
    rows = np.concatenate([bkv, valid.reshape(1, -1)] + [I[f"L{n}_xattn_bv"].reshape(1, -1) for n in (1, 2, 3)]
                          + [I["L3_ffn_gate_b"].reshape(1, -1)], axis=1)

    att = []
    for n in (1, 2, 3):
        w = {k: I[f"L{n}_xattn_W{k}"] for k in "qkvo"}
        if n != 2:
            w = {k: v.T for k, v in w.items()}
        att.append(pack(ATT_W, wq=w["q"], wk=w["k"], wv=w["v"], wo=w["o"],
                        **{f"b{k}": col(I[f"L{n}_xattn_b{k}"]) for k in "qko"}))
    att = np.concatenate(att, axis=1)

    up = np.concatenate([I["L0_ffn_shared_up"], I["L0_ffn_routed_up"]]).reshape(18 * 64, D)
    down = np.concatenate([I["L0_ffn_shared_down"], I["L0_ffn_routed_down"]]).transpose(0, 2, 1).reshape(18 * 64, D)
    f0 = pack(F0_W, rw=I["L0_ffn_router_w"].T, up=up.T, down=rowsof(down))
    f1 = pack(F1_W, rw=I["L1_ffn_wg"].T, w1=I["L1_ffn_w1"].reshape(-1, D).T, w3=I["L1_ffn_w3"].reshape(-1, D).T,
              w2=rowsof(I["L1_ffn_w2"].transpose(0, 2, 1).reshape(-1, D)))
    f2 = pack(F2_W, w1=I["L2_ffn_w1"], w2=rowsof(I["L2_ffn_w2"]), b1=I["L2_ffn_b1"].reshape(4, 128).T,
              b2=col(I["L2_ffn_b2"]))
    f3 = pack(F3_W, rw=I["L3_ffn_gate_w"].T, b1=I["L3_ffn_b1"].reshape(32, 128).T, b2=I["L3_ffn_b2"].T)
    f3big = pack(F3_BIG, w1=I["L3_ffn_W1"].transpose(1, 0, 2).reshape(D, -1), w2=rowsof(I["L3_ffn_W2"].reshape(-1, D)))

    mbf = np.zeros((B, M, 4), np.bool_)
    mbf[:, :, 0] = I["mask_BxS2_bf0"]
    mbf = mbf.view(np.int32)[:, :, 0]
    tiles = lambda a: a.reshape(NT, 128, M).transpose(1, 0, 2)
    arrays = dict(
        xT=I["x"].reshape(B * T, D).T, g8=np.tile(np.stack([I["g_xattn"], I["g_ffn"]], 1).reshape(1, 8), (128, 1)),
        const=pack(CONST_W, **const), l0=l0, att=att, f0=f0, f1=f1, f2=f2, f3=f3, f3big=f3big, rows=rows,
        am_tok=tiles(I["fside_SxS2_0"]), am_T=I["fside_SxS2_0"].T,
        ik_tok=tiles(I["mask_SxS2_ik0"]), ik_T=I["mask_SxS2_ik0"].T,
        mif=np.tile(I["mask_BxS2_if0"].reshape(1, -1), (128, 1)),
        mbf_tok=np.tile(mbf.reshape(1, -1), (128, 1)), mbf_T=mbf.T)
    arrays = {k: np.ascontiguousarray(v) for k, v in arrays.items()}

    nc = _bacc.Bacc("TRN2", target_bir_lowering=False, num_devices=1)
    args = {k: nc.dram_tensor(k, v.shape, _mybir.dt.from_np(v.dtype), kind="ExternalInput").ap()
            for k, v in arrays.items()}
    out = nc.dram_tensor("outT", (D, B * T), _mybir.dt.from_np(np.dtype(f4)), kind="ExternalOutput").ap()
    bass_flamingo_gated_layers_kernel(nc, outT=out, **args)
    res = _run(nc, [arrays], core_ids=[0])
    return res.results[0]["outT"].T.reshape(B, T, D)
```
